# Optimizing a Trainium2 kernel written in Bass

```python
import numpy as np
import jax
import jax.numpy as jnp

def _softmax(x, axis=-1):
    return jax.nn.softmax(x, axis=axis)

def _gelu(x):
    return jax.nn.gelu(x, approximate=True)

def _silu(x):
    return jax.nn.silu(x)

def _sigmoid(x):
    return jax.nn.sigmoid(x)

def _layernorm(x, axis=-1, eps=1e-05):
    m = jnp.mean(x, axis=axis, keepdims=True)
    v = jnp.var(x, axis=axis, keepdims=True)
    return (x - m) / jnp.sqrt(v + eps)

def _scatter_add(tgt, idx, src, axis=0):
    return tgt.at[idx].add(src)

def _segment_sum(src, seg, n):
    return jax.ops.segment_sum(src, seg, n)
kernel_name = 'mk_metaformer_d2_conv_nhwc512_r4_b62b75'

def setup_inputs(seed: int=0):
    np.random.seed(seed)
    _w = jnp.asarray

    def _rec_inputs():
        import jax
        import jax.numpy as jnp
        _gk = jax.random.key(seed)
        x = -0.0003929 + 0.9999 * jax.random.normal(jax.random.fold_in(_gk, 1), (2, 16, 64, 128), jnp.float32)
        return x
    x = _rec_inputs()

    def _L0_conv_setup():
        import jax, jax.numpy as jnp
        import numpy as np
        HEADS = 8
        DK = 16
        NEIGHBORS = 3
        KSIZE = 1 + 2 * NEIGHBORS
        key = jax.random.key(seed)
        k1, k2, k3, k4 = jax.random.split(key, 4)
        B, HW, S, D = (2, 16, 64, 128)
        inputs = jax.random.normal(k1, (B, HW, S, D), dtype=jnp.float32)
        pos_bias = jax.random.normal(k2, (HEADS, S, KSIZE), dtype=jnp.float32)
        W_qkv = jax.random.normal(k3, (D, 3 * HEADS * DK), dtype=jnp.float32) * 0.02
        W_out = jax.random.normal(k4, (HEADS * DK, D), dtype=jnp.float32) * 0.02
        return {'inputs': inputs, 'pos_bias': pos_bias, 'W_qkv': W_qkv, 'W_out': W_out}
    _L0_conv_all = _L0_conv_setup()
    _L0_conv_in = {k: v for k, v in _L0_conv_all.items() if k in ('pos_bias', 'W_qkv', 'W_out')}
    del _L0_conv_all

    def _L0_ffn_setup():
        import jax, jax.numpy as jnp
        import numpy as np
        B, S, D, F, E, NS, K = (2, 512, 128, 512, 8, 2, 2)
        key = jax.random.key(seed)
        ks = jax.random.split(key, 6)
        scale = 0.02

        def p(k, shape):
            return jax.random.normal(k, shape, jnp.float32) * scale
        return {'x': jax.random.normal(ks[0], (B, S, D), jnp.float32), 'gate_w': p(ks[1], (E, D)), 'gate_b': jnp.zeros((E,), jnp.float32), 'sw1': p(ks[2], (NS, F, D)), 'sb1': jnp.zeros((NS, F), jnp.float32), 'sw2': p(ks[3], (NS, D, F)), 'sb2': jnp.zeros((NS, D), jnp.float32), 'rw1': p(ks[4], (E, F, D)), 'rb1': jnp.zeros((E, F), jnp.float32), 'rw2': p(ks[5], (E, D, F)), 'rb2': jnp.zeros((E, D), jnp.float32)}
    _L0_ffn_all = _L0_ffn_setup()
    _L0_ffn_in = {k: v for k, v in _L0_ffn_all.items() if k in ('gate_w', 'gate_b', 'sw1', 'sb1', 'sw2', 'sb2', 'rw1', 'rb1', 'rw2', 'rb2')}
    del _L0_ffn_all

    def _L1_conv_setup():
        import jax, jax.numpy as jnp
        import numpy as np
        B, W, S, E = (8, 16, 64, 128)
        H = 8
        D = E // H
        SCALE = D ** (-0.5)
        key = jax.random.key(seed)
        ks = jax.random.split(key, 12)
        init = lambda k, shape, fan_in: jax.random.uniform(k, shape, jnp.float32, -1.0, 1.0) * fan_in ** (-0.5)
        return {'x': jax.random.normal(ks[0], (B, W, S, E), jnp.float32), 'mask': jax.random.normal(ks[1], (1, W, 1, S, S), jnp.float32), 'Wq': init(ks[2], (E, E), E), 'bq': init(ks[3], (E,), E), 'Wk': init(ks[4], (E, E), E), 'bk': init(ks[5], (E,), E), 'Wv': init(ks[6], (E, E), E), 'bv': init(ks[7], (E,), E), 'Wp': init(ks[8], (E, E), E), 'bp': init(ks[9], (E,), E), 'pos_bias': jax.random.normal(ks[10], (H, S, S), jnp.float32) * 0.02}
    _L1_conv_all = _L1_conv_setup()
    _L1_conv_in = {k: v for k, v in _L1_conv_all.items() if k in ('mask', 'Wq', 'bq', 'Wk', 'bk', 'Wv', 'bv', 'Wp', 'bp', 'pos_bias')}
    del _L1_conv_all

    def _L1_ffn_setup():
        import jax, jax.numpy as jnp
        import numpy as np
        GRID_SIZE = 5
        SPLINE_ORDER = 3
        NUM_EXPERTS = 8
        TOP_K = 2
        HIDDEN = 128
        D_FF = 256
        N_BASES = GRID_SIZE + SPLINE_ORDER

        def _grid():
            h = 2.0 / GRID_SIZE
            g = jnp.arange(-SPLINE_ORDER, GRID_SIZE + SPLINE_ORDER + 1, dtype=jnp.float32) * h - 1.0
            return g[None, :]

        def b_splines(x, grid):
            xe = x[..., None]
            bases = ((xe >= grid[:, :-1]) & (xe < grid[:, 1:])).astype(x.dtype)
            for j in range(1, SPLINE_ORDER + 1):
                left = (xe - grid[:, :-(j + 1)]) / (grid[:, j:-1] - grid[:, :-(j + 1)])
                right = (grid[:, j + 1:] - xe) / (grid[:, j + 1:] - grid[:, 1:-j])
                bases = left * bases[..., :-1] + right * bases[..., 1:]
            return bases

        def kan_linear(x, base_w, spline_w, scaler, grid):
            base = jax.nn.silu(x) @ base_w.T
            sb = b_splines(x, grid)
            spline = jnp.einsum('nic,oic->no', sb, spline_w * scaler[..., None])
            return base + spline

        def expert_ffn(x, b1, s1, c1, b2, s2, c2, b3, s3, c3, gh, gf):
            h1 = kan_linear(x, b1, s1, c1, gh)
            h2 = kan_linear(x, b2, s2, c2, gh)
            return kan_linear(h1 * h2, b3, s3, c3, gf)
        key = jax.random.key(seed)
        ks = jax.random.split(key, 8)
        x = jax.random.normal(ks[0], (2, 256, HIDDEN), dtype=jnp.float32)
        gate_w = jax.random.normal(ks[1], (NUM_EXPERTS, HIDDEN), dtype=jnp.float32) * HIDDEN ** (-0.5)
        base_w1 = jax.random.normal(ks[2], (NUM_EXPERTS, D_FF, HIDDEN), dtype=jnp.float32) * HIDDEN ** (-0.5)
        spline_w1 = jax.random.normal(ks[3], (NUM_EXPERTS, D_FF, HIDDEN, N_BASES), dtype=jnp.float32) * 0.02
        scaler_w1 = jnp.ones((NUM_EXPERTS, D_FF, HIDDEN), dtype=jnp.float32)
        base_w2 = jax.random.normal(ks[4], (NUM_EXPERTS, D_FF, HIDDEN), dtype=jnp.float32) * HIDDEN ** (-0.5)
        spline_w2 = jax.random.normal(ks[5], (NUM_EXPERTS, D_FF, HIDDEN, N_BASES), dtype=jnp.float32) * 0.02
        scaler_w2 = jnp.ones((NUM_EXPERTS, D_FF, HIDDEN), dtype=jnp.float32)
        base_w3 = jax.random.normal(ks[6], (NUM_EXPERTS, HIDDEN, D_FF), dtype=jnp.float32) * D_FF ** (-0.5)
        spline_w3 = jax.random.normal(ks[7], (NUM_EXPERTS, HIDDEN, D_FF, N_BASES), dtype=jnp.float32) * 0.02
        scaler_w3 = jnp.ones((NUM_EXPERTS, HIDDEN, D_FF), dtype=jnp.float32)
        return {'x': x, 'gate_w': gate_w, 'base_w1': base_w1, 'spline_w1': spline_w1, 'scaler_w1': scaler_w1, 'base_w2': base_w2, 'spline_w2': spline_w2, 'scaler_w2': scaler_w2, 'base_w3': base_w3, 'spline_w3': spline_w3, 'scaler_w3': scaler_w3}
    _L1_ffn_all = _L1_ffn_setup()
    _L1_ffn_in = {k: v for k, v in _L1_ffn_all.items() if k in ('gate_w', 'base_w1', 'spline_w1', 'scaler_w1', 'base_w2', 'spline_w2', 'scaler_w2', 'base_w3', 'spline_w3', 'scaler_w3')}
    del _L1_ffn_all
    return {'x': x, 'L0_conv_pos_bias': _L0_conv_in['pos_bias'], 'L0_conv_W_qkv': _L0_conv_in['W_qkv'], 'L0_conv_W_out': _L0_conv_in['W_out'], 'L0_ffn_gate_w': _L0_ffn_in['gate_w'], 'L0_ffn_gate_b': _L0_ffn_in['gate_b'], 'L0_ffn_sw1': _L0_ffn_in['sw1'], 'L0_ffn_sb1': _L0_ffn_in['sb1'], 'L0_ffn_sw2': _L0_ffn_in['sw2'], 'L0_ffn_sb2': _L0_ffn_in['sb2'], 'L0_ffn_rw1': _L0_ffn_in['rw1'], 'L0_ffn_rb1': _L0_ffn_in['rb1'], 'L0_ffn_rw2': _L0_ffn_in['rw2'], 'L0_ffn_rb2': _L0_ffn_in['rb2'], 'L1_conv_mask': _L1_conv_in['mask'], 'L1_conv_Wq': _L1_conv_in['Wq'], 'L1_conv_bq': _L1_conv_in['bq'], 'L1_conv_Wk': _L1_conv_in['Wk'], 'L1_conv_bk': _L1_conv_in['bk'], 'L1_conv_Wv': _L1_conv_in['Wv'], 'L1_conv_bv': _L1_conv_in['bv'], 'L1_conv_Wp': _L1_conv_in['Wp'], 'L1_conv_bp': _L1_conv_in['bp'], 'L1_conv_pos_bias': _L1_conv_in['pos_bias'], 'L1_ffn_gate_w': _L1_ffn_in['gate_w'], 'L1_ffn_base_w1': _L1_ffn_in['base_w1'], 'L1_ffn_spline_w1': _L1_ffn_in['spline_w1'], 'L1_ffn_scaler_w1': _L1_ffn_in['scaler_w1'], 'L1_ffn_base_w2': _L1_ffn_in['base_w2'], 'L1_ffn_spline_w2': _L1_ffn_in['spline_w2'], 'L1_ffn_scaler_w2': _L1_ffn_in['scaler_w2'], 'L1_ffn_base_w3': _L1_ffn_in['base_w3'], 'L1_ffn_spline_w3': _L1_ffn_in['spline_w3'], 'L1_ffn_scaler_w3': _L1_ffn_in['scaler_w3']}

def reference(x, L0_conv_pos_bias, L0_conv_W_qkv, L0_conv_W_out, L0_ffn_gate_w, L0_ffn_gate_b, L0_ffn_sw1, L0_ffn_sb1, L0_ffn_sw2, L0_ffn_sb2, L0_ffn_rw1, L0_ffn_rb1, L0_ffn_rw2, L0_ffn_rb2, L1_conv_mask, L1_conv_Wq, L1_conv_bq, L1_conv_Wk, L1_conv_bk, L1_conv_Wv, L1_conv_bv, L1_conv_Wp, L1_conv_bp, L1_conv_pos_bias, L1_ffn_gate_w, L1_ffn_base_w1, L1_ffn_spline_w1, L1_ffn_scaler_w1, L1_ffn_base_w2, L1_ffn_spline_w2, L1_ffn_scaler_w2, L1_ffn_base_w3, L1_ffn_spline_w3, L1_ffn_scaler_w3):
    import jax
    import jax.numpy as jnp

    def _L0_conv_ref(inputs, pos_bias, W_qkv, W_out):
        import jax, jax.numpy as jnp
        import numpy as np
        HEADS = 8
        DK = 16
        NEIGHBORS = 3
        KSIZE = 1 + 2 * NEIGHBORS
        B, HW, S, D = inputs.shape
        qkv = inputs @ W_qkv
        q, k, v = jnp.split(qkv, 3, axis=-1)
        q = (q / jnp.sqrt(jnp.float32(DK))).reshape(B, HW, S, HEADS, DK)
        k = k.reshape(B, HW, S, HEADS, DK)
        v = v.reshape(B, HW, S, HEADS, DK)
        pad = NEIGHBORS
        kp = jnp.pad(k, ((0, 0), (0, 0), (pad, pad), (0, 0), (0, 0)))
        vp = jnp.pad(v, ((0, 0), (0, 0), (pad, pad), (0, 0), (0, 0)))
        idx = jnp.arange(S)[:, None] + jnp.arange(KSIZE)[None, :]
        kw = kp[:, :, idx]
        vw = vp[:, :, idx]
        attn = jnp.einsum('bnshd,bnswhd->bnswh', q, kw)
        attn = attn + jnp.transpose(pos_bias, (1, 2, 0))[None, None]
        attn = jax.nn.softmax(attn, axis=-2)
        out = jnp.einsum('bnswh,bnswhd->bnshd', attn, vw)
        out = out.reshape(B, HW, S, HEADS * DK)
        return out @ W_out

    def _L0_ffn_ref(x, gate_w, gate_b, sw1, sb1, sw2, sb2, rw1, rb1, rw2, rb2):
        import jax, jax.numpy as jnp
        import numpy as np
        B, S, D, F, E, NS, K = (2, 512, 128, 512, 8, 2, 2)
        b, s, d = x.shape
        t = x.reshape(-1, d)
        T = t.shape[0]
        hs = jax.nn.gelu(jnp.einsum('td,nfd->ntf', t, sw1) + sb1[:, None, :], approximate=False)
        shared = jnp.einsum('ntf,ndf->td', hs, sw2) + sb2.sum(axis=0)
        logits = t @ gate_w.T + gate_b
        probs = jax.nn.softmax(logits, axis=-1)
        top_v, top_i = jax.lax.top_k(probs, K)
        cw = jnp.zeros_like(probs).at[jnp.arange(T)[:, None], top_i].add(top_v)
        hr = jax.nn.gelu(jnp.einsum('td,efd->etf', t, rw1) + rb1[:, None, :], approximate=False)
        oe = jnp.einsum('etf,edf->etd', hr, rw2) + rb2[:, None, :]
        routed = jnp.einsum('etd,te->td', oe, cw)
        return (shared + routed).reshape(b, s, d)

    def _L1_conv_ref(x, mask, Wq, bq, Wk, bk, Wv, bv, Wp, bp, pos_bias):
        import jax, jax.numpy as jnp
        import numpy as np
        B, W, S, E = (8, 16, 64, 128)
        H = 8
        D = E // H
        SCALE = D ** (-0.5)
        b, w, s, e = x.shape
        q = (x @ Wq.T + bq) * SCALE
        k = x @ Wk.T + bk
        v = x @ Wv.T + bv
        q = q.reshape(b, w, s, H, D)
        k = k.reshape(b, w, s, H, D)
        v = v.reshape(b, w, s, H, D)
        attn = jnp.einsum('bwihd,bwjhd->bwhij', q, k)
        attn = attn + pos_bias
        attn = attn + mask
        attn = jax.nn.softmax(attn, axis=-1)
        z = jnp.einsum('bwhij,bwjhd->bwihd', attn, v)
        z = z.reshape(b, w, s, H * D)
        return z @ Wp.T + bp

    def _L1_ffn_ref(x, gate_w, base_w1, spline_w1, scaler_w1, base_w2, spline_w2, scaler_w2, base_w3, spline_w3, scaler_w3):
        import jax, jax.numpy as jnp
        import numpy as np
        GRID_SIZE = 5
        SPLINE_ORDER = 3
        NUM_EXPERTS = 8
        TOP_K = 2
        HIDDEN = 128
        D_FF = 256
        N_BASES = GRID_SIZE + SPLINE_ORDER

        def _grid():
            h = 2.0 / GRID_SIZE
            g = jnp.arange(-SPLINE_ORDER, GRID_SIZE + SPLINE_ORDER + 1, dtype=jnp.float32) * h - 1.0
            return g[None, :]

        def b_splines(x, grid):
            xe = x[..., None]
            bases = ((xe >= grid[:, :-1]) & (xe < grid[:, 1:])).astype(x.dtype)
            for j in range(1, SPLINE_ORDER + 1):
                left = (xe - grid[:, :-(j + 1)]) / (grid[:, j:-1] - grid[:, :-(j + 1)])
                right = (grid[:, j + 1:] - xe) / (grid[:, j + 1:] - grid[:, 1:-j])
                bases = left * bases[..., :-1] + right * bases[..., 1:]
            return bases

        def kan_linear(x, base_w, spline_w, scaler, grid):
            base = jax.nn.silu(x) @ base_w.T
            sb = b_splines(x, grid)
            spline = jnp.einsum('nic,oic->no', sb, spline_w * scaler[..., None])
            return base + spline

        def expert_ffn(x, b1, s1, c1, b2, s2, c2, b3, s3, c3, gh, gf):
            h1 = kan_linear(x, b1, s1, c1, gh)
            h2 = kan_linear(x, b2, s2, c2, gh)
            return kan_linear(h1 * h2, b3, s3, c3, gf)
        B, S, H = x.shape
        gh, gf = (_grid(), _grid())
        xt = x.reshape(-1, H)
        logits = xt @ gate_w.T
        topw, sel = jax.lax.top_k(logits, TOP_K)
        topw = jax.nn.softmax(topw.astype(jnp.float32), axis=-1).astype(x.dtype)
        out = jnp.zeros_like(xt)
        for i in range(NUM_EXPERTS):
            ey = expert_ffn(xt, base_w1[i], spline_w1[i], scaler_w1[i], base_w2[i], spline_w2[i], scaler_w2[i], base_w3[i], spline_w3[i], scaler_w3[i], gh, gf)
            gi = jnp.sum(jnp.where(sel == i, topw, 0.0), axis=-1)
            out = out + gi[:, None] * ey
        return out.reshape(B, S, H)

    def _gn(v, G=32, eps=1e-05):
        B_, H_, W_, C_ = v.shape
        g = v.reshape(B_, H_, W_, G, C_ // G)
        m = jnp.mean(g, axis=(1, 2, 4), keepdims=True)
        s = jnp.var(g, axis=(1, 2, 4), keepdims=True)
        return ((g - m) / jnp.sqrt(s + eps)).reshape(v.shape)

    def _ln_c(v, eps=1e-06):
        m = jnp.mean(v, axis=-1, keepdims=True)
        s = jnp.var(v, axis=-1, keepdims=True)
        return (v - m) / jnp.sqrt(s + eps)

    def _ln_t(v, eps=1e-05):
        m = jnp.mean(v, axis=-1, keepdims=True)
        s = jnp.var(v, axis=-1, keepdims=True)
        return (v - m) / jnp.sqrt(s + eps)

    def _to_tokens(v):
        B_, H_, W_, C_ = v.shape
        return v.reshape(B_, H_ * W_, C_)

    def _from_tokens(t, like):
        return t.reshape(like.shape)
    x = x + _L0_conv_ref(_ln_c(x), L0_conv_pos_bias, L0_conv_W_qkv, L0_conv_W_out)
    t = _to_tokens(x)
    t = t + _L0_ffn_ref(_ln_t(t), L0_ffn_gate_w, L0_ffn_gate_b, L0_ffn_sw1, L0_ffn_sb1, L0_ffn_sw2, L0_ffn_sb2, L0_ffn_rw1, L0_ffn_rb1, L0_ffn_rw2, L0_ffn_rb2)
    x = _from_tokens(t, x)
    x = x + _L1_conv_ref(_ln_c(x), L1_conv_mask, L1_conv_Wq, L1_conv_bq, L1_conv_Wk, L1_conv_bk, L1_conv_Wv, L1_conv_bv, L1_conv_Wp, L1_conv_bp, L1_conv_pos_bias)
    t = _to_tokens(x)
    t = t + _L1_ffn_ref(_ln_t(t), L1_ffn_gate_w, L1_ffn_base_w1, L1_ffn_spline_w1, L1_ffn_scaler_w1, L1_ffn_base_w2, L1_ffn_spline_w2, L1_ffn_scaler_w2, L1_ffn_base_w3, L1_ffn_spline_w3, L1_ffn_scaler_w3)
    x = _from_tokens(t, x)
    return x

_drawn_inputs = setup_inputs


def setup_inputs(seed=0):
    import zlib

    import numpy as np

    out = dict(_drawn_inputs(seed))
    spreads = {'L0_ffn_gate_b': (0.0, 0.273),
     'L0_ffn_sb1': (0.0, 0.1),
     'L0_ffn_sb2': (0.0, 0.1),
     'L0_ffn_rb1': (0.0, 0.55),
     'L0_ffn_rb2': (0.0, 0.1),
     'L1_ffn_scaler_w1': (1.0, 0.6),
     'L1_ffn_scaler_w2': (1.0, 0.6),
     'L1_ffn_scaler_w3': (1.0, 0.2)}
    factors = {'L0_ffn_rw1': 2.703, 'L1_conv_bq': 7.909, 'L1_conv_bk': 64.0, 'L1_conv_pos_bias': 22.588}
    for name, (base, spread) in spreads.items():
        noise = np.random.default_rng([zlib.crc32(name.encode()), seed]).standard_normal(out[name].shape)
        drawn = base * np.exp(spread * noise) if base else spread * noise
        out[name] = jnp.asarray(drawn.astype(out[name].dtype))
    for name, factor in factors.items():
        out[name] = (out[name] * factor).astype(out[name].dtype)
    return out
```

```python
from contextlib import ExitStack

import concourse.bass as bass
import numpy as np
from concourse import mybir

F32 = mybir.dt.float32
U32 = mybir.dt.uint32
I32 = mybir.dt.int32
ACT = mybir.ActivationFunctionType
ALU = mybir.AluOpType
X = mybir.AxisListType.X

P = 128
TOKENS = 2048
TILES = TOKENS // P
GROUP = 4
TURNS = TILES // GROUP
HEADS = 8
DK = 16
PAIRS = HEADS // 2
BLK = 64
NEIGH = 3
FAR = -1.0e30
WINDOWS = 16
EXPERTS = 8
SHARED = 2
FF0 = 512
CH0 = FF0 // P
ROW0 = 2 * FF0 + CH0
FF1 = 256
CH1 = FF1 // P
BASES = 8
FEAT = BASES + 1
W12 = FEAT * 2 * FF1
W3 = CH1 * FEAT * P
ROW1 = W12 + W3
SCAL12 = 2 * FF1
SCAL1 = SCAL12 + CH1 * P
CHOICES = 2
SLOT_TILES = CHOICES * TOKENS // P + EXPERTS - 1
SLOTS = SLOT_TILES * P
KNOTS_PER_UNIT = 2.5
FIRST_CENTRE = -3.5

C_ID = 0
C_HEAD = C_ID + P
C_UPPER = C_HEAD + HEADS
C_ONES = C_UPPER + P
C_EARLIER = C_ONES + P
C_TILE = C_EARLIER + EXPERTS * EXPERTS
C_LANE = C_TILE + SLOT_TILES
C_END = C_LANE + 1


class Count:

    def __init__(self, sem, per_turn, credit=0):
        self.sem, self.per_turn, self.credit = sem, per_turn, credit

    def give_credit(self, eng):
        eng.sem_inc(self.sem, self.credit)

    def wait(self, eng, turn, n):
        eng.wait_ge(self.sem, turn * self.per_turn + (self.credit + n))


class Chain:

    def __init__(self, eng, sem, turn=0, per_turn=0, done=0):
        self.eng, self.sem, self.turn, self.per_turn, self.done = eng, sem, turn, per_turn, done

    def after(self, ins):
        ins.then_inc(self.sem, 1)
        self.done += 1
        self.eng.wait_ge(self.sem, self.turn * self.per_turn + self.done if self.per_turn else self.done)


def layer_norm_stats(sb, sem, tag, x_sb, eps):
    stats = sb(f"{tag}_stats", [P, TILES, 6])
    moments = sb(f"{tag}_moments", [P, TILES, 2])
    dev = sb(f"{tag}_dev", [P, TILES])
    rstd = sb(f"{tag}_rstd", [P, TILES])
    s_stats, s_mom, s_dev, s_rstd = (sem(f"{tag}_{n}") for n in ("s_stats", "s_mom", "s_dev", "s_rstd"))

    def vector(eng):
        for t in range(TILES):
            eng.bn_stats(stats[:, t, :], x_sb[:, t, :]).then_inc(s_stats, 1)
        for t in range(TILES):
            eng.wait_ge(s_stats, t + 1)
            eng.bn_aggr(moments[:, t, :], stats[:, t, :]).then_inc(s_mom, 1)
        eng.wait_ge(s_mom, TILES)
        eng.tensor_scalar(dev[:, :], moments[:, :, 1], eps, None, ALU.add).then_inc(s_mom, 1)
        eng.wait_ge(s_dev, 1)
        eng.reciprocal(rstd[:, :], dev[:, :]).then_inc(s_rstd, 1)
        eng.wait_ge(s_rstd, 1)

    def scalar(eng):
        eng.wait_ge(s_mom, TILES + 1)
        eng.activation(dev[:, :], dev[:, :], ACT.Sqrt).then_inc(s_dev, 1)

    return moments, rstd, vector, scalar


def attention(nc, ctx, tag, x_sb, ident, head_cols, load, arrived, keys, bias_of, fill, w, eps):
    bq, bk, bv, bp = w.get("bq"), w.get("bk"), w.get("bv"), w.get("bp")
    with ExitStack() as own:
        def sb(name, shape, dt=F32):
            return own.enter_context(nc.sbuf_tensor(f"{tag}_{name}", shape, dt))

        def ps(name, shape):
            return own.enter_context(nc.psum_tensor(f"{tag}_{name}", shape, F32))

        def sem(name):
            return ctx.enter_context(nc.semaphore(f"{tag}_{name}"))

        moments, rstd, stats_vector, stats_scalar = layer_norm_stats(sb, sem, "ln", x_sb, eps)
        xn = sb("xn", [P, GROUP, P])
        xnT = sb("xnT", [P, GROUP * P])
        qT = sb("qT", [P, GROUP * P])
        kT = sb("kT", [P, GROUP * P])
        v = sb("v", [P, GROUP, P])
        q_heads = sb("q_heads", [P, 2 * GROUP, HEADS, BLK])
        logits = [sb(f"logits{i}", [P, HEADS, keys]) for i in range(2)]
        probs = [sb(f"probs{i}", [P, HEADS, keys]) for i in range(2)]
        weights = [sb(f"weights{i}", [P, HEADS, BLK]) for i in range(2)]
        probsT = [sb(f"probsT{i}", [P, PAIRS, P]) for i in range(2)]
        top = sb("top", [P, 2, HEADS])
        total = sb("total", [P, 2, HEADS])
        z = sb("z", [P, GROUP, P])
        zT = sb("zT", [P, GROUP * P])
        res = sb("res", [P, GROUP, P])

        ps_T = ps("ps_T", [P, GROUP, P])
        ps_qk = ps("ps_qk", [P, GROUP * P])
        ps_v = ps("ps_v", [P, GROUP, P])
        ps_S = [ps(f"ps_S{i}", [P, HEADS, BLK]) for i in range(2)]
        ps_P = ps("ps_P", [P, PAIRS, P])
        ps_Z = [ps(f"ps_Z{i}", [P, GROUP, P]) for i in range(2)]

        normed = Count(sem("normed"), GROUP)
        turned = Count(sem("turned"), 2, credit=2)
        turned_out = Count(sem("turned_out"), 2, credit=2)
        proj = Count(sem("proj"), 3, credit=3)
        q_out = Count(sem("q_out"), 1, credit=1)
        k_out = Count(sem("k_out"), 1, credit=1)
        v_out = Count(sem("v_out"), 1)
        heads = Count(sem("heads"), 1, credit=1)
        scored = Count(sem("scored"), GROUP)
        biased = Count(sem("biased"), GROUP, credit=2)
        shifted = Count(sem("shifted"), GROUP, credit=2)
        exped = Count(sem("exped"), GROUP)
        inv = Count(sem("inv"), GROUP)
        norm_p = Count(sem("norm_p"), GROUP, credit=2)
        probs_turned = Count(sem("probs_turned"), GROUP, credit=2)
        probsT_out = Count(sem("probsT_out"), GROUP, credit=1)
        mixed = Count(sem("mixed"), GROUP, credit=2)
        z_out = Count(sem("z_out"), 2, credit=2)
        out_done = Count(sem("out_done"), 1)
        added = Count(sem("added"), 1, credit=1)
        s_chain = sem("chain")
        gate = sem("gate")
        CHAIN = 2 * GROUP + (bp is not None)

        with nc.Block() as block:
            @block.sync
            def _(eng):
                load(eng)

            @block.tensor
            def _(eng):
                turned_out.give_credit(eng)
                q_out.give_credit(eng)
                k_out.give_credit(eng)
                biased.give_credit(eng)
                probsT_out.give_credit(eng)
                z_out.give_credit(eng)
                added.give_credit(eng)
                arrived(eng)

                def score(g, t):
                    biased.wait(eng, g, t - 1)
                    for hp in range(PAIRS):
                        for b in range(2):
                            at = (2 * t + b) * BLK
                            mm = eng.matmul(ps_S[t % 2][:, 2 * hp + b, :],
                                            q_heads[:, 2 * t + b, 2 * hp:2 * hp + 2, :],
                                            kT[:, at:at + BLK], start=True, stop=True)
                    mm.then_inc(scored.sem, 1)

                def turn_probs(g, t):
                    norm_p.wait(eng, g, t + 1)
                    probsT_out.wait(eng, g, t)
                    for hp in range(PAIRS):
                        mm = eng.transpose(ps_P[:, hp, :],
                                           weights[t % 2][:, 2 * hp:2 * hp + 2, :], ident)
                    mm.then_inc(probs_turned.sem, 1)

                def mix(g, t):
                    probsT_out.wait(eng, g, t + 1)
                    eng.sem_inc(gate, 1)
                    for h in range(HEADS):
                        for b in range(2):
                            rows = slice(b * BLK, (b + 1) * BLK)
                            cols = slice((h % 2) * BLK, (h % 2 + 1) * BLK)
                            mm = eng.matmul(ps_Z[b][rows, t, h * DK:(h + 1) * DK],
                                            probsT[t % 2][rows, h // 2, cols],
                                            v[rows, t, h * DK:(h + 1) * DK], start=True, stop=True)
                    mm.then_inc(mixed.sem, 1)

                with eng.Fori(0, TURNS) as g:
                    turned_out.wait(eng, g, 0)
                    for t in range(GROUP):
                        normed.wait(eng, g, t + 1)
                        mm = eng.transpose(ps_T[:, t, :], xn[:, t, :], ident)
                    mm.then_inc(turned.sem, 1)
                    turned_out.wait(eng, g, 1)
                    k_out.wait(eng, g, 0)
                    eng.matmul(ps_qk[:, :], w["wq"], xnT[:, :], start=True, stop=True).then_inc(proj.sem, 1)
                    added.wait(eng, g, 0)
                    for t in range(GROUP):
                        mm = eng.matmul(ps_v[:, t, :], xnT[:, t * P:(t + 1) * P], w["wv"], start=True, stop=True)
                    mm.then_inc(proj.sem, 1)
                    q_out.wait(eng, g, 1)
                    eng.matmul(ps_qk[:, :], w["wk"], xnT[:, :], start=True, stop=True).then_inc(proj.sem, 1)
                    heads.wait(eng, g, 1)
                    k_out.wait(eng, g, 1)
                    for s in range(GROUP + 2):
                        if s < GROUP:
                            score(g, s)
                        if 0 <= s - 1 < GROUP:
                            turn_probs(g, s - 1)
                        if s - 2 == 0:
                            v_out.wait(eng, g, 1)
                            z_out.wait(eng, g, 0)
                        if 0 <= s - 2 < GROUP:
                            mix(g, s - 2)
                    z_out.wait(eng, g, 2)
                    for t in range(GROUP):
                        mm = eng.transpose(ps_T[:, t, :], z[:, t, :], ident)
                    mm.then_inc(turned.sem, 1)
                    turned_out.wait(eng, g, 2)
                    for t in range(GROUP):
                        mm = eng.matmul(ps_v[:, t, :], zT[:, t * P:(t + 1) * P], w["wo"], start=True, stop=True)
                    mm.then_inc(out_done.sem, 1)

            @block.scalar
            def _(eng):
                turned.give_credit(eng)
                norm_p.give_credit(eng)
                heads.give_credit(eng)
                probs_turned.give_credit(eng)
                mixed.give_credit(eng)
                arrived(eng)
                stats_scalar(eng)
                eng.preload_act_table(ACT.Exp)

                def expo(g, t):
                    shifted.wait(eng, g, t + 1)
                    eng.activation(probs[t % 2][:, :, :], probs[t % 2][:, :, :], ACT.Exp)\
                       .then_inc(exped.sem, 1)

                def copy_probsT(g, t):
                    probs_turned.wait(eng, g, t + 1)
                    mixed.wait(eng, g, t - 1)
                    eng.activation(probsT[t % 2][:, :, :], ps_P[:, :, :], ACT.Copy)\
                       .then_inc(probsT_out.sem, 1)

                with eng.Fori(0, TURNS) as g:
                    turned.wait(eng, g, 1)
                    proj.wait(eng, g, 0)
                    eng.activation(xnT[:, :], ps_T[:, :, :], ACT.Copy).then_inc(turned_out.sem, 1)
                    proj.wait(eng, g, 1)
                    heads.wait(eng, g, 0)
                    if bq is not None:
                        eng.activation(qT[:, :], ps_qk[:, :], ACT.Identity, bias=bq).then_inc(q_out.sem, 1)
                    else:
                        eng.activation(qT[:, :], ps_qk[:, :], ACT.Copy).then_inc(q_out.sem, 1)
                    proj.wait(eng, g, 3)
                    if bk is not None:
                        eng.activation(kT[:, :], ps_qk[:, :], ACT.Identity, bias=bk).then_inc(k_out.sem, 1)
                    else:
                        eng.activation(kT[:, :], ps_qk[:, :], ACT.Copy).then_inc(k_out.sem, 1)
                    for s in range(GROUP + 1):
                        if s < GROUP:
                            expo(g, s)
                        if 0 <= s - 1 < GROUP:
                            copy_probsT(g, s - 1)
                    mixed.wait(eng, g, GROUP)
                    for b in range(2):
                        rows = slice(b * BLK, (b + 1) * BLK)
                        eng.activation(z[rows, :, :], ps_Z[b][rows, :, :], ACT.Copy).then_inc(z_out.sem, 1)
                    turned.wait(eng, g, 2)
                    eng.activation(zT[:, :], ps_T[:, :, :], ACT.Copy).then_inc(turned_out.sem, 1)

            @block.gpsimd
            def _(eng):
                with eng.Fori(0, TURNS) as g:
                    for t in range(GROUP):
                        inv.wait(eng, g, t + 1)
                        probs_turned.wait(eng, g, t - 1)
                        eng.tensor_tensor(weights[t % 2][:, :, :], probs[t % 2][:, :, 0:BLK],
                                          total[:, t % 2, :].unsqueeze(2).to_broadcast([P, HEADS, BLK]),
                                          ALU.mult).then_inc(norm_p.sem, 1)

            @block.vector
            def _(eng):
                proj.give_credit(eng)
                shifted.give_credit(eng)
                arrived(eng)
                stats_vector(eng)
                fill(eng, logits)

                with eng.Fori(0, TURNS) as g:
                    chain = Chain(eng, s_chain, g, CHAIN)
                    turned.wait(eng, g, 0)
                    for t in range(GROUP):
                        at = bass.ds(g * GROUP + t, 1)
                        eng.tensor_scalar(xn[:, t, :], x_sb[:, at, :],
                                          moments[:, at, 0], rstd[:, at], ALU.subtract, ALU.mult)\
                           .then_inc(normed.sem, 1)
                    q_out.wait(eng, g, 1)
                    for h in range(HEADS):
                        ins = eng.tensor_scalar(q_heads[:, :, h, :], qT[:, :].rearrange("p (b i) -> p b i", i=BLK),
                                                head_cols[:, h:h + 1],
                                                float(DK) ** -0.5, ALU.mult, ALU.mult)
                    ins.then_inc(heads.sem, 1)
                    proj.wait(eng, g, 2)
                    if bv is not None:
                        eng.tensor_tensor(v[:, :, :], ps_v[:, :, :],
                                          bv.unsqueeze(1).to_broadcast([P, GROUP, P]), ALU.add)\
                           .then_inc(v_out.sem, 1)
                    else:
                        eng.tensor_copy(v[:, :, :], ps_v[:, :, :]).then_inc(v_out.sem, 1)

                    def shift(t):
                        scored.wait(eng, g, t + 1)
                        shifted.wait(eng, g, t - 1)
                        eng.tensor_tensor(logits[t % 2][:, :, 0:BLK], ps_S[t % 2][:, :, :], bias_of(g, t), ALU.add)\
                           .then_inc(biased.sem, 1)
                        biased.wait(eng, g, t + 1)
                        chain.after(eng.tensor_reduce(top[:, t % 2, :], logits[t % 2][:, :, :], X, ALU.max))
                        norm_p.wait(eng, g, t - 1)
                        eng.tensor_tensor(probs[t % 2][:, :, :], logits[t % 2][:, :, :],
                                          top[:, t % 2, :].unsqueeze(2).to_broadcast([P, HEADS, keys]),
                                          ALU.subtract).then_inc(shifted.sem, 1)

                    def row_sums(t):
                        exped.wait(eng, g, t + 1)
                        chain.after(eng.tensor_reduce(total[:, t % 2, :], probs[t % 2][:, :, :], X, ALU.add))
                        eng.reciprocal(total[:, t % 2, :], total[:, t % 2, :]).then_inc(inv.sem, 1)

                    for s in range(GROUP + 1):
                        if s < GROUP:
                            shift(s)
                        if 0 <= s - 1 < GROUP:
                            row_sums(s - 1)
                    out_done.wait(eng, g, 1)
                    at = bass.ds(g * GROUP, GROUP)
                    src = ps_v[:, :, :]
                    if bp is not None:
                        chain.after(eng.tensor_tensor(res[:, :, :], ps_v[:, :, :],
                                                      bp.unsqueeze(1).to_broadcast([P, GROUP, P]), ALU.add))
                        src = res[:, :, :]
                    eng.tensor_tensor(x_sb[:, at, :], x_sb[:, at, :], src, ALU.add).then_inc(added.sem, 1)
                    assert chain.done == CHAIN
                added.wait(eng, TURNS, 0)


def rank_experts(eng, chain, sb, scores, earlier, tag):
    shape = [P, TILES, EXPERTS, EXPERTS]
    above = sb(f"{tag}_above", shape)
    level = sb(f"{tag}_level", shape)
    rank = sb(f"{tag}_rank", [P, TILES, EXPERTS])
    other = scores.unsqueeze(2).to_broadcast(shape)
    own = scores.unsqueeze(3).to_broadcast(shape)
    first = earlier.rearrange("p (a b) -> p a b", b=EXPERTS).unsqueeze(1).to_broadcast(shape)
    eng.tensor_tensor(above[:, :, :, :], other, own, ALU.is_gt)
    chain.after(eng.tensor_tensor(level[:, :, :, :], other, own, ALU.is_equal))
    chain.after(eng.tensor_tensor(level[:, :, :, :], level[:, :, :, :], first, ALU.mult))
    chain.after(eng.tensor_tensor(above[:, :, :, :], above[:, :, :, :], level[:, :, :, :], ALU.add))
    chain.after(eng.tensor_reduce(rank[:, :, :], above[:, :, :, :], X, ALU.add))
    return rank


def gelu_experts(nc, ctx, x_sb, consts, d, pool_work):
    ident = consts[:, C_ID:C_ID + P]
    with ExitStack() as own:
        def sb(name, shape, dt=F32):
            return own.enter_context(nc.sbuf_tensor(f"f0_{name}", shape, dt))

        def ps(name, shape):
            return own.enter_context(nc.psum_tensor(f"f0_{name}", shape, F32))

        def sem(name):
            return ctx.enter_context(nc.semaphore(f"f0_{name}"))

        ALL = EXPERTS + SHARED
        moments, rstd, stats_vector, stats_scalar = layer_norm_stats(sb, sem, "ln", x_sb, 1e-5)
        xn = sb("xn", [P, TILES, P])
        nT = sb("nT", [P, TILES, P])
        gate = sb("gate", [P, 2 * EXPERTS])
        b2 = sb("b2", [ALL, P])
        probs = sb("probs", [P, TILES, EXPERTS])
        top = sb("top", [P, TILES])
        mix = sb("mix", [P, TILES, ALL])
        mixT = sb("mixT", [ALL, TILES, P])
        wt = [sb(f"wt{i}", [P, ROW0]) for i in range(2)]
        mix_now = [sb(f"mix_now{i}", [P, TILES]) for i in range(2)]
        hid = [sb(f"hid{i}", [P, CH0, GROUP * P]) for i in range(2)]
        ps_up = [ps(f"ps_up{i}", [P, GROUP * P]) for i in range(4)]
        ps_dn = [ps(f"ps_dn{i}", [P, GROUP, P]) for i in range(2)]
        ps_g = ps("ps_g", [P, TILES, EXPERTS])
        ps_t = ps_dn[0]

        HALF = ALL // 2
        STEPS = 2 * TURNS
        s_small = sem("s_small")
        s_w = [Count(sem(f"s_w{i}"), 16) for i in range(2)]
        normed = sem("normed")
        turned = sem("turned")
        turned_out = sem("turned_out")
        gated = sem("gated")
        s_exp = sem("s_exp")
        s_shift = sem("s_shift")
        mixed = sem("mixed")
        mixT_mm = sem("mixT_mm")
        mixT_out = sem("mixT_out")
        b2_mm = sem("b2_mm")
        b2_added = sem("b2_added")
        up = Count(sem("up"), STEPS * CH0)
        acted = Count(sem("acted"), STEPS * CH0, credit=4)
        down = Count(sem("down"), STEPS, credit=TURNS + 1)
        added = Count(sem("added"), STEPS * GROUP, credit=2 * GROUP)
        cols = Count(sem("cols"), 2)
        s_chain = sem("chain")

        with nc.Block() as block:
            @block.sync
            def _(eng):
                eng.dma_start(gate[:, :], d["gate0"]).then_inc(s_small, 16)
                eng.dma_start(b2[:, :], d["b2"]).then_inc(s_small, 16)
                with eng.Fori(0, HALF) as i:
                    for a in range(2):
                        down.wait(eng, i, (a - 1) * TURNS)
                        eng.dma_start(wt[a][:, :], d["experts0"][bass.ds(2 * i + a, 1), :, :])\
                           .then_inc(s_w[a].sem, 16)

            @block.tensor
            def _(eng):
                acted.give_credit(eng)
                added.give_credit(eng)
                eng.wait_ge(s_small, 32)
                for g in range(TURNS):
                    if g >= 1:
                        eng.wait_ge(turned_out, g)
                    for t in range(GROUP):
                        eng.wait_ge(normed, g * GROUP + t + 1)
                        mm = eng.transpose(ps_t[:, t, :], xn[:, g * GROUP + t, :], ident)
                    mm.then_inc(turned, 1)
                eng.wait_ge(turned_out, TURNS)
                for t in range(TILES):
                    mm = eng.matmul(ps_g[:, t, :], nT[:, t, :], gate[:, 0:EXPERTS], start=True, stop=True)
                mm.then_inc(gated, 1)
                eng.wait_ge(mixed, 1)
                for g in range(TURNS):
                    if g >= 1:
                        eng.wait_ge(mixT_out, g)
                    for t in range(GROUP):
                        mm = eng.transpose(ps_t[0:ALL, t, :], mix[:, g * GROUP + t, :], ident)
                    mm.then_inc(mixT_mm, 1)
                for g in range(TURNS):
                    eng.wait_ge(mixT_out, max(TURNS, g + 1))
                    if g >= 2:
                        eng.wait_ge(b2_added, g - 1)
                    for t in range(GROUP):
                        mm = eng.matmul(ps_dn[g % 2][:, t, :], mixT[:, g * GROUP + t, :], b2[:, :],
                                        start=True, stop=True)
                    mm.then_inc(b2_mm, 1)
                eng.wait_ge(b2_added, TURNS)

                def go_up(i, s):
                    a, g = divmod(s, TURNS)
                    if g == 0:
                        s_w[a].wait(eng, i, 16)
                    for c in range(CH0):
                        acted.wait(eng, i, s * CH0 + c + 1 - 4)
                        eng.matmul(ps_up[c][:, :], wt[a][:, c * P:(c + 1) * P],
                                   nT[:, g * GROUP:(g + 1) * GROUP, :], start=True, stop=True)\
                           .then_inc(up.sem, 1)

                def go_down(i, s):
                    a, g = divmod(s, TURNS)
                    acted.wait(eng, i, (s + 1) * CH0)
                    added.wait(eng, i, (s - 1) * GROUP)
                    for t in range(GROUP):
                        for c in range(CH0):
                            mm = eng.matmul(ps_dn[s % 2][:, t, :], hid[s % 2][:, c, t * P:(t + 1) * P],
                                            wt[a][:, FF0 + c * P:FF0 + (c + 1) * P],
                                            start=(c == 0), stop=(c == CH0 - 1))
                    mm.then_inc(down.sem, 1)

                with eng.Fori(0, HALF) as i:
                    for s in range(STEPS + 1):
                        if s < STEPS:
                            go_up(i, s)
                        if s >= 1:
                            go_down(i, s - 1)

            @block.scalar
            def _(eng):
                down.give_credit(eng)
                stats_scalar(eng)
                for g in range(TURNS):
                    eng.wait_ge(turned, g + 1)
                    eng.activation(nT[:, g * GROUP:(g + 1) * GROUP, :], ps_t[:, :, :], ACT.Copy)\
                       .then_inc(turned_out, 1)
                eng.wait_ge(s_shift, 1)
                eng.activation(probs[:, :, :], probs[:, :, :], ACT.Exp).then_inc(s_exp, 1)
                for g in range(TURNS):
                    eng.wait_ge(mixT_mm, g + 1)
                    eng.activation(mixT[:, g * GROUP:(g + 1) * GROUP, :], ps_t[0:ALL, :, :], ACT.Copy)\
                       .then_inc(mixT_out, 1)
                eng.preload_act_table(ACT.Gelu)
                with eng.Fori(0, HALF) as i:
                    for s in range(STEPS):
                        a = s // TURNS
                        down.wait(eng, i, s - 1)
                        for c in range(CH0):
                            up.wait(eng, i, s * CH0 + c + 1)
                            eng.activation(hid[s % 2][:, c, :], ps_up[c][:, :], ACT.Gelu,
                                           bias=wt[a][:, 2 * FF0 + c:2 * FF0 + c + 1]).then_inc(acted.sem, 1)

            @block.gpsimd
            def _(eng):
                pool_work(eng)

            @block.vector
            def _(eng):
                stats_vector(eng)
                for t in range(TILES):
                    eng.tensor_scalar(xn[:, t, :], x_sb[:, t, :], moments[:, t, 0:1], rstd[:, t:t + 1],
                                      ALU.subtract, ALU.mult).then_inc(normed, 1)
                eng.wait_ge(s_small, 32)
                eng.wait_ge(gated, 1)
                chain = Chain(eng, s_chain)
                wide = [P, TILES, EXPERTS]
                chain.after(eng.tensor_tensor(probs[:, :, :], ps_g[:, :, :],
                                              gate[:, EXPERTS:].unsqueeze(1).to_broadcast(wide), ALU.add))
                chain.after(eng.tensor_reduce(top[:, :], probs[:, :, :], X, ALU.max))
                eng.tensor_tensor(probs[:, :, :], probs[:, :, :], top[:, :].unsqueeze(2).to_broadcast(wide),
                                  ALU.subtract).then_inc(s_shift, 1)
                eng.wait_ge(s_exp, 1)
                chain.after(eng.tensor_reduce(top[:, :], probs[:, :, :], X, ALU.add))
                chain.after(eng.reciprocal(top[:, :], top[:, :]))
                chain.after(eng.tensor_tensor(probs[:, :, :], probs[:, :, :],
                                              top[:, :].unsqueeze(2).to_broadcast(wide), ALU.mult))
                rank = rank_experts(eng, chain, sb, probs[:, :, :], consts[:, C_EARLIER:C_TILE], "route")
                chain.after(eng.tensor_scalar(rank[:, :, :], rank[:, :, :], float(CHOICES), None, ALU.is_lt))
                eng.memset(mix[:, :, EXPERTS:], 1.0)
                eng.tensor_tensor(mix[:, :, 0:EXPERTS], rank[:, :, :], probs[:, :, :], ALU.mult)\
                   .then_inc(mixed, 1)
                eng.wait_ge(mixed, 1)
                for g in range(TURNS):
                    eng.wait_ge(b2_mm, g + 1)
                    at = slice(g * GROUP, (g + 1) * GROUP)
                    eng.tensor_tensor(x_sb[:, at, :], x_sb[:, at, :], ps_dn[g % 2][:, :, :], ALU.add)\
                       .then_inc(b2_added, 1)
                eng.wait_ge(b2_added, TURNS)
                with eng.Fori(0, HALF) as i:
                    for s in range(STEPS):
                        a, g = divmod(s, TURNS)
                        if g == 0:
                            eng.tensor_copy(mix_now[a][:, :], mix[:, :, bass.ds(2 * i + a, 1)]).then_inc(cols.sem, 1)
                            cols.wait(eng, i, a + 1)
                            added.wait(eng, i, s * GROUP)
                        down.wait(eng, i, s + 1)
                        for t in range(GROUP):
                            xt = x_sb[:, g * GROUP + t, :]
                            eng.scalar_tensor_tensor(xt, ps_dn[s % 2][:, t, :],
                                                     mix_now[a][:, g * GROUP + t:g * GROUP + t + 1], xt,
                                                     ALU.mult, ALU.add).then_inc(added.sem, 1)
                added.wait(eng, HALF, 0)


def spline_weights(nc, sb, sem, d, w12_dram, w3_dram, window_bias):
    raw = [sb(f"raw{i}", [P, ROW1]) for i in range(2)]
    scal = [sb(f"scal{i}", [P, SCAL1]) for i in range(2)]
    pos1 = sb("pos1", [P, PAIRS, BLK])
    mask1 = sb("mask1", [P, WINDOWS, BLK])
    loaded = [Count(sem(f"loaded{i}"), 32) for i in range(2)]
    stored = [Count(sem(f"stored{i}"), 32) for i in range(2)]
    scaled = Count(sem("scaled"), 2)
    prepared = Count(sem("prepared"), 4)
    s_tab = sem("s_tab")
    gate = sem("gate")
    s_added = sem("s_added")

    def work(eng):
        eng.dma_start(pos1[:, :, :], d["pos1"]).then_inc(s_tab, 16)
        eng.dma_start(mask1[:, :, :], d["mask1"]).then_inc(s_tab, 16)
        eng.wait_ge(s_tab, 32)
        shape = [P, PAIRS, 2, BLK]
        for n in range(WINDOWS // 2):
            eng.tensor_tensor(window_bias[:, n, :, :].rearrange("p (h b) k -> p h b k", b=2),
                              pos1[:, :, :].unsqueeze(2).to_broadcast(shape),
                              mask1[:, 2 * n:2 * n + 2, :].unsqueeze(1).to_broadcast(shape), ALU.add)\
               .then_inc(s_added, 1)
        with eng.Fori(0, EXPERTS // 2) as i:
            for a in range(2):
                at = bass.ds(2 * i + a, 1)
                eng.dma_start(raw[a][:, :], d["experts1"][at, :, :]).then_inc(loaded[a].sem, 16)
                eng.dma_start(scal[a][:, :], d["scalers1"][at, :, :]).then_inc(loaded[a].sem, 16)
            for a in range(2):
                loaded[a].wait(eng, i, 32)
                eng.sem_inc(gate, 1)
                eng.tensor_scalar(scal[a][:, :], scal[a][:, :], -1.0 / 6.0, None, ALU.mult)\
                   .then_inc(scaled.sem, 1)
                scaled.wait(eng, i, a + 1)
                first = raw[a][:, 0:BASES * 2 * FF1].rearrange("p (c o) -> p c o", c=BASES)
                eng.tensor_tensor(first, first, scal[a][:, 0:SCAL12].unsqueeze(1)
                                  .to_broadcast([P, BASES, 2 * FF1]), ALU.mult).then_inc(prepared.sem, 1)
                last = raw[a][:, W12:].rearrange("p (k c o) -> p k c o", k=CH1, c=FEAT)[:, :, 0:BASES, :]
                eng.tensor_tensor(last, last, scal[a][:, SCAL12:].rearrange("p (k o) -> p k o", k=CH1)
                                  .unsqueeze(2).to_broadcast([P, CH1, BASES, P]), ALU.mult)\
                   .then_inc(prepared.sem, 1)
                prepared.wait(eng, i, 2 * a + 2)
                rows = bass.ds((2 * i + a) * P, P)
                eng.dma_start(w12_dram[rows, :], raw[a][:, 0:W12]).then_inc(stored[a].sem, 16)
                eng.dma_start(w3_dram[rows, :], raw[a][:, W12:]).then_inc(stored[a].sem, 16)
            for a in range(2):
                stored[a].wait(eng, i, 32)
        eng.wait_ge(s_added, WINDOWS // 2)
    return work


def route(nc, ctx, x_sb, consts, d, slots_dram, place, lots, shares):
    ident = consts[:, C_ID:C_ID + P]
    with ExitStack() as own:
        def sb(name, shape, dt=F32):
            return own.enter_context(nc.sbuf_tensor(f"rt_{name}", shape, dt))

        def ps(name, shape):
            return own.enter_context(nc.psum_tensor(f"rt_{name}", shape, F32))

        def sem(name):
            return ctx.enter_context(nc.semaphore(f"rt_{name}"))

        moments, rstd, stats_vector, stats_scalar = layer_norm_stats(sb, sem, "ln", x_sb, 1e-5)
        wide = [P, TILES, EXPERTS]
        xn = sb("xn", [P, TILES, P])
        nT = sb("nT", [P, TILES, P])
        gate = sb("gate", [P, EXPERTS])
        scores = sb("scores", wide)
        chosen = sb("chosen", wide)
        choice = [sb(f"choice{k}", wide) for k in range(CHOICES)]
        picked = sb("picked", wide)
        value = [sb(f"value{k}", [P, TILES]) for k in range(CHOICES)]
        base = sb("base", wide)
        total = sb("total", wide)
        upto = [sb(f"upto{i}", wide) for i in range(2)]
        many = sb("many", [P, EXPERTS, TILES])
        tiles_of = sb("tiles_of", [P, EXPERTS])
        before = sb("before", [P, EXPERTS, EXPERTS])
        start = sb("start", [P, EXPERTS])
        begun = sb("begun", [P, SLOT_TILES, EXPERTS])
        owner = sb("owner", [P, SLOT_TILES])
        ps_t = ps("ps_t", [P, GROUP, P])
        ps_g = ps("ps_g", wide)
        ps_before = ps("ps_before", wide)
        ps_total = ps("ps_total", wide)
        s_gate = sem("s_gate")
        normed = sem("normed")
        turned = sem("turned")
        turned_out = sem("turned_out")
        gated = sem("gated")
        chosen_ok = sem("chosen_ok")
        counted = sem("counted")
        s_gap = sem("s_gap")
        s_exp = sem("s_exp")
        placed = sem("placed")
        scattered = sem("scattered")
        s_chain = sem("chain")

        with nc.Block() as block:
            @block.sync
            def _(eng):
                eng.dma_start(gate[:, :], d["gate1"]).then_inc(s_gate, 16)

            @block.tensor
            def _(eng):
                eng.wait_ge(s_gate, 16)
                for g in range(TURNS):
                    if g >= 1:
                        eng.wait_ge(turned_out, g)
                    for t in range(GROUP):
                        eng.wait_ge(normed, g * GROUP + t + 1)
                        mm = eng.transpose(ps_t[:, t, :], xn[:, g * GROUP + t, :], ident)
                    mm.then_inc(turned, 1)
                eng.wait_ge(turned_out, TURNS)
                for t in range(TILES):
                    mm = eng.matmul(ps_g[:, t, :], nT[:, t, :], gate[:, :], start=True, stop=True)
                mm.then_inc(gated, 1)
                eng.wait_ge(chosen_ok, 1)
                eng.matmul(ps_before[:, :, :], consts[:, C_UPPER:C_UPPER + P], chosen[:, :, :],
                           start=True, stop=True)
                eng.matmul(ps_total[:, :, :], consts[:, C_ONES:C_ONES + P], chosen[:, :, :],
                           start=True, stop=True).then_inc(counted, 1)

            @block.scalar
            def _(eng):
                stats_scalar(eng)
                for g in range(TURNS):
                    eng.wait_ge(turned, g + 1)
                    eng.activation(nT[:, g * GROUP:(g + 1) * GROUP, :], ps_t[:, :, :], ACT.Copy)\
                       .then_inc(turned_out, 1)
                eng.wait_ge(s_gap, 1)
                eng.activation(value[1][:, :], value[1][:, :], ACT.Exp).then_inc(s_exp, 1)

            @block.vector
            def _(eng):
                stats_vector(eng)
                for t in range(TILES):
                    eng.tensor_scalar(xn[:, t, :], x_sb[:, t, :], moments[:, t, 0:1], rstd[:, t:t + 1],
                                      ALU.subtract, ALU.mult).then_inc(normed, 1)
                eng.wait_ge(gated, 1)
                chain = Chain(eng, s_chain)
                chain.after(eng.tensor_copy(scores[:, :, :], ps_g[:, :, :]))
                rank = rank_experts(eng, chain, sb, scores[:, :, :], consts[:, C_EARLIER:C_TILE], "route")
                for k in range(CHOICES):
                    chain.after(eng.tensor_scalar(choice[k][:, :, :], rank[:, :, :], float(k), None, ALU.is_equal))
                eng.tensor_tensor(chosen[:, :, :], choice[0][:, :, :], choice[1][:, :, :], ALU.add)\
                   .then_inc(chosen_ok, 1)
                for k in range(CHOICES):
                    chain.after(eng.tensor_tensor(picked[:, :, :], choice[k][:, :, :], scores[:, :, :], ALU.mult))
                    chain.after(eng.tensor_reduce(value[k][:, :], picked[:, :, :], X, ALU.add))
                eng.tensor_tensor(value[1][:, :], value[1][:, :], value[0][:, :], ALU.subtract).then_inc(s_gap, 1)

                eng.wait_ge(counted, 1)
                chain.after(eng.tensor_copy(total[:, :, :], ps_total[:, :, :]))
                chain.after(eng.tensor_copy(upto[0][:, :, :], total[:, :, :]))
                a, step = 0, 1
                while step < TILES:
                    new, old = upto[1 - a], upto[a]
                    eng.tensor_copy(new[:, 0:step, :], old[:, 0:step, :])
                    chain.after(eng.tensor_tensor(new[:, step:, :], old[:, step:, :], old[:, 0:TILES - step, :],
                                                  ALU.add))
                    a, step = 1 - a, 2 * step
                starts = consts[:, C_TILE:C_TILE + SLOT_TILES]
                shape = [P, EXPERTS, TILES]
                chain.after(eng.tensor_tensor(many[:, :, :], upto[a][:, TILES - 1, :].unsqueeze(2).to_broadcast(shape),
                                              starts[:, 0:TILES].unsqueeze(1).to_broadcast(shape), ALU.is_gt))
                chain.after(eng.tensor_reduce(tiles_of[:, :], many[:, :, :], X, ALU.add))
                shape = [P, EXPERTS, EXPERTS]
                chain.after(eng.tensor_tensor(
                    before[:, :, :], tiles_of[:, :].unsqueeze(1).to_broadcast(shape),
                    consts[:, C_EARLIER:C_TILE].rearrange("p (a b) -> p a b", b=EXPERTS), ALU.mult))
                chain.after(eng.tensor_reduce(start[:, :], before[:, :, :], X, ALU.add))
                chain.after(eng.tensor_scalar(start[:, :], start[:, :], float(P), None, ALU.mult))
                chain.after(eng.tensor_tensor(base[:, :, :], upto[a][:, :, :], total[:, :, :], ALU.subtract))
                chain.after(eng.tensor_tensor(base[:, :, :], base[:, :, :], ps_before[:, :, :], ALU.add))
                chain.after(eng.tensor_tensor(base[:, :, :], base[:, :, :],
                                              start[:, :].unsqueeze(1).to_broadcast(wide), ALU.add))
                for k in range(CHOICES):
                    chain.after(eng.tensor_tensor(picked[:, :, :], choice[k][:, :, :], base[:, :, :], ALU.mult))
                    chain.after(eng.tensor_reduce(total[:, :, k], picked[:, :, :], X, ALU.add))
                    eng.tensor_copy(place[k][:, :], total[:, :, k]).then_inc(placed, 1)
                shape = [P, SLOT_TILES, EXPERTS]
                chain.after(eng.tensor_tensor(begun[:, :, :], start[:, :].unsqueeze(1).to_broadcast(shape),
                                              starts.unsqueeze(2).to_broadcast(shape), ALU.is_le))
                chain.after(eng.tensor_reduce(owner[:, :], begun[:, :, :], X, ALU.add))
                chain.after(eng.tensor_scalar(owner[:, :], owner[:, :], float(P), consts[:, C_LANE:C_LANE + 1],
                                              ALU.mult, ALU.add))
                chain.after(eng.tensor_scalar(lots[:, :], owner[:, :], -float(P), None, ALU.add))
                eng.wait_ge(s_exp, 1)
                chain.after(eng.tensor_scalar(value[0][:, :], value[1][:, :], 1.0, None, ALU.add))
                chain.after(eng.reciprocal(shares[0][:, :], value[0][:, :]))
                chain.after(eng.tensor_tensor(shares[1][:, :], value[1][:, :], shares[0][:, :], ALU.mult))

            @block.gpsimd
            def _(eng):
                eng.wait_ge(placed, CHOICES)
                for k in range(CHOICES):
                    for t in range(TILES):
                        eng.indirect_dma_start(
                            out=slots_dram, out_offset=bass.IndirectOffsetOnAxis(ap=place[k][:, t:t + 1], axis=0),
                            in_=xn[:, t, :], in_offset=None).then_inc(scattered, 16)
                eng.wait_ge(scattered, 16 * CHOICES * TILES)


class TileCount:

    def __init__(self, sem, times=1):
        self.sem, self.times = sem, times
        self.credit = 2 * times

    def give_credit(self, eng):
        eng.sem_inc(self.sem, self.credit)

    def wait(self, eng, turn, n):
        eng.wait_ge(self.sem, turn * (2 * self.times) + ((n + 1) * self.times + self.credit))


class ArrivalCount:

    def __init__(self, even, odd, credit=0):
        self.sems, self.credit = (even, odd), credit

    def give_credit(self, eng):
        for s in self.sems:
            eng.sem_inc(s, self.credit)

    def of(self, n):
        return self.sems[n % 2]

    def wait(self, eng, turn, n):
        eng.wait_ge(self.sems[n % 2], turn * 16 + (16 * (n // 2 + 1) + self.credit))


def spline_experts(nc, ctx, ident, slots_dram, y_dram, w12_dram, w3_dram, lots):
    with ExitStack() as own:
        def sb(name, shape, dt=F32):
            return own.enter_context(nc.sbuf_tensor(f"kan_{name}", shape, dt))

        def ps(name, shape):
            return own.enter_context(nc.psum_tensor(f"kan_{name}", shape, F32))

        def sem(name):
            return ctx.enter_context(nc.semaphore(f"kan_{name}"))

        def pair(name, credit=0):
            return ArrivalCount(sem(name + "0"), sem(name + "1"), credit)

        w12 = [sb(f"w12_{i}", [P, W12]) for i in range(2)]
        w3 = [sb(f"w3_{i}", [P, W3]) for i in range(2)]
        rows12 = [sb(f"rows12_{i}", [P, 1], U32) for i in range(2)]
        rows3 = [sb(f"rows3_{i}", [P, 1], U32) for i in range(2)]
        slot_x = [sb(f"slot_x{i}", [P, P]) for i in range(2)]
        y_sb = [sb(f"y_sb{i}", [P, P]) for i in range(2)]
        h1 = sb("h1", [P, FF1])
        h = sb("h", [P, FF1])

        class Part:

            def __init__(self, tag, n):
                self.n = n
                self.u = sb(tag + "u", [P, n])
                self.t = sb(tag + "t", [P, BASES, n])
                self.a = sb(tag + "a", [P, BASES, n])
                self.b = sb(tag + "b", [P, BASES, n])
                self.f = sb(tag + "f", [P, BASES, n])
                self.s = sb(tag + "s", [P, n])
                self.turned = TileCount(sem(tag + "turned"))
                self.taken = TileCount(sem(tag + "taken"), 2)
                self.offset = TileCount(sem(tag + "offset"))
                self.dist = TileCount(sem(tag + "dist"))
                self.squares = TileCount(sem(tag + "squares"), 2)
                self.cubes = TileCount(sem(tag + "cubes"), 2)
                self.near = TileCount(sem(tag + "near"))
                self.ready = TileCount(sem(tag + "ready"))
                self.used = TileCount(sem(tag + "used"))

        px, ph = Part("x", P), Part("h", FF1)
        ps_x = ps("ps_x", [P, P])
        ps_h = [ps(f"ps_h{i}", [P, 2 * FF1]) for i in range(2)]
        ps_ht = ps("ps_ht", [P, CH1, P])
        ps_y = ps("ps_y", [P, P])
        in_x, in_12, in_3 = pair("in_x"), pair("in_12"), pair("in_3")
        out_y = pair("out_y", 16)
        rows_ok12 = TileCount(sem("rows_ok12"))
        rows_ok3 = TileCount(sem("rows_ok3"))
        gate = sem("gate")
        h1_ok = TileCount(sem("h1_ok"))
        h_ok = TileCount(sem("h_ok"))
        y_ok = TileCount(sem("y_ok"))

        LAST = SLOT_TILES - 1
        LOOP = (SLOT_TILES - 3) // 2
        assert SLOT_TILES % 2 == 1

        def tiles(eng, step):
            step(0, 0)
            with eng.Fori(0, LOOP) as i:
                step(i, 1)
                step(i, 2)
            step(LOOP, 1)
            step(LOOP, 2)

        def exists(turn, n):
            return not isinstance(turn, int) or 2 * turn + n <= LAST

        with nc.Block() as block:
            @block.sync
            def _(eng):
                px.turned.give_credit(eng)

                def fetch(turn, n):
                    if exists(turn, n):
                        px.turned.wait(eng, turn, n - 2)
                        eng.dma_start(slot_x[n % 2][:, :], slots_dram[bass.ds((2 * turn + n) * P, P), :])\
                           .then_inc(in_x.of(n), 16)

                def step(turn, n):
                    fetch(turn, n + 2)
                    y_ok.wait(eng, turn, n)
                    eng.dma_start(y_dram[bass.ds((2 * turn + n) * P, P), :], y_sb[n % 2][:, :])\
                       .then_inc(out_y.of(n), 16)

                fetch(0, 0)
                fetch(0, 1)
                tiles(eng, step)
                out_y.wait(eng, LOOP, 1)
                out_y.wait(eng, LOOP, 2)

            @block.gpsimd
            def _(eng):
                px.used.give_credit(eng)
                ph.used.give_credit(eng)

                def fetch12(turn, n):
                    if exists(turn, n):
                        px.used.wait(eng, turn, n - 2)
                        eng.sem_inc(gate, 1)
                        eng.tensor_copy(rows12[n % 2][:, :], lots[:, bass.ds(2 * turn + n, 1)])\
                           .then_inc(rows_ok12.sem, 1)
                        rows_ok12.wait(eng, turn, n)
                        eng.sem_inc(gate, 1)
                        eng.indirect_dma_start(out=w12[n % 2][:, :], out_offset=None, in_=w12_dram,
                                               in_offset=bass.IndirectOffsetOnAxis(ap=rows12[n % 2][:, 0:1], axis=0))\
                           .then_inc(in_12.of(n), 16)

                def fetch3(turn, n):
                    if exists(turn, n):
                        ph.used.wait(eng, turn, n - 2)
                        eng.sem_inc(gate, 1)
                        eng.tensor_copy(rows3[n % 2][:, :], lots[:, bass.ds(2 * turn + n, 1)])\
                           .then_inc(rows_ok3.sem, 1)
                        rows_ok3.wait(eng, turn, n)
                        eng.sem_inc(gate, 1)
                        eng.indirect_dma_start(out=w3[n % 2][:, :], out_offset=None, in_=w3_dram,
                                               in_offset=bass.IndirectOffsetOnAxis(ap=rows3[n % 2][:, 0:1], axis=0))\
                           .then_inc(in_3.of(n), 16)

                rows_ok12.give_credit(eng)
                rows_ok3.give_credit(eng)
                fetch12(0, 0)
                fetch12(0, 1)
                fetch3(0, 0)

                def step(turn, n):
                    fetch3(turn, n + 1)
                    fetch12(turn, n + 2)

                tiles(eng, step)

            @block.tensor
            def _(eng):
                px.taken.give_credit(eng)
                ph.taken.give_credit(eng)
                h_ok.give_credit(eng)
                y_ok.give_credit(eng)

                def turn_x(turn, n):
                    if exists(turn, n):
                        in_x.wait(eng, turn, n)
                        px.taken.wait(eng, turn, n - 1)
                        eng.transpose(ps_x[:, :], slot_x[n % 2][:, :], ident).then_inc(px.turned.sem, 1)

                def layers12(turn, n):
                    if exists(turn, n):
                        in_12.wait(eng, turn, n)
                        h_ok.wait(eng, turn, n - 2)
                        px.ready.wait(eng, turn, n)
                        for c in range(FEAT):
                            lhs = px.f[:, c, :] if c < BASES else px.s[:, :]
                            mm = eng.matmul(ps_h[n % 2][:, :], lhs,
                                            w12[n % 2][:, c * 2 * FF1:(c + 1) * 2 * FF1],
                                            start=(c == 0), stop=(c == BASES))
                        mm.then_inc(px.used.sem, 1)

                def turn_h(turn, n):
                    h_ok.wait(eng, turn, n)
                    ph.taken.wait(eng, turn, n - 1)
                    for k in range(CH1):
                        mm = eng.transpose(ps_ht[:, k, :], h[:, k * P:(k + 1) * P], ident)
                    mm.then_inc(ph.turned.sem, 1)

                def layer3(turn, n):
                    in_3.wait(eng, turn, n)
                    y_ok.wait(eng, turn, n - 1)
                    ph.ready.wait(eng, turn, n)
                    for k in range(CH1):
                        for c in range(FEAT):
                            lhs = ph.f[:, c, k * P:(k + 1) * P] if c < BASES else ph.s[:, k * P:(k + 1) * P]
                            at = (k * FEAT + c) * P
                            mm = eng.matmul(ps_y[:, :], lhs, w3[n % 2][:, at:at + P],
                                            start=(k + c == 0), stop=(k == CH1 - 1 and c == BASES))
                    mm.then_inc(ph.used.sem, 1)

                turn_x(0, 0)
                layers12(0, 0)
                turn_x(0, 1)

                def step(turn, n):
                    turn_h(turn, n)
                    layers12(turn, n + 1)
                    layer3(turn, n)
                    turn_x(turn, n + 2)

                tiles(eng, step)

            def take(eng, part, psum, turn, n):
                part.turned.wait(eng, turn, n)
                part.dist.wait(eng, turn, n - 1)
                eng.activation(part.u[:, :], psum, ACT.Copy, scale=KNOTS_PER_UNIT).then_inc(part.taken.sem, 1)
                part.used.wait(eng, turn, n - 1)
                eng.activation(part.s[:, :], psum, ACT.Silu).then_inc(part.taken.sem, 1)

            def squares(eng, part, turn, n):
                part.dist.wait(eng, turn, n)
                part.ready.wait(eng, turn, n - 1)
                eng.activation(part.a[:, :, :], part.t[:, :, :], ACT.Square, bias=bias_m2, scale=1.0)\
                   .then_inc(part.squares.sem, 1)
                eng.activation(part.b[:, :, :], part.t[:, :, :], ACT.Square, bias=bias_m2, scale=2.0)\
                   .then_inc(part.squares.sem, 1)

            def near(eng, part, turn, n):
                part.cubes.wait(eng, turn, n)
                eng.activation(part.b[:, :, :], part.b[:, :, :], ACT.Relu, scale=-1.0).then_inc(part.near.sem, 1)

            minus2 = sb("minus2", [P, 1])
            m2_ok = sem("m2_ok")
            bias_m2 = minus2[:, 0:1]

            @block.scalar
            def _(eng):
                px.dist.give_credit(eng)
                ph.dist.give_credit(eng)
                px.ready.give_credit(eng)
                ph.ready.give_credit(eng)
                out_y.give_credit(eng)
                eng.wait_ge(m2_ok, 1)
                eng.preload_act_table(ACT.Silu)

                def half(turn, n):
                    px.used.wait(eng, turn, n)
                    h_ok.wait(eng, turn, n - 1)
                    eng.activation(h1[:, :], ps_h[n % 2][:, 0:FF1], ACT.Copy).then_inc(h1_ok.sem, 1)

                def store(turn, n):
                    ph.used.wait(eng, turn, n)
                    out_y.wait(eng, turn, n - 2)
                    eng.activation(y_sb[n % 2][:, :], ps_y[:, :], ACT.Copy).then_inc(y_ok.sem, 1)

                take(eng, px, ps_x[:, :], 0, 0)
                squares(eng, px, 0, 0)
                near(eng, px, 0, 0)

                def step(turn, n):
                    half(turn, n)
                    if exists(turn, n + 1):
                        take(eng, px, ps_x[:, :], turn, n + 1)
                        squares(eng, px, turn, n + 1)
                    if not (isinstance(turn, int) and 2 * turn + n == 0):
                        store(turn, n - 1)
                    take(eng, ph, ps_ht[:, :, :], turn, n)
                    if exists(turn, n + 1):
                        near(eng, px, turn, n + 1)
                    squares(eng, ph, turn, n)
                    near(eng, ph, turn, n)

                tiles(eng, step)
                store(LOOP, 2)

            @block.vector
            def _(eng):
                px.offset.give_credit(eng)
                ph.offset.give_credit(eng)
                px.squares.give_credit(eng)
                ph.squares.give_credit(eng)
                px.cubes.give_credit(eng)
                ph.cubes.give_credit(eng)
                px.near.give_credit(eng)
                ph.near.give_credit(eng)
                ph.turned.give_credit(eng)
                h1_ok.give_credit(eng)
                eng.memset(minus2[:, :], -2.0).then_inc(m2_ok, 1)

                def distances(part, turn, n):
                    part.taken.wait(eng, turn, n)
                    part.squares.wait(eng, turn, n - 1)
                    part.cubes.wait(eng, turn, n - 1)
                    for c in range(BASES):
                        ins = eng.tensor_scalar(part.t[:, c, :], part.u[:, :], FIRST_CENTRE + c, None,
                                                ALU.subtract)
                    ins.then_inc(part.offset.sem, 1)
                    part.offset.wait(eng, turn, n)
                    bits = part.t[:, :, :].bitcast(U32)
                    eng.tensor_scalar(bits, bits, 0x7FFFFFFF, None, ALU.bitwise_and).then_inc(part.dist.sem, 1)

                def cubes(part, turn, n):
                    part.dist.wait(eng, turn, n)
                    part.squares.wait(eng, turn, n)
                    eng.scalar_tensor_tensor(part.a[:, :, :], part.t[:, :, :], 2.0, part.a[:, :, :],
                                             ALU.subtract, ALU.mult).then_inc(part.cubes.sem, 1)
                    eng.scalar_tensor_tensor(part.b[:, :, :], part.t[:, :, :], 1.0, part.b[:, :, :],
                                             ALU.subtract, ALU.mult).then_inc(part.cubes.sem, 1)

                def bases(part, turn, n):
                    part.near.wait(eng, turn, n)
                    part.cubes.wait(eng, turn, n)
                    part.used.wait(eng, turn, n - 1)
                    eng.scalar_tensor_tensor(part.f[:, :, :], part.a[:, :, :], 0.0, part.b[:, :, :],
                                             ALU.min, ALU.add).then_inc(part.ready.sem, 1)

                def product(turn, n):
                    h1_ok.wait(eng, turn, n)
                    ph.turned.wait(eng, turn, n - 1)
                    eng.tensor_tensor(h[:, :], h1[:, :], ps_h[n % 2][:, FF1:], ALU.mult).then_inc(h_ok.sem, 1)

                distances(px, 0, 0)
                cubes(px, 0, 0)
                bases(px, 0, 0)

                def step(turn, n):
                    product(turn, n)
                    if exists(turn, n + 1):
                        distances(px, turn, n + 1)
                        cubes(px, turn, n + 1)
                    distances(ph, turn, n)
                    if exists(turn, n + 1):
                        bases(px, turn, n + 1)
                    cubes(ph, turn, n)
                    bases(ph, turn, n)

                tiles(eng, step)


def combine(nc, ctx, x_sb, y_dram, place, shares, out):
    with ExitStack() as own:
        y = [own.enter_context(nc.sbuf_tensor(f"y{k}", [P, TILES, P], F32)) for k in range(CHOICES)]
        fetched = [ctx.enter_context(nc.semaphore(f"fetched{g}")) for g in range(TURNS)]
        added = ctx.enter_context(nc.semaphore("y_added"))
        stored = ctx.enter_context(nc.semaphore("stored"))
        out_v = out.rearrange("(t p) c -> p t c", p=P)
        with nc.Block() as block:
            @block.gpsimd
            def _(eng):
                for t in range(TILES):
                    for k in range(CHOICES):
                        eng.indirect_dma_start(
                            out=y[k][:, t, :], out_offset=None, in_=y_dram,
                            in_offset=bass.IndirectOffsetOnAxis(ap=place[k][:, t:t + 1], axis=0))\
                           .then_inc(fetched[t // GROUP], 16)

            @block.vector
            def _(eng):
                for t in range(TILES):
                    if t % GROUP == 0:
                        eng.wait_ge(fetched[t // GROUP], 16 * CHOICES * GROUP)
                    for k in range(CHOICES):
                        if k:
                            eng.wait_ge(added, CHOICES * t + k)
                        eng.scalar_tensor_tensor(x_sb[:, t, :], y[k][:, t, :], shares[k][:, t:t + 1],
                                                 x_sb[:, t, :], ALU.mult, ALU.add).then_inc(added, 1)

            @block.sync
            def _(eng):
                for g in range(TURNS):
                    at = slice(g * GROUP, (g + 1) * GROUP)
                    eng.wait_ge(added, CHOICES * GROUP * (g + 1))
                    eng.dma_start(out_v[:, at, :], x_sb[:, at, :]).then_inc(stored, 16)
                eng.wait_ge(stored, 16 * TURNS)


def build(nc, d, out, stop=9):
    with ExitStack() as ctx:
        def sb(name, shape, dt=F32):
            return ctx.enter_context(nc.sbuf_tensor(name, shape, dt))

        def sem(name):
            return ctx.enter_context(nc.semaphore(name))

        x_sb = sb("x_sb", [P, TILES, P])
        consts = sb("consts", [P, C_END])
        ident = consts[:, C_ID:C_ID + P]
        head_cols = consts[:, C_HEAD:C_HEAD + HEADS]
        w0_sb = sb("w0_sb", [P, 4 * P])
        s_x = sem("s_x")
        s_c = sem("s_c")
        s_w0 = sem("s_w0")
        s_out = sem("s_out")

        with ExitStack() as own:
            bias0 = own.enter_context(nc.sbuf_tensor("bias0", [P, HEADS, BLK], F32))
            pads0 = own.enter_context(nc.sbuf_tensor("pads0", [P, HEADS, 2 * NEIGH], F32))
            filled = sem("filled")

            def load0(eng):
                eng.dma_start(x_sb[:, :, :], d["x"].rearrange("(t p) c -> p t c", p=P)).then_inc(s_x, 16)
                eng.dma_start(consts[:, :], d["consts"]).then_inc(s_c, 16)
                eng.dma_start(w0_sb[:, :], d["w0"]).then_inc(s_w0, 16)
                eng.dma_start(bias0[:, :, :], d["bias0"]).then_inc(s_w0, 16)
                eng.dma_start(pads0[:, :, :], d["pads0"]).then_inc(s_w0, 16)

            def arrived0(eng):
                eng.wait_ge(s_x, 16)
                eng.wait_ge(s_c, 16)
                eng.wait_ge(s_w0, 48)

            def fill0(eng, logits):
                for lg in logits:
                    eng.tensor_copy(lg[:, :, BLK:BLK + 2 * NEIGH], pads0[:, :, :]).then_inc(filled, 1)
                eng.wait_ge(filled, 2)

            attention(nc, ctx, "a0", x_sb, ident, head_cols, load0, arrived0, BLK + 2 * NEIGH,
                      lambda g, t: bias0[:, :, :], fill0,
                      {n: w0_sb[:, i * P:(i + 1) * P] for i, n in enumerate(("wq", "wk", "wv", "wo"))}, 1e-6)

        w12_dram = nc.dram_tensor("w12_dram", (EXPERTS * P, W12), F32).ap()
        w3_dram = nc.dram_tensor("w3_dram", (EXPERTS * P, W3), F32).ap()
        slots_dram = nc.dram_tensor("slots_dram", (SLOTS, P), F32).ap()
        y_dram = nc.dram_tensor("y_dram", (SLOTS, P), F32).ap()
        window_bias = sb("window_bias", [P, WINDOWS // 2, HEADS, BLK])
        place = [sb(f"place{k}", [P, TILES], U32) for k in range(CHOICES)]
        shares = [sb(f"shares{k}", [P, TILES]) for k in range(CHOICES)]
        lots = sb("lots", [P, SLOT_TILES], U32)

        with ExitStack() as own:
            work = spline_weights(nc, lambda name, shape: own.enter_context(nc.sbuf_tensor(f"sw_{name}", shape, F32)),
                                  lambda name: sem(f"sw_{name}"), d, w12_dram, w3_dram, window_bias)
            gelu_experts(nc, ctx, x_sb, consts, d, work)

        with ExitStack() as own:
            w1_sb = own.enter_context(nc.sbuf_tensor("w1_sb", [P, 4 * P + 2], F32))
            rows1 = own.enter_context(nc.sbuf_tensor("rows1", [P, 2 * P], F32))
            zero = own.enter_context(nc.sbuf_tensor("zero", [P, SLOT_TILES * P], F32))
            s_w1 = sem("s_w1")
            s_zero = sem("s_zero")
            s_cleared = sem("s_cleared")

            def load1(eng):
                eng.dma_start(w1_sb[:, :], d["w1"]).then_inc(s_w1, 16)
                eng.dma_start(rows1[:, :], d["rows1"]).then_inc(s_w1, 16)
                eng.wait_ge(s_zero, 1)
                eng.dma_start(slots_dram.rearrange("(p t) c -> p (t c)", p=P), zero[:, :]).then_inc(s_cleared, 16)
                eng.wait_ge(s_cleared, 16)

            def arrived1(eng):
                eng.wait_ge(s_w1, 32)

            def fill1(eng, logits):
                eng.memset(zero[:, :], 0.0).then_inc(s_zero, 1)

            w = {n: w1_sb[:, i * P:(i + 1) * P] for i, n in enumerate(("wq", "wk", "wv", "wo"))}
            w |= {"bq": w1_sb[:, 4 * P:4 * P + 1], "bk": w1_sb[:, 4 * P + 1:4 * P + 2],
                  "bv": rows1[:, 0:P], "bp": rows1[:, P:]}
            attention(nc, ctx, "a1", x_sb, ident, head_cols, load1, arrived1, BLK,
                      lambda g, t: window_bias[:, bass.ds((g % 2) * GROUP + t, 1), :, :], fill1, w, 1e-6)

        route(nc, ctx, x_sb, consts, d, slots_dram, place, lots, shares)
        spline_experts(nc, ctx, ident, slots_dram, y_dram, w12_dram, w3_dram, lots)
        combine(nc, ctx, x_sb, y_dram, place, shares, out)


def constants():
    c = np.zeros((P, C_END), np.float32)
    lane = np.arange(P)
    c[:, C_ID:C_ID + P] = np.eye(P)
    c[lane, C_HEAD + lane // DK] = 1.0
    c[:, C_UPPER:C_UPPER + P] = lane[:, None] < lane[None, :]
    c[:, C_ONES:C_ONES + P] = 1.0
    e = np.arange(EXPERTS)
    c[:, C_EARLIER:C_TILE] = (e[None, :] < e[:, None]).reshape(1, -1)
    c[:, C_TILE:C_LANE] = np.arange(SLOT_TILES) * P
    c[:, C_LANE] = lane
    return c


def layouts(i):
    a = {k: np.asarray(v) for k, v in i.items()}
    f = np.float32
    d = {"x": a["x"].reshape(TOKENS, P), "consts": constants()}
    wqkv = a["L0_conv_W_qkv"]
    d["w0"] = np.concatenate([wqkv, a["L0_conv_W_out"]], 1)
    keys = np.full((HEADS, BLK, BLK + 2 * NEIGH), FAR, f)
    for s in range(BLK):
        keys[:, s, s:s + 2 * NEIGH + 1] = a["L0_conv_pos_bias"][:, s, :]
    rows = keys.reshape(PAIRS, 2 * BLK, -1).transpose(1, 0, 2)
    rows = np.repeat(rows, 2, 1)
    d["bias0"] = rows[:, :, NEIGH:NEIGH + BLK]
    d["pads0"] = np.concatenate([rows[:, :, :NEIGH], rows[:, :, NEIGH + BLK:]], 2)
    w1 = np.concatenate([a["L0_ffn_rw1"], a["L0_ffn_sw1"]])
    w2 = np.concatenate([a["L0_ffn_rw2"], a["L0_ffn_sw2"]])
    b1 = np.concatenate([a["L0_ffn_rb1"], a["L0_ffn_sb1"]])
    n = len(w1)
    d["experts0"] = np.concatenate([
        w1.transpose(0, 2, 1),
        w2.reshape(n, P, CH0, P).transpose(0, 3, 2, 1).reshape(n, P, FF0),
        b1.reshape(n, CH0, P).transpose(0, 2, 1)], 2)
    d["b2"] = np.concatenate([a["L0_ffn_rb2"], a["L0_ffn_sb2"]])
    d["gate0"] = np.concatenate([a["L0_ffn_gate_w"].T, np.tile(a["L0_ffn_gate_b"], (P, 1))], 1)
    d["w1"] = np.concatenate([a["L1_conv_Wq"].T, a["L1_conv_Wk"].T, a["L1_conv_Wv"].T, a["L1_conv_Wp"].T,
                              a["L1_conv_bq"][:, None], a["L1_conv_bk"][:, None]], 1)
    d["rows1"] = np.tile(np.concatenate([a["L1_conv_bv"], a["L1_conv_bp"]]), (P, 1))
    d["pos1"] = a["L1_conv_pos_bias"].reshape(PAIRS, P, BLK).transpose(1, 0, 2)
    mask = a["L1_conv_mask"].reshape(WINDOWS, BLK, BLK).transpose(1, 0, 2)
    d["mask1"] = np.concatenate([mask, mask])
    d["gate1"] = a["L1_ffn_gate_w"].T
    def layer(n):
        base = a[f"L1_ffn_base_w{n}"].transpose(0, 2, 1)[:, :, None, :]
        spline = a[f"L1_ffn_spline_w{n}"].transpose(0, 2, 3, 1)
        return np.concatenate([spline, base], 2), a[f"L1_ffn_scaler_w{n}"].transpose(0, 2, 1)
    (f1, s1), (f2, s2), (f3, s3) = layer(1), layer(2), layer(3)
    split = lambda m: m.reshape(EXPERTS, CH1, P, -1).transpose(0, 2, 1, 3).reshape(EXPERTS, P, -1)
    d["experts1"] = np.concatenate([np.concatenate([f1, f2], 3).reshape(EXPERTS, P, W12), split(f3)], 2)
    d["scalers1"] = np.concatenate([s1, s2, split(s3)], 2)
    return {k: np.ascontiguousarray(v) for k, v in d.items()}


def kernel(**inputs):
    import concourse.bacc as bacc
    from concourse.bass_utils import run_bass_kernel_spmd as run

    nc = bacc.Bacc("TRN2", target_bir_lowering=False, num_devices=1)
    arrays = layouts(inputs)
    d = {n: nc.dram_tensor(f"in_{n}", a.shape, mybir.dt.from_np(a.dtype), kind="ExternalInput").ap()
         for n, a in arrays.items()}
    out = nc.dram_tensor("out", (TOKENS, P), F32, kind="ExternalOutput").ap()
    build(nc, d, out)
    r = run(nc, [{f"in_{n}": a for n, a in arrays.items()}], core_ids=[0])
    return r.results[0]["out"].reshape(2, 16, 64, P)
```

```python
from contextlib import ExitStack

import concourse.bass as bass
import numpy as np
from concourse import mybir

F32 = mybir.dt.float32
U32 = mybir.dt.uint32
I32 = mybir.dt.int32
ACT = mybir.ActivationFunctionType
ALU = mybir.AluOpType
X = mybir.AxisListType.X

P = 128
TOKENS = 2048
TILES = TOKENS // P
GROUP = 4
TURNS = TILES // GROUP
HEADS = 8
DK = 16
PAIRS = HEADS // 2
BLK = 64
NEIGH = 3
FAR = -1.0e30
WINDOWS = 16
EXPERTS = 8
SHARED = 2
FF0 = 512
CH0 = FF0 // P
ROW0 = 2 * FF0 + CH0
FF1 = 256
CH1 = FF1 // P
BASES = 8
FEAT = BASES + 1
W12 = FEAT * 2 * FF1
W3 = CH1 * FEAT * P
ROW1 = W12 + W3
SCAL12 = 2 * FF1
SCAL1 = SCAL12 + CH1 * P
CHOICES = 2
SLOT_TILES = CHOICES * TOKENS // P + EXPERTS - 1
SLOTS = SLOT_TILES * P
KNOTS_PER_UNIT = 2.5
FIRST_CENTRE = -3.5

C_ID = 0
C_HEAD = C_ID + P
C_UPPER = C_HEAD + HEADS
C_ONES = C_UPPER + P
C_EARLIER = C_ONES + P
C_TILE = C_EARLIER + EXPERTS * EXPERTS
C_LANE = C_TILE + SLOT_TILES
C_END = C_LANE + 1


class Count:

    def __init__(self, sem, per_turn, credit=0):
        self.sem, self.per_turn, self.credit = sem, per_turn, credit

    def give_credit(self, eng):
        eng.sem_inc(self.sem, self.credit)

    def wait(self, eng, turn, n):
        eng.wait_ge(self.sem, turn * self.per_turn + (self.credit + n))


class Chain:

    def __init__(self, eng, sem, turn=0, per_turn=0, done=0):
        self.eng, self.sem, self.turn, self.per_turn, self.done = eng, sem, turn, per_turn, done

    def after(self, ins):
        ins.then_inc(self.sem, 1)
        self.done += 1
        self.eng.wait_ge(self.sem, self.turn * self.per_turn + self.done if self.per_turn else self.done)


def layer_norm_stats(sb, sem, tag, x_sb, eps):
    stats = sb(f"{tag}_stats", [P, TILES, 6])
    moments = sb(f"{tag}_moments", [P, TILES, 2])
    dev = sb(f"{tag}_dev", [P, TILES])
    rstd = sb(f"{tag}_rstd", [P, TILES])
    s_stats, s_mom, s_dev, s_rstd = (sem(f"{tag}_{n}") for n in ("s_stats", "s_mom", "s_dev", "s_rstd"))

    def vector(eng):
        for t in range(TILES):
            eng.bn_stats(stats[:, t, :], x_sb[:, t, :]).then_inc(s_stats, 1)
        for t in range(TILES):
            eng.wait_ge(s_stats, t + 1)
            eng.bn_aggr(moments[:, t, :], stats[:, t, :]).then_inc(s_mom, 1)
        eng.wait_ge(s_mom, TILES)
        eng.tensor_scalar(dev[:, :], moments[:, :, 1], eps, None, ALU.add).then_inc(s_mom, 1)
        eng.wait_ge(s_dev, 1)
        eng.reciprocal(rstd[:, :], dev[:, :]).then_inc(s_rstd, 1)
        eng.wait_ge(s_rstd, 1)

    def scalar(eng):
        eng.wait_ge(s_mom, TILES + 1)
        eng.activation(dev[:, :], dev[:, :], ACT.Sqrt).then_inc(s_dev, 1)

    return moments, rstd, vector, scalar


def attention(nc, ctx, tag, x_sb, ident, head_cols, load, arrived, keys, bias_of, fill, w, eps):
    bq, bk, bv, bp = w.get("bq"), w.get("bk"), w.get("bv"), w.get("bp")
    with ExitStack() as own:
        def sb(name, shape, dt=F32):
            return own.enter_context(nc.sbuf_tensor(f"{tag}_{name}", shape, dt))

        def ps(name, shape):
            return own.enter_context(nc.psum_tensor(f"{tag}_{name}", shape, F32))

        def sem(name):
            return ctx.enter_context(nc.semaphore(f"{tag}_{name}"))

        moments, rstd, stats_vector, stats_scalar = layer_norm_stats(sb, sem, "ln", x_sb, eps)
        xn = sb("xn", [P, GROUP, P])
        xnT = sb("xnT", [P, GROUP * P])
        qT = sb("qT", [P, GROUP * P])
        kT = sb("kT", [P, GROUP * P])
        v = sb("v", [P, GROUP, P])
        q_heads = sb("q_heads", [P, 2 * GROUP, HEADS, BLK])
        logits = [sb(f"logits{i}", [P, HEADS, keys]) for i in range(2)]
        probs = [sb(f"probs{i}", [P, HEADS, keys]) for i in range(2)]
        weights = [sb(f"weights{i}", [P, HEADS, BLK]) for i in range(2)]
        probsT = [sb(f"probsT{i}", [P, PAIRS, P]) for i in range(2)]
        top = sb("top", [P, 2, HEADS])
        total = sb("total", [P, 2, HEADS])
        z = sb("z", [P, GROUP, P])
        zT = sb("zT", [P, GROUP * P])
        res = sb("res", [P, GROUP, P])

        ps_T = ps("ps_T", [P, GROUP, P])
        ps_qk = ps("ps_qk", [P, GROUP * P])
        ps_v = ps("ps_v", [P, GROUP, P])
        ps_S = [ps(f"ps_S{i}", [P, HEADS, BLK]) for i in range(2)]
        ps_P = ps("ps_P", [P, PAIRS, P])
        ps_Z = [ps(f"ps_Z{i}", [P, GROUP, P]) for i in range(2)]

        normed = Count(sem("normed"), GROUP)
        turned = Count(sem("turned"), 2, credit=2)
        turned_out = Count(sem("turned_out"), 2, credit=2)
        proj = Count(sem("proj"), 3, credit=3)
        q_out = Count(sem("q_out"), 1, credit=1)
        k_out = Count(sem("k_out"), 1, credit=1)
        v_out = Count(sem("v_out"), 1)
        heads = Count(sem("heads"), 1, credit=1)
        scored = Count(sem("scored"), GROUP)
        biased = Count(sem("biased"), GROUP, credit=2)
        shifted = Count(sem("shifted"), GROUP, credit=2)
        exped = Count(sem("exped"), GROUP)
        inv = Count(sem("inv"), GROUP)
        norm_p = Count(sem("norm_p"), GROUP, credit=2)
        probs_turned = Count(sem("probs_turned"), GROUP, credit=2)
        probsT_out = Count(sem("probsT_out"), GROUP, credit=1)
        mixed = Count(sem("mixed"), GROUP, credit=2)
        z_out = Count(sem("z_out"), 2, credit=2)
        out_done = Count(sem("out_done"), 1)
        added = Count(sem("added"), 1, credit=1)
        s_chain = sem("chain")
        gate = sem("gate")
        CHAIN = 2 * GROUP + (bp is not None)

        with nc.Block() as block:
            @block.sync
            def _(eng):
                load(eng)

            @block.tensor
            def _(eng):
                turned_out.give_credit(eng)
                q_out.give_credit(eng)
                k_out.give_credit(eng)
                biased.give_credit(eng)
                probsT_out.give_credit(eng)
                z_out.give_credit(eng)
                added.give_credit(eng)
                arrived(eng)

                def score(g, t):
                    biased.wait(eng, g, t - 1)
                    for hp in range(PAIRS):
                        for b in range(2):
                            at = (2 * t + b) * BLK
                            mm = eng.matmul(ps_S[t % 2][:, 2 * hp + b, :],
                                            q_heads[:, 2 * t + b, 2 * hp:2 * hp + 2, :],
                                            kT[:, at:at + BLK], start=True, stop=True)
                    mm.then_inc(scored.sem, 1)

                def turn_probs(g, t):
                    norm_p.wait(eng, g, t + 1)
                    probsT_out.wait(eng, g, t)
                    for hp in range(PAIRS):
                        mm = eng.transpose(ps_P[:, hp, :],
                                           weights[t % 2][:, 2 * hp:2 * hp + 2, :], ident)
                    mm.then_inc(probs_turned.sem, 1)

                def mix(g, t):
                    probsT_out.wait(eng, g, t + 1)
                    eng.sem_inc(gate, 1)
                    for h in range(HEADS):
                        for b in range(2):
                            rows = slice(b * BLK, (b + 1) * BLK)
                            cols = slice((h % 2) * BLK, (h % 2 + 1) * BLK)
                            mm = eng.matmul(ps_Z[b][rows, t, h * DK:(h + 1) * DK],
                                            probsT[t % 2][rows, h // 2, cols],
                                            v[rows, t, h * DK:(h + 1) * DK], start=True, stop=True)
                    mm.then_inc(mixed.sem, 1)

                with eng.Fori(0, TURNS) as g:
                    turned_out.wait(eng, g, 0)
                    for t in range(GROUP):
                        normed.wait(eng, g, t + 1)
                        mm = eng.transpose(ps_T[:, t, :], xn[:, t, :], ident)
                    mm.then_inc(turned.sem, 1)
                    turned_out.wait(eng, g, 1)
                    k_out.wait(eng, g, 0)
                    eng.matmul(ps_qk[:, :], w["wq"], xnT[:, :], start=True, stop=True).then_inc(proj.sem, 1)
                    added.wait(eng, g, 0)
                    for t in range(GROUP):
                        mm = eng.matmul(ps_v[:, t, :], xnT[:, t * P:(t + 1) * P], w["wv"], start=True, stop=True)
                    mm.then_inc(proj.sem, 1)
                    q_out.wait(eng, g, 1)
                    eng.matmul(ps_qk[:, :], w["wk"], xnT[:, :], start=True, stop=True).then_inc(proj.sem, 1)
                    heads.wait(eng, g, 1)
                    k_out.wait(eng, g, 1)
                    for s in range(GROUP + 2):
                        if s < GROUP:
                            score(g, s)
                        if 0 <= s - 1 < GROUP:
                            turn_probs(g, s - 1)
                        if s - 2 == 0:
                            v_out.wait(eng, g, 1)
                            z_out.wait(eng, g, 0)
                        if 0 <= s - 2 < GROUP:
                            mix(g, s - 2)
                    z_out.wait(eng, g, 2)
                    for t in range(GROUP):
                        mm = eng.transpose(ps_T[:, t, :], z[:, t, :], ident)
                    mm.then_inc(turned.sem, 1)
                    turned_out.wait(eng, g, 2)
                    for t in range(GROUP):
                        mm = eng.matmul(ps_v[:, t, :], zT[:, t * P:(t + 1) * P], w["wo"], start=True, stop=True)
                    mm.then_inc(out_done.sem, 1)

            @block.scalar
            def _(eng):
                turned.give_credit(eng)
                norm_p.give_credit(eng)
                heads.give_credit(eng)
                probs_turned.give_credit(eng)
                mixed.give_credit(eng)
                arrived(eng)
                stats_scalar(eng)
                eng.preload_act_table(ACT.Exp)

                def expo(g, t):
                    shifted.wait(eng, g, t + 1)
                    eng.activation(probs[t % 2][:, :, :], probs[t % 2][:, :, :], ACT.Exp)\
                       .then_inc(exped.sem, 1)

                def copy_probsT(g, t):
                    probs_turned.wait(eng, g, t + 1)
                    mixed.wait(eng, g, t - 1)
                    eng.activation(probsT[t % 2][:, :, :], ps_P[:, :, :], ACT.Copy)\
                       .then_inc(probsT_out.sem, 1)

                with eng.Fori(0, TURNS) as g:
                    turned.wait(eng, g, 1)
                    proj.wait(eng, g, 0)
                    eng.activation(xnT[:, :], ps_T[:, :, :], ACT.Copy).then_inc(turned_out.sem, 1)
                    proj.wait(eng, g, 1)
                    heads.wait(eng, g, 0)
                    if bq is not None:
                        eng.activation(qT[:, :], ps_qk[:, :], ACT.Identity, bias=bq).then_inc(q_out.sem, 1)
                    else:
                        eng.activation(qT[:, :], ps_qk[:, :], ACT.Copy).then_inc(q_out.sem, 1)
                    proj.wait(eng, g, 3)
                    if bk is not None:
                        eng.activation(kT[:, :], ps_qk[:, :], ACT.Identity, bias=bk).then_inc(k_out.sem, 1)
                    else:
                        eng.activation(kT[:, :], ps_qk[:, :], ACT.Copy).then_inc(k_out.sem, 1)
                    for s in range(GROUP + 1):
                        if s < GROUP:
                            expo(g, s)
                        if 0 <= s - 1 < GROUP:
                            copy_probsT(g, s - 1)
                    mixed.wait(eng, g, GROUP)
                    for b in range(2):
                        rows = slice(b * BLK, (b + 1) * BLK)
                        eng.activation(z[rows, :, :], ps_Z[b][rows, :, :], ACT.Copy).then_inc(z_out.sem, 1)
                    turned.wait(eng, g, 2)
                    eng.activation(zT[:, :], ps_T[:, :, :], ACT.Copy).then_inc(turned_out.sem, 1)

            @block.gpsimd
            def _(eng):
                with eng.Fori(0, TURNS) as g:
                    for t in range(GROUP):
                        inv.wait(eng, g, t + 1)
                        probs_turned.wait(eng, g, t - 1)
                        eng.tensor_tensor(weights[t % 2][:, :, :], probs[t % 2][:, :, 0:BLK],
                                          total[:, t % 2, :].unsqueeze(2).to_broadcast([P, HEADS, BLK]),
                                          ALU.mult).then_inc(norm_p.sem, 1)

            @block.vector
            def _(eng):
                proj.give_credit(eng)
                shifted.give_credit(eng)
                arrived(eng)
                stats_vector(eng)
                fill(eng, logits)

                with eng.Fori(0, TURNS) as g:
                    chain = Chain(eng, s_chain, g, CHAIN)
                    turned.wait(eng, g, 0)
                    for t in range(GROUP):
                        at = bass.ds(g * GROUP + t, 1)
                        eng.tensor_scalar(xn[:, t, :], x_sb[:, at, :],
                                          moments[:, at, 0], rstd[:, at], ALU.subtract, ALU.mult)\
                           .then_inc(normed.sem, 1)
                    q_out.wait(eng, g, 1)
                    for h in range(HEADS):
                        ins = eng.tensor_scalar(q_heads[:, :, h, :], qT[:, :].rearrange("p (b i) -> p b i", i=BLK),
                                                head_cols[:, h:h + 1],
                                                float(DK) ** -0.5, ALU.mult, ALU.mult)
                    ins.then_inc(heads.sem, 1)
                    proj.wait(eng, g, 2)
                    if bv is not None:
                        eng.tensor_tensor(v[:, :, :], ps_v[:, :, :],
                                          bv.unsqueeze(1).to_broadcast([P, GROUP, P]), ALU.add)\
                           .then_inc(v_out.sem, 1)
                    else:
                        eng.tensor_copy(v[:, :, :], ps_v[:, :, :]).then_inc(v_out.sem, 1)

                    def shift(t):
                        scored.wait(eng, g, t + 1)
                        shifted.wait(eng, g, t - 1)
                        eng.tensor_tensor(logits[t % 2][:, :, 0:BLK], ps_S[t % 2][:, :, :], bias_of(g, t), ALU.add)\
                           .then_inc(biased.sem, 1)
                        biased.wait(eng, g, t + 1)
                        chain.after(eng.tensor_reduce(top[:, t % 2, :], logits[t % 2][:, :, :], X, ALU.max))
                        norm_p.wait(eng, g, t - 1)
                        eng.tensor_tensor(probs[t % 2][:, :, :], logits[t % 2][:, :, :],
                                          top[:, t % 2, :].unsqueeze(2).to_broadcast([P, HEADS, keys]),
                                          ALU.subtract).then_inc(shifted.sem, 1)

                    def row_sums(t):
                        exped.wait(eng, g, t + 1)
                        chain.after(eng.tensor_reduce(total[:, t % 2, :], probs[t % 2][:, :, :], X, ALU.add))
                        eng.reciprocal(total[:, t % 2, :], total[:, t % 2, :]).then_inc(inv.sem, 1)

                    for s in range(GROUP + 1):
                        if s < GROUP:
                            shift(s)
                        if 0 <= s - 1 < GROUP:
                            row_sums(s - 1)
                    out_done.wait(eng, g, 1)
                    at = bass.ds(g * GROUP, GROUP)
                    src = ps_v[:, :, :]
                    if bp is not None:
                        chain.after(eng.tensor_tensor(res[:, :, :], ps_v[:, :, :],
                                                      bp.unsqueeze(1).to_broadcast([P, GROUP, P]), ALU.add))
                        src = res[:, :, :]
                    eng.tensor_tensor(x_sb[:, at, :], x_sb[:, at, :], src, ALU.add).then_inc(added.sem, 1)
                    assert chain.done == CHAIN
                added.wait(eng, TURNS, 0)


def rank_experts(eng, chain, sb, scores, earlier, tag):
    shape = [P, TILES, EXPERTS, EXPERTS]
    above = sb(f"{tag}_above", shape)
    level = sb(f"{tag}_level", shape)
    rank = sb(f"{tag}_rank", [P, TILES, EXPERTS])
    other = scores.unsqueeze(2).to_broadcast(shape)
    own = scores.unsqueeze(3).to_broadcast(shape)
    first = earlier.rearrange("p (a b) -> p a b", b=EXPERTS).unsqueeze(1).to_broadcast(shape)
    eng.tensor_tensor(above[:, :, :, :], other, own, ALU.is_gt)
    chain.after(eng.tensor_tensor(level[:, :, :, :], other, own, ALU.is_equal))
    chain.after(eng.tensor_tensor(level[:, :, :, :], level[:, :, :, :], first, ALU.mult))
    chain.after(eng.tensor_tensor(above[:, :, :, :], above[:, :, :, :], level[:, :, :, :], ALU.add))
    chain.after(eng.tensor_reduce(rank[:, :, :], above[:, :, :, :], X, ALU.add))
    return rank


def gelu_experts(nc, ctx, x_sb, consts, d, pool_work):
    ident = consts[:, C_ID:C_ID + P]
    with ExitStack() as own:
        def sb(name, shape, dt=F32):
            return own.enter_context(nc.sbuf_tensor(f"f0_{name}", shape, dt))

        def ps(name, shape):
            return own.enter_context(nc.psum_tensor(f"f0_{name}", shape, F32))

        def sem(name):
            return ctx.enter_context(nc.semaphore(f"f0_{name}"))

        ALL = EXPERTS + SHARED
        moments, rstd, stats_vector, stats_scalar = layer_norm_stats(sb, sem, "ln", x_sb, 1e-5)
        xn = sb("xn", [P, TILES, P])
        nT = sb("nT", [P, TILES, P])
        gate = sb("gate", [P, 2 * EXPERTS])
        b2 = sb("b2", [ALL, P])
        probs = sb("probs", [P, TILES, EXPERTS])
        top = sb("top", [P, TILES])
        mix = sb("mix", [P, TILES, ALL])
        mixT = sb("mixT", [ALL, TILES, P])
        wt = [sb(f"wt{i}", [P, ROW0]) for i in range(2)]
        mix_now = [sb(f"mix_now{i}", [P, TILES]) for i in range(2)]
        hid = [sb(f"hid{i}", [P, CH0, GROUP * P]) for i in range(2)]
        ps_up = [ps(f"ps_up{i}", [P, GROUP * P]) for i in range(4)]
        ps_dn = [ps(f"ps_dn{i}", [P, GROUP, P]) for i in range(2)]
        ps_g = ps("ps_g", [P, TILES, EXPERTS])
        ps_t = ps_dn[0]

        HALF = ALL // 2
        STEPS = 2 * TURNS
        s_small = sem("s_small")
        s_w = [Count(sem(f"s_w{i}"), 16) for i in range(2)]
        normed = sem("normed")
        turned = sem("turned")
        turned_out = sem("turned_out")
        gated = sem("gated")
        s_exp = sem("s_exp")
        s_shift = sem("s_shift")
        mixed = sem("mixed")
        mixT_mm = sem("mixT_mm")
        mixT_out = sem("mixT_out")
        b2_mm = sem("b2_mm")
        b2_added = sem("b2_added")
        up = Count(sem("up"), STEPS * CH0)
        acted = Count(sem("acted"), STEPS * CH0, credit=4)
        down = Count(sem("down"), STEPS, credit=TURNS + 1)
        added = Count(sem("added"), STEPS * GROUP, credit=2 * GROUP)
        cols = Count(sem("cols"), 2)
        s_chain = sem("chain")

        with nc.Block() as block:
            @block.sync
            def _(eng):
                eng.dma_start(gate[:, :], d["gate0"]).then_inc(s_small, 16)
                eng.dma_start(b2[:, :], d["b2"]).then_inc(s_small, 16)
                with eng.Fori(0, HALF) as i:
                    for a in range(2):
                        down.wait(eng, i, (a - 1) * TURNS)
                        eng.dma_start(wt[a][:, :], d["experts0"][bass.ds(2 * i + a, 1), :, :])\
                           .then_inc(s_w[a].sem, 16)

            @block.tensor
            def _(eng):
                acted.give_credit(eng)
                added.give_credit(eng)
                eng.wait_ge(s_small, 32)
                for g in range(TURNS):
                    if g >= 1:
                        eng.wait_ge(turned_out, g)
                    for t in range(GROUP):
                        eng.wait_ge(normed, g * GROUP + t + 1)
                        mm = eng.transpose(ps_t[:, t, :], xn[:, g * GROUP + t, :], ident)
                    mm.then_inc(turned, 1)
                eng.wait_ge(turned_out, TURNS)
                for t in range(TILES):
                    mm = eng.matmul(ps_g[:, t, :], nT[:, t, :], gate[:, 0:EXPERTS], start=True, stop=True)
                mm.then_inc(gated, 1)
                eng.wait_ge(mixed, 1)
                for g in range(TURNS):
                    if g >= 1:
                        eng.wait_ge(mixT_out, g)
                    for t in range(GROUP):
                        mm = eng.transpose(ps_t[0:ALL, t, :], mix[:, g * GROUP + t, :], ident)
                    mm.then_inc(mixT_mm, 1)
                for g in range(TURNS):
                    eng.wait_ge(mixT_out, max(TURNS, g + 1))
                    if g >= 2:
                        eng.wait_ge(b2_added, g - 1)
                    for t in range(GROUP):
                        mm = eng.matmul(ps_dn[g % 2][:, t, :], mixT[:, g * GROUP + t, :], b2[:, :],
                                        start=True, stop=True)
                    mm.then_inc(b2_mm, 1)
                eng.wait_ge(b2_added, TURNS)

                def go_up(i, s):
                    a, g = divmod(s, TURNS)
                    if g == 0:
                        s_w[a].wait(eng, i, 16)
                    for c in range(CH0):
                        acted.wait(eng, i, s * CH0 + c + 1 - 4)
                        eng.matmul(ps_up[c][:, :], wt[a][:, c * P:(c + 1) * P],
                                   nT[:, g * GROUP:(g + 1) * GROUP, :], start=True, stop=True)\
                           .then_inc(up.sem, 1)

                def go_down(i, s):
                    a, g = divmod(s, TURNS)
                    acted.wait(eng, i, (s + 1) * CH0)
                    added.wait(eng, i, (s - 1) * GROUP)
                    for t in range(GROUP):
                        for c in range(CH0):
                            mm = eng.matmul(ps_dn[s % 2][:, t, :], hid[s % 2][:, c, t * P:(t + 1) * P],
                                            wt[a][:, FF0 + c * P:FF0 + (c + 1) * P],
                                            start=(c == 0), stop=(c == CH0 - 1))
                    mm.then_inc(down.sem, 1)

                with eng.Fori(0, HALF) as i:
                    for s in range(STEPS + 1):
                        if s < STEPS:
                            go_up(i, s)
                        if s >= 1:
                            go_down(i, s - 1)

            @block.scalar
            def _(eng):
                down.give_credit(eng)
                stats_scalar(eng)
                for g in range(TURNS):
                    eng.wait_ge(turned, g + 1)
                    eng.activation(nT[:, g * GROUP:(g + 1) * GROUP, :], ps_t[:, :, :], ACT.Copy)\
                       .then_inc(turned_out, 1)
                eng.wait_ge(s_shift, 1)
                eng.activation(probs[:, :, :], probs[:, :, :], ACT.Exp).then_inc(s_exp, 1)
                for g in range(TURNS):
                    eng.wait_ge(mixT_mm, g + 1)
                    eng.activation(mixT[:, g * GROUP:(g + 1) * GROUP, :], ps_t[0:ALL, :, :], ACT.Copy)\
                       .then_inc(mixT_out, 1)
                eng.preload_act_table(ACT.Gelu)
                with eng.Fori(0, HALF) as i:
                    for s in range(STEPS):
                        a = s // TURNS
                        down.wait(eng, i, s - 1)
                        for c in range(CH0):
                            up.wait(eng, i, s * CH0 + c + 1)
                            eng.activation(hid[s % 2][:, c, :], ps_up[c][:, :], ACT.Gelu,
                                           bias=wt[a][:, 2 * FF0 + c:2 * FF0 + c + 1]).then_inc(acted.sem, 1)

            @block.gpsimd
            def _(eng):
                pool_work(eng)

            @block.vector
            def _(eng):
                stats_vector(eng)
                for t in range(TILES):
                    eng.tensor_scalar(xn[:, t, :], x_sb[:, t, :], moments[:, t, 0:1], rstd[:, t:t + 1],
                                      ALU.subtract, ALU.mult).then_inc(normed, 1)
                eng.wait_ge(s_small, 32)
                eng.wait_ge(gated, 1)
                chain = Chain(eng, s_chain)
                wide = [P, TILES, EXPERTS]
                chain.after(eng.tensor_tensor(probs[:, :, :], ps_g[:, :, :],
                                              gate[:, EXPERTS:].unsqueeze(1).to_broadcast(wide), ALU.add))
                chain.after(eng.tensor_reduce(top[:, :], probs[:, :, :], X, ALU.max))
                eng.tensor_tensor(probs[:, :, :], probs[:, :, :], top[:, :].unsqueeze(2).to_broadcast(wide),
                                  ALU.subtract).then_inc(s_shift, 1)
                eng.wait_ge(s_exp, 1)
                chain.after(eng.tensor_reduce(top[:, :], probs[:, :, :], X, ALU.add))
                chain.after(eng.reciprocal(top[:, :], top[:, :]))
                chain.after(eng.tensor_tensor(probs[:, :, :], probs[:, :, :],
                                              top[:, :].unsqueeze(2).to_broadcast(wide), ALU.mult))
                rank = rank_experts(eng, chain, sb, probs[:, :, :], consts[:, C_EARLIER:C_TILE], "route")
                chain.after(eng.tensor_scalar(rank[:, :, :], rank[:, :, :], float(CHOICES), None, ALU.is_lt))
                eng.memset(mix[:, :, EXPERTS:], 1.0)
                eng.tensor_tensor(mix[:, :, 0:EXPERTS], rank[:, :, :], probs[:, :, :], ALU.mult)\
                   .then_inc(mixed, 1)
                eng.wait_ge(mixed, 1)
                for g in range(TURNS):
                    eng.wait_ge(b2_mm, g + 1)
                    at = slice(g * GROUP, (g + 1) * GROUP)
                    eng.tensor_tensor(x_sb[:, at, :], x_sb[:, at, :], ps_dn[g % 2][:, :, :], ALU.add)\
                       .then_inc(b2_added, 1)
                eng.wait_ge(b2_added, TURNS)
                with eng.Fori(0, HALF) as i:
                    for s in range(STEPS):
                        a, g = divmod(s, TURNS)
                        if g == 0:
                            eng.tensor_copy(mix_now[a][:, :], mix[:, :, bass.ds(2 * i + a, 1)]).then_inc(cols.sem, 1)
                            cols.wait(eng, i, a + 1)
                            added.wait(eng, i, s * GROUP)
                        down.wait(eng, i, s + 1)
                        for t in range(GROUP):
                            xt = x_sb[:, g * GROUP + t, :]
                            eng.scalar_tensor_tensor(xt, ps_dn[s % 2][:, t, :],
                                                     mix_now[a][:, g * GROUP + t:g * GROUP + t + 1], xt,
                                                     ALU.mult, ALU.add).then_inc(added.sem, 1)
                added.wait(eng, HALF, 0)


def spline_weights(nc, sb, sem, d, w12_dram, w3_dram, window_bias):
    raw = [sb(f"raw{i}", [P, ROW1]) for i in range(2)]
    scal = [sb(f"scal{i}", [P, SCAL1]) for i in range(2)]
    pos1 = sb("pos1", [P, PAIRS, BLK])
    mask1 = sb("mask1", [P, WINDOWS, BLK])
    loaded = [Count(sem(f"loaded{i}"), 32) for i in range(2)]
    stored = [Count(sem(f"stored{i}"), 32) for i in range(2)]
    scaled = Count(sem("scaled"), 2)
    prepared = Count(sem("prepared"), 4)
    s_tab = sem("s_tab")
    gate = sem("gate")
    s_added = sem("s_added")

    def work(eng):
        eng.dma_start(pos1[:, :, :], d["pos1"]).then_inc(s_tab, 16)
        eng.dma_start(mask1[:, :, :], d["mask1"]).then_inc(s_tab, 16)
        eng.wait_ge(s_tab, 32)
        shape = [P, PAIRS, 2, BLK]
        for n in range(WINDOWS // 2):
            eng.tensor_tensor(window_bias[:, n, :, :].rearrange("p (h b) k -> p h b k", b=2),
                              pos1[:, :, :].unsqueeze(2).to_broadcast(shape),
                              mask1[:, 2 * n:2 * n + 2, :].unsqueeze(1).to_broadcast(shape), ALU.add)\
               .then_inc(s_added, 1)
        with eng.Fori(0, EXPERTS // 2) as i:
            for a in range(2):
                at = bass.ds(2 * i + a, 1)
                eng.dma_start(raw[a][:, :], d["experts1"][at, :, :]).then_inc(loaded[a].sem, 16)
                eng.dma_start(scal[a][:, :], d["scalers1"][at, :, :]).then_inc(loaded[a].sem, 16)
            for a in range(2):
                loaded[a].wait(eng, i, 32)
                eng.sem_inc(gate, 1)
                eng.tensor_scalar(scal[a][:, :], scal[a][:, :], -1.0 / 6.0, None, ALU.mult)\
                   .then_inc(scaled.sem, 1)
                scaled.wait(eng, i, a + 1)
                first = raw[a][:, 0:BASES * 2 * FF1].rearrange("p (c o) -> p c o", c=BASES)
                eng.tensor_tensor(first, first, scal[a][:, 0:SCAL12].unsqueeze(1)
                                  .to_broadcast([P, BASES, 2 * FF1]), ALU.mult).then_inc(prepared.sem, 1)
                last = raw[a][:, W12:].rearrange("p (k c o) -> p k c o", k=CH1, c=FEAT)[:, :, 0:BASES, :]
                eng.tensor_tensor(last, last, scal[a][:, SCAL12:].rearrange("p (k o) -> p k o", k=CH1)
                                  .unsqueeze(2).to_broadcast([P, CH1, BASES, P]), ALU.mult)\
                   .then_inc(prepared.sem, 1)
                prepared.wait(eng, i, 2 * a + 2)
                rows = bass.ds((2 * i + a) * P, P)
                eng.dma_start(w12_dram[rows, :], raw[a][:, 0:W12]).then_inc(stored[a].sem, 16)
                eng.dma_start(w3_dram[rows, :], raw[a][:, W12:]).then_inc(stored[a].sem, 16)
            for a in range(2):
                stored[a].wait(eng, i, 32)
        eng.wait_ge(s_added, WINDOWS // 2)
    return work


def route(nc, ctx, x_sb, consts, d, slots_dram, place, lots, shares):
    ident = consts[:, C_ID:C_ID + P]
    with ExitStack() as own:
        def sb(name, shape, dt=F32):
            return own.enter_context(nc.sbuf_tensor(f"rt_{name}", shape, dt))

        def ps(name, shape):
            return own.enter_context(nc.psum_tensor(f"rt_{name}", shape, F32))

        def sem(name):
            return ctx.enter_context(nc.semaphore(f"rt_{name}"))

        moments, rstd, stats_vector, stats_scalar = layer_norm_stats(sb, sem, "ln", x_sb, 1e-5)
        wide = [P, TILES, EXPERTS]
        xn = sb("xn", [P, TILES, P])
        nT = sb("nT", [P, TILES, P])
        gate = sb("gate", [P, EXPERTS])
        scores = sb("scores", wide)
        chosen = sb("chosen", wide)
        choice = [sb(f"choice{k}", wide) for k in range(CHOICES)]
        picked = sb("picked", wide)
        value = [sb(f"value{k}", [P, TILES]) for k in range(CHOICES)]
        base = sb("base", wide)
        total = sb("total", wide)
        upto = [sb(f"upto{i}", wide) for i in range(2)]
        many = sb("many", [P, EXPERTS, TILES])
        tiles_of = sb("tiles_of", [P, EXPERTS])
        before = sb("before", [P, EXPERTS, EXPERTS])
        start = sb("start", [P, EXPERTS])
        begun = sb("begun", [P, SLOT_TILES, EXPERTS])
        owner = sb("owner", [P, SLOT_TILES])
        ps_t = ps("ps_t", [P, GROUP, P])
        ps_g = ps("ps_g", wide)
        ps_before = ps("ps_before", wide)
        ps_total = ps("ps_total", wide)
        s_gate = sem("s_gate")
        normed = sem("normed")
        turned = sem("turned")
        turned_out = sem("turned_out")
        gated = sem("gated")
        chosen_ok = sem("chosen_ok")
        counted = sem("counted")
        s_gap = sem("s_gap")
        s_exp = sem("s_exp")
        placed = sem("placed")
        scattered = sem("scattered")
        s_chain = sem("chain")

        with nc.Block() as block:
            @block.sync
            def _(eng):
                eng.dma_start(gate[:, :], d["gate1"]).then_inc(s_gate, 16)

            @block.tensor
            def _(eng):
                eng.wait_ge(s_gate, 16)
                for g in range(TURNS):
                    if g >= 1:
                        eng.wait_ge(turned_out, g)
                    for t in range(GROUP):
                        eng.wait_ge(normed, g * GROUP + t + 1)
                        mm = eng.transpose(ps_t[:, t, :], xn[:, g * GROUP + t, :], ident)
                    mm.then_inc(turned, 1)
                eng.wait_ge(turned_out, TURNS)
                for t in range(TILES):
                    mm = eng.matmul(ps_g[:, t, :], nT[:, t, :], gate[:, :], start=True, stop=True)
                mm.then_inc(gated, 1)
                eng.wait_ge(chosen_ok, 1)
                eng.matmul(ps_before[:, :, :], consts[:, C_UPPER:C_UPPER + P], chosen[:, :, :],
                           start=True, stop=True)
                eng.matmul(ps_total[:, :, :], consts[:, C_ONES:C_ONES + P], chosen[:, :, :],
                           start=True, stop=True).then_inc(counted, 1)

            @block.scalar
            def _(eng):
                stats_scalar(eng)
                for g in range(TURNS):
                    eng.wait_ge(turned, g + 1)
                    eng.activation(nT[:, g * GROUP:(g + 1) * GROUP, :], ps_t[:, :, :], ACT.Copy)\
                       .then_inc(turned_out, 1)
                eng.wait_ge(s_gap, 1)
                eng.activation(value[1][:, :], value[1][:, :], ACT.Exp).then_inc(s_exp, 1)

            @block.vector
            def _(eng):
                stats_vector(eng)
                for t in range(TILES):
                    eng.tensor_scalar(xn[:, t, :], x_sb[:, t, :], moments[:, t, 0:1], rstd[:, t:t + 1],
                                      ALU.subtract, ALU.mult).then_inc(normed, 1)
                eng.wait_ge(gated, 1)
                chain = Chain(eng, s_chain)
                chain.after(eng.tensor_copy(scores[:, :, :], ps_g[:, :, :]))
                rank = rank_experts(eng, chain, sb, scores[:, :, :], consts[:, C_EARLIER:C_TILE], "route")
                for k in range(CHOICES):
                    chain.after(eng.tensor_scalar(choice[k][:, :, :], rank[:, :, :], float(k), None, ALU.is_equal))
                eng.tensor_tensor(chosen[:, :, :], choice[0][:, :, :], choice[1][:, :, :], ALU.add)\
                   .then_inc(chosen_ok, 1)
                for k in range(CHOICES):
                    chain.after(eng.tensor_tensor(picked[:, :, :], choice[k][:, :, :], scores[:, :, :], ALU.mult))
                    chain.after(eng.tensor_reduce(value[k][:, :], picked[:, :, :], X, ALU.add))
                eng.tensor_tensor(value[1][:, :], value[1][:, :], value[0][:, :], ALU.subtract).then_inc(s_gap, 1)

                eng.wait_ge(counted, 1)
                chain.after(eng.tensor_copy(total[:, :, :], ps_total[:, :, :]))
                chain.after(eng.tensor_copy(upto[0][:, :, :], total[:, :, :]))
                a, step = 0, 1
                while step < TILES:
                    new, old = upto[1 - a], upto[a]
                    eng.tensor_copy(new[:, 0:step, :], old[:, 0:step, :])
                    chain.after(eng.tensor_tensor(new[:, step:, :], old[:, step:, :], old[:, 0:TILES - step, :],
                                                  ALU.add))
                    a, step = 1 - a, 2 * step
                starts = consts[:, C_TILE:C_TILE + SLOT_TILES]
                shape = [P, EXPERTS, TILES]
                chain.after(eng.tensor_tensor(many[:, :, :], upto[a][:, TILES - 1, :].unsqueeze(2).to_broadcast(shape),
                                              starts[:, 0:TILES].unsqueeze(1).to_broadcast(shape), ALU.is_gt))
                chain.after(eng.tensor_reduce(tiles_of[:, :], many[:, :, :], X, ALU.add))
                shape = [P, EXPERTS, EXPERTS]
                chain.after(eng.tensor_tensor(
                    before[:, :, :], tiles_of[:, :].unsqueeze(1).to_broadcast(shape),
                    consts[:, C_EARLIER:C_TILE].rearrange("p (a b) -> p a b", b=EXPERTS), ALU.mult))
                chain.after(eng.tensor_reduce(start[:, :], before[:, :, :], X, ALU.add))
                chain.after(eng.tensor_scalar(start[:, :], start[:, :], float(P), None, ALU.mult))
                chain.after(eng.tensor_tensor(base[:, :, :], upto[a][:, :, :], total[:, :, :], ALU.subtract))
                chain.after(eng.tensor_tensor(base[:, :, :], base[:, :, :], ps_before[:, :, :], ALU.add))
                chain.after(eng.tensor_tensor(base[:, :, :], base[:, :, :],
                                              start[:, :].unsqueeze(1).to_broadcast(wide), ALU.add))
                for k in range(CHOICES):
                    chain.after(eng.tensor_tensor(picked[:, :, :], choice[k][:, :, :], base[:, :, :], ALU.mult))
                    chain.after(eng.tensor_reduce(total[:, :, k], picked[:, :, :], X, ALU.add))
                    eng.tensor_copy(place[k][:, :], total[:, :, k]).then_inc(placed, 1)
                shape = [P, SLOT_TILES, EXPERTS]
                chain.after(eng.tensor_tensor(begun[:, :, :], start[:, :].unsqueeze(1).to_broadcast(shape),
                                              starts.unsqueeze(2).to_broadcast(shape), ALU.is_le))
                chain.after(eng.tensor_reduce(owner[:, :], begun[:, :, :], X, ALU.add))
                chain.after(eng.tensor_scalar(owner[:, :], owner[:, :], float(P), consts[:, C_LANE:C_LANE + 1],
                                              ALU.mult, ALU.add))
                chain.after(eng.tensor_scalar(lots[:, :], owner[:, :], -float(P), None, ALU.add))
                eng.wait_ge(s_exp, 1)
                chain.after(eng.tensor_scalar(value[0][:, :], value[1][:, :], 1.0, None, ALU.add))
                chain.after(eng.reciprocal(shares[0][:, :], value[0][:, :]))
                chain.after(eng.tensor_tensor(shares[1][:, :], value[1][:, :], shares[0][:, :], ALU.mult))

            @block.gpsimd
            def _(eng):
                eng.wait_ge(placed, CHOICES)
                for k in range(CHOICES):
                    for t in range(TILES):
                        eng.indirect_dma_start(
                            out=slots_dram, out_offset=bass.IndirectOffsetOnAxis(ap=place[k][:, t:t + 1], axis=0),
                            in_=xn[:, t, :], in_offset=None).then_inc(scattered, 16)
                eng.wait_ge(scattered, 16 * CHOICES * TILES)


class TileCount:

    def __init__(self, sem, times=1):
        self.sem, self.times = sem, times
        self.credit = 2 * times

    def give_credit(self, eng):
        eng.sem_inc(self.sem, self.credit)

    def wait(self, eng, turn, n):
        eng.wait_ge(self.sem, turn * (2 * self.times) + ((n + 1) * self.times + self.credit))


class ArrivalCount:

    def __init__(self, even, odd, credit=0):
        self.sems, self.credit = (even, odd), credit

    def give_credit(self, eng):
        for s in self.sems:
            eng.sem_inc(s, self.credit)

    def of(self, n):
        return self.sems[n % 2]

    def wait(self, eng, turn, n):
        eng.wait_ge(self.sems[n % 2], turn * 16 + (16 * (n // 2 + 1) + self.credit))


def spline_experts(nc, ctx, ident, slots_dram, y_dram, w12_dram, w3_dram, lots):
    with ExitStack() as own:
        def sb(name, shape, dt=F32):
            return own.enter_context(nc.sbuf_tensor(f"kan_{name}", shape, dt))

        def ps(name, shape):
            return own.enter_context(nc.psum_tensor(f"kan_{name}", shape, F32))

        def sem(name):
            return ctx.enter_context(nc.semaphore(f"kan_{name}"))

        def pair(name, credit=0):
            return ArrivalCount(sem(name + "0"), sem(name + "1"), credit)

        w12 = [sb(f"w12_{i}", [P, W12]) for i in range(2)]
        w3 = [sb(f"w3_{i}", [P, W3]) for i in range(2)]
        slot_x = [sb(f"slot_x{i}", [P, P]) for i in range(2)]
        y_sb = [sb(f"y_sb{i}", [P, P]) for i in range(2)]
        h1 = sb("h1", [P, FF1])
        h = sb("h", [P, FF1])
        h_u = sb("h_u", [P, FF1])
        offsets = sb("offsets", [P, BASES + 1])
        minus2 = offsets[:, BASES:BASES + 1]

        class Part:

            def __init__(self, tag, n, ahead):
                self.t = [sb(f"{tag}t{i}", [P, BASES, n]) for i in range(ahead)] * (3 - ahead)
                self.f = [sb(f"{tag}f{i}", [P, BASES, n]) for i in range(ahead)] * (3 - ahead)
                self.s = [sb(f"{tag}s{i}", [P, n]) for i in range(2)]
                self.near = sb(tag + "near", [P, BASES, n])
                self.far = sb(tag + "far", [P, BASES, n])
                self.turned = TileCount(sem(tag + "turned"))
                self.dist = TileCount(sem(tag + "dist"))
                self.near_square = TileCount(sem(tag + "near_square"))
                self.far_square = TileCount(sem(tag + "far_square"))
                self.near_cube = TileCount(sem(tag + "near_cube"))
                self.far_cube = TileCount(sem(tag + "far_cube"))
                self.near_part = TileCount(sem(tag + "near_part"))
                self.silu = TileCount(sem(tag + "silu"))
                self.ready = TileCount(sem(tag + "ready"))
                self.used = TileCount(sem(tag + "used"))

        px, ph = Part("x", P, 2), Part("h", FF1, 1)
        ps_x = [ps(f"ps_x{i}", [P, P]) for i in range(2)]
        ps_h = [ps(f"ps_h{i}", [P, 2 * FF1]) for i in range(2)]
        ps_ht = ps("ps_ht", [P, CH1, P])
        ps_y = ps("ps_y", [P, P])
        in_x, in_12, in_3 = pair("in_x"), pair("in_12"), pair("in_3")
        out_y = pair("out_y", 16)
        offsets_ok = sem("offsets_ok")
        gate = sem("gate")
        u_ok = TileCount(sem("u_ok"))
        offset_ok = TileCount(sem("offset_ok"))
        h1_ok = TileCount(sem("h1_ok"))
        h_ok = TileCount(sem("h_ok"))
        y_ok = TileCount(sem("y_ok"))

        LAST = SLOT_TILES - 1
        AFTER = 4
        LOOP = (SLOT_TILES - 1 - AFTER) // 2
        assert 1 + 2 * LOOP + AFTER == SLOT_TILES

        def tiles(eng, step):
            step(0, 0)
            with eng.Fori(0, LOOP) as i:
                step(i, 1)
                step(i, 2)
            for n in range(1, AFTER + 1):
                step(LOOP, n)

        def exists(turn, n):
            return not isinstance(turn, int) or 0 <= 2 * turn + n <= LAST

        with nc.Block() as block:
            @block.sync
            def _(eng):
                px.turned.give_credit(eng)
                px.used.give_credit(eng)
                ph.used.give_credit(eng)
                y_ok.give_credit(eng)

                def fetch_x(turn, n):
                    if exists(turn, n):
                        px.turned.wait(eng, turn, n - 2)
                        eng.dma_start(slot_x[n % 2][:, :], slots_dram[bass.ds((2 * turn + n) * P, P), :])\
                           .then_inc(in_x.of(n), 16)

                def fetch_weights(turn, n, buffers, table, arrived):
                    def lot(n):
                        return eng.value_load(lots[0:1, bass.ds(2 * turn + n, 1)], min_val=0,
                                              max_val=(EXPERTS - 1) * P)

                    def fetch():
                        eng.dma_start(buffers[n % 2][:, :], table[bass.ds(now, P), :]).then_inc(arrived.of(n), 16)

                    now = lot(n)
                    if isinstance(turn, int) and 2 * turn + n < 2:
                        fetch()
                        return
                    with eng.If(now != lot(n - 2)):
                        fetch()
                    with eng.Else():
                        eng.sem_inc(arrived.of(n), 16)

                def fetch12(turn, n):
                    if exists(turn, n):
                        px.used.wait(eng, turn, n - 2)
                        eng.sem_inc(gate, 1)
                        fetch_weights(turn, n, w12, w12_dram, in_12)

                def fetch3(turn, n):
                    if exists(turn, n):
                        ph.used.wait(eng, turn, n - 2)
                        eng.sem_inc(gate, 1)
                        fetch_weights(turn, n, w3, w3_dram, in_3)

                def store(turn, n):
                    if exists(turn, n):
                        y_ok.wait(eng, turn, n)
                        eng.dma_start(y_dram[bass.ds((2 * turn + n) * P, P), :], y_sb[n % 2][:, :])\
                           .then_inc(out_y.of(n), 16)

                fetch_x(0, 0)
                fetch_x(0, 1)
                fetch12(0, 0)
                fetch12(0, 1)
                fetch3(0, 0)
                fetch_x(0, 2)
                fetch_x(0, 3)

                def step(turn, n):
                    fetch_x(turn, n + 4)
                    fetch12(turn, n + 2)
                    fetch3(turn, n + 1)
                    store(turn, n - 1)

                tiles(eng, step)
                store(LOOP, AFTER)
                out_y.wait(eng, LOOP, AFTER - 1)
                out_y.wait(eng, LOOP, AFTER)

            @block.tensor
            def _(eng):
                px.silu.give_credit(eng)
                ph.silu.give_credit(eng)
                h_ok.give_credit(eng)

                def turn_x(turn, n):
                    if exists(turn, n):
                        in_x.wait(eng, turn, n)
                        px.silu.wait(eng, turn, n - 2)
                        px.dist.wait(eng, turn, n - 2)
                        eng.transpose(ps_x[n % 2][:, :], slot_x[n % 2][:, :], ident).then_inc(px.turned.sem, 1)

                def layers12(turn, n):
                    if exists(turn, n):
                        in_12.wait(eng, turn, n)
                        h_ok.wait(eng, turn, n - 2)
                        px.silu.wait(eng, turn, n)
                        px.ready.wait(eng, turn, n)
                        for c in range(FEAT):
                            lhs = px.f[n % 2][:, c, :] if c < BASES else px.s[n % 2][:, :]
                            mm = eng.matmul(ps_h[n % 2][:, :], lhs,
                                            w12[n % 2][:, c * 2 * FF1:(c + 1) * 2 * FF1],
                                            start=(c == 0), stop=(c == BASES))
                        mm.then_inc(px.used.sem, 1)

                def turn_h(turn, n):
                    h_ok.wait(eng, turn, n)
                    u_ok.wait(eng, turn, n - 1)
                    ph.silu.wait(eng, turn, n - 1)
                    for k in range(CH1):
                        mm = eng.transpose(ps_ht[:, k, :], h[:, k * P:(k + 1) * P], ident)
                    mm.then_inc(ph.turned.sem, 1)

                def layer3(turn, n):
                    if exists(turn, n):
                        in_3.wait(eng, turn, n)
                        y_ok.wait(eng, turn, n - 1)
                        ph.silu.wait(eng, turn, n)
                        ph.ready.wait(eng, turn, n)
                        for k in range(CH1):
                            for c in range(FEAT):
                                cols = slice(k * P, (k + 1) * P)
                                lhs = ph.f[n % 2][:, c, cols] if c < BASES else ph.s[n % 2][:, cols]
                                at = (k * FEAT + c) * P
                                mm = eng.matmul(ps_y[:, :], lhs, w3[n % 2][:, at:at + P],
                                                start=(k + c == 0), stop=(k == CH1 - 1 and c == BASES))
                        mm.then_inc(ph.used.sem, 1)

                turn_x(0, 0)
                turn_x(0, 1)
                layers12(0, 0)
                turn_x(0, 2)

                def step(turn, n):
                    turn_x(turn, n + 3)
                    turn_h(turn, n)
                    layer3(turn, n - 1)
                    layers12(turn, n + 1)

                tiles(eng, step)
                layer3(LOOP, AFTER)

            @block.scalar
            def _(eng):
                px.near_cube.give_credit(eng)
                px.far_cube.give_credit(eng)
                ph.near_cube.give_credit(eng)
                px.dist.give_credit(eng)
                ph.dist.give_credit(eng)
                px.ready.give_credit(eng)
                ph.ready.give_credit(eng)
                out_y.give_credit(eng)
                eng.wait_ge(offsets_ok, 1)
                eng.preload_act_table(ACT.Silu)

                def distances_x(turn, n):
                    if exists(turn, n):
                        px.turned.wait(eng, turn, n)
                        px.far_cube.wait(eng, turn, n - 2)
                        px.near_cube.wait(eng, turn, n - 2)
                        for c in range(BASES):
                            ins = eng.activation(px.t[n % 2][:, c, :], ps_x[n % 2][:, :], ACT.Abs,
                                                 bias=offsets[:, c:c + 1], scale=KNOTS_PER_UNIT)
                        ins.then_inc(px.dist.sem, 1)

                def silu_x(turn, n):
                    if exists(turn, n):
                        px.turned.wait(eng, turn, n)
                        px.used.wait(eng, turn, n - 2)
                        eng.activation(px.s[n % 2][:, :], ps_x[n % 2][:, :], ACT.Silu).then_inc(px.silu.sem, 1)

                def take_h(turn, n):
                    ph.turned.wait(eng, turn, n)
                    ph.dist.wait(eng, turn, n - 1)
                    eng.activation(h_u[:, :], ps_ht[:, :, :], ACT.Copy, scale=KNOTS_PER_UNIT).then_inc(u_ok.sem, 1)
                    ph.used.wait(eng, turn, n - 2)
                    eng.activation(ph.s[n % 2][:, :], ps_ht[:, :, :], ACT.Silu).then_inc(ph.silu.sem, 1)

                def near_square(part, turn, n):
                    if exists(turn, n):
                        part.dist.wait(eng, turn, n)
                        part.ready.wait(eng, turn, n - 1)
                        eng.activation(part.near[:, :, :], part.t[n % 2][:, :, :], ACT.Square, bias=minus2, scale=2.0)\
                           .then_inc(part.near_square.sem, 1)

                def far_square(part, turn, n):
                    if exists(turn, n):
                        eng.activation(part.far[:, :, :], part.t[n % 2][:, :, :], ACT.Square, bias=minus2, scale=1.0)\
                           .then_inc(part.far_square.sem, 1)

                def near_part(part, turn, n):
                    if exists(turn, n):
                        part.near_cube.wait(eng, turn, n)
                        eng.activation(part.near[:, :, :], part.near[:, :, :], ACT.Relu, scale=-1.0)\
                           .then_inc(part.near_part.sem, 1)

                def half(turn, n):
                    px.used.wait(eng, turn, n)
                    h_ok.wait(eng, turn, n - 1)
                    eng.activation(h1[:, :], ps_h[n % 2][:, 0:FF1], ACT.Copy).then_inc(h1_ok.sem, 1)

                def store(turn, n):
                    if exists(turn, n):
                        ph.used.wait(eng, turn, n)
                        out_y.wait(eng, turn, n - 2)
                        eng.activation(y_sb[n % 2][:, :], ps_y[:, :], ACT.Copy).then_inc(y_ok.sem, 1)

                for n in range(3):
                    distances_x(0, n)
                    near_square(px, 0, n)
                    far_square(px, 0, n)
                    if n < 2:
                        silu_x(0, n)
                        near_part(px, 0, n)

                def step(turn, n):
                    half(turn, n)
                    take_h(turn, n)
                    near_part(px, turn, n + 2)
                    distances_x(turn, n + 3)
                    near_square(ph, turn, n)
                    far_square(ph, turn, n)
                    store(turn, n - 1)
                    near_part(ph, turn, n)
                    silu_x(turn, n + 2)
                    near_square(px, turn, n + 3)
                    far_square(px, turn, n + 3)

                tiles(eng, step)
                store(LOOP, AFTER)

            @block.vector
            def _(eng):
                for part in (px, ph):
                    part.near_square.give_credit(eng)
                    part.far_square.give_credit(eng)
                    part.near_part.give_credit(eng)
                ph.far_cube.give_credit(eng)
                ph.turned.give_credit(eng)
                u_ok.give_credit(eng)
                offset_ok.give_credit(eng)
                h1_ok.give_credit(eng)
                for c in range(BASES):
                    eng.memset(offsets[:, c:c + 1], -(FIRST_CENTRE + c))
                eng.memset(minus2, -2.0).then_inc(offsets_ok, 1)

                def distances_h(turn, n):
                    u_ok.wait(eng, turn, n)
                    ph.ready.wait(eng, turn, n - 1)
                    t = ph.t[n % 2]
                    for c in range(BASES):
                        ins = eng.tensor_scalar(t[:, c, :], h_u[:, :], FIRST_CENTRE + c, None, ALU.subtract)
                    ins.then_inc(offset_ok.sem, 1)
                    offset_ok.wait(eng, turn, n)
                    bits = t[:, :, :].bitcast(U32)
                    eng.tensor_scalar(bits, bits, 0x7FFFFFFF, None, ALU.bitwise_and).then_inc(ph.dist.sem, 1)

                def near_cube(part, turn, n):
                    if exists(turn, n):
                        part.near_square.wait(eng, turn, n)
                        eng.scalar_tensor_tensor(part.near[:, :, :], part.t[n % 2][:, :, :], 1.0, part.near[:, :, :],
                                                 ALU.subtract, ALU.mult).then_inc(part.near_cube.sem, 1)

                def far_cube(part, turn, n):
                    if exists(turn, n):
                        part.far_square.wait(eng, turn, n)
                        eng.scalar_tensor_tensor(part.far[:, :, :], part.t[n % 2][:, :, :], 2.0, part.far[:, :, :],
                                                 ALU.subtract, ALU.mult).then_inc(part.far_cube.sem, 1)

                def bases(part, turn, n, back):
                    if exists(turn, n):
                        part.far_cube.wait(eng, turn, n)
                        part.near_part.wait(eng, turn, n)
                        part.used.wait(eng, turn, n - back)
                        eng.scalar_tensor_tensor(part.f[n % 2][:, :, :], part.far[:, :, :], 0.0, part.near[:, :, :],
                                                 ALU.min, ALU.add).then_inc(part.ready.sem, 1)

                def product(turn, n):
                    h1_ok.wait(eng, turn, n)
                    ph.turned.wait(eng, turn, n - 1)
                    eng.tensor_tensor(h[:, :], h1[:, :], ps_h[n % 2][:, FF1:], ALU.mult).then_inc(h_ok.sem, 1)

                for n in range(2):
                    near_cube(px, 0, n)
                    far_cube(px, 0, n)
                    bases(px, 0, n, 2)

                def step(turn, n):
                    product(turn, n)
                    near_cube(px, turn, n + 2)
                    distances_h(turn, n)
                    far_cube(px, turn, n + 2)
                    bases(px, turn, n + 2, 2)
                    near_cube(ph, turn, n)
                    far_cube(ph, turn, n)
                    bases(ph, turn, n, 1)

                tiles(eng, step)


def combine(nc, ctx, x_sb, y_dram, place, shares, out):
    with ExitStack() as own:
        y = [own.enter_context(nc.sbuf_tensor(f"y{k}", [P, TILES, P], F32)) for k in range(CHOICES)]
        fetched = [ctx.enter_context(nc.semaphore(f"fetched{g}")) for g in range(TURNS)]
        added = ctx.enter_context(nc.semaphore("y_added"))
        stored = ctx.enter_context(nc.semaphore("stored"))
        out_v = out.rearrange("(t p) c -> p t c", p=P)
        with nc.Block() as block:
            @block.gpsimd
            def _(eng):
                for t in range(TILES):
                    for k in range(CHOICES):
                        eng.indirect_dma_start(
                            out=y[k][:, t, :], out_offset=None, in_=y_dram,
                            in_offset=bass.IndirectOffsetOnAxis(ap=place[k][:, t:t + 1], axis=0))\
                           .then_inc(fetched[t // GROUP], 16)

            @block.vector
            def _(eng):
                for t in range(TILES):
                    if t % GROUP == 0:
                        eng.wait_ge(fetched[t // GROUP], 16 * CHOICES * GROUP)
                    for k in range(CHOICES):
                        if k:
                            eng.wait_ge(added, CHOICES * t + k)
                        eng.scalar_tensor_tensor(x_sb[:, t, :], y[k][:, t, :], shares[k][:, t:t + 1],
                                                 x_sb[:, t, :], ALU.mult, ALU.add).then_inc(added, 1)

            @block.sync
            def _(eng):
                for g in range(TURNS):
                    at = slice(g * GROUP, (g + 1) * GROUP)
                    eng.wait_ge(added, CHOICES * GROUP * (g + 1))
                    eng.dma_start(out_v[:, at, :], x_sb[:, at, :]).then_inc(stored, 16)
                eng.wait_ge(stored, 16 * TURNS)


def build(nc, d, out, stop=9):
    with ExitStack() as ctx:
        def sb(name, shape, dt=F32):
            return ctx.enter_context(nc.sbuf_tensor(name, shape, dt))

        def sem(name):
            return ctx.enter_context(nc.semaphore(name))

        x_sb = sb("x_sb", [P, TILES, P])
        consts = sb("consts", [P, C_END])
        ident = consts[:, C_ID:C_ID + P]
        head_cols = consts[:, C_HEAD:C_HEAD + HEADS]
        w0_sb = sb("w0_sb", [P, 4 * P])
        s_x = sem("s_x")
        s_c = sem("s_c")
        s_w0 = sem("s_w0")
        s_out = sem("s_out")

        with ExitStack() as own:
            bias0 = own.enter_context(nc.sbuf_tensor("bias0", [P, HEADS, BLK], F32))
            pads0 = own.enter_context(nc.sbuf_tensor("pads0", [P, HEADS, 2 * NEIGH], F32))
            filled = sem("filled")

            def load0(eng):
                eng.dma_start(x_sb[:, :, :], d["x"].rearrange("(t p) c -> p t c", p=P)).then_inc(s_x, 16)
                eng.dma_start(consts[:, :], d["consts"]).then_inc(s_c, 16)
                eng.dma_start(w0_sb[:, :], d["w0"]).then_inc(s_w0, 16)
                eng.dma_start(bias0[:, :, :], d["bias0"]).then_inc(s_w0, 16)
                eng.dma_start(pads0[:, :, :], d["pads0"]).then_inc(s_w0, 16)

            def arrived0(eng):
                eng.wait_ge(s_x, 16)
                eng.wait_ge(s_c, 16)
                eng.wait_ge(s_w0, 48)

            def fill0(eng, logits):
                for lg in logits:
                    eng.tensor_copy(lg[:, :, BLK:BLK + 2 * NEIGH], pads0[:, :, :]).then_inc(filled, 1)
                eng.wait_ge(filled, 2)

            attention(nc, ctx, "a0", x_sb, ident, head_cols, load0, arrived0, BLK + 2 * NEIGH,
                      lambda g, t: bias0[:, :, :], fill0,
                      {n: w0_sb[:, i * P:(i + 1) * P] for i, n in enumerate(("wq", "wk", "wv", "wo"))}, 1e-6)

        w12_dram = nc.dram_tensor("w12_dram", (EXPERTS * P, W12), F32).ap()
        w3_dram = nc.dram_tensor("w3_dram", (EXPERTS * P, W3), F32).ap()
        slots_dram = nc.dram_tensor("slots_dram", (SLOTS, P), F32).ap()
        y_dram = nc.dram_tensor("y_dram", (SLOTS, P), F32).ap()
        window_bias = sb("window_bias", [P, WINDOWS // 2, HEADS, BLK])
        place = [sb(f"place{k}", [P, TILES], U32) for k in range(CHOICES)]
        shares = [sb(f"shares{k}", [P, TILES]) for k in range(CHOICES)]
        lots = sb("lots", [P, SLOT_TILES], U32)

        with ExitStack() as own:
            work = spline_weights(nc, lambda name, shape: own.enter_context(nc.sbuf_tensor(f"sw_{name}", shape, F32)),
                                  lambda name: sem(f"sw_{name}"), d, w12_dram, w3_dram, window_bias)
            gelu_experts(nc, ctx, x_sb, consts, d, work)

        with ExitStack() as own:
            w1_sb = own.enter_context(nc.sbuf_tensor("w1_sb", [P, 4 * P + 2], F32))
            rows1 = own.enter_context(nc.sbuf_tensor("rows1", [P, 2 * P], F32))
            zero = own.enter_context(nc.sbuf_tensor("zero", [P, SLOT_TILES * P], F32))
            s_w1 = sem("s_w1")
            s_zero = sem("s_zero")
            s_cleared = sem("s_cleared")

            def load1(eng):
                eng.dma_start(w1_sb[:, :], d["w1"]).then_inc(s_w1, 16)
                eng.dma_start(rows1[:, :], d["rows1"]).then_inc(s_w1, 16)
                eng.wait_ge(s_zero, 1)
                eng.dma_start(slots_dram.rearrange("(p t) c -> p (t c)", p=P), zero[:, :]).then_inc(s_cleared, 16)
                eng.wait_ge(s_cleared, 16)

            def arrived1(eng):
                eng.wait_ge(s_w1, 32)

            def fill1(eng, logits):
                eng.memset(zero[:, :], 0.0).then_inc(s_zero, 1)

            w = {n: w1_sb[:, i * P:(i + 1) * P] for i, n in enumerate(("wq", "wk", "wv", "wo"))}
            w |= {"bq": w1_sb[:, 4 * P:4 * P + 1], "bk": w1_sb[:, 4 * P + 1:4 * P + 2],
                  "bv": rows1[:, 0:P], "bp": rows1[:, P:]}
            attention(nc, ctx, "a1", x_sb, ident, head_cols, load1, arrived1, BLK,
                      lambda g, t: window_bias[:, bass.ds((g % 2) * GROUP + t, 1), :, :], fill1, w, 1e-6)

        route(nc, ctx, x_sb, consts, d, slots_dram, place, lots, shares)
        spline_experts(nc, ctx, ident, slots_dram, y_dram, w12_dram, w3_dram, lots)
        combine(nc, ctx, x_sb, y_dram, place, shares, out)


def constants():
    c = np.zeros((P, C_END), np.float32)
    lane = np.arange(P)
    c[:, C_ID:C_ID + P] = np.eye(P)
    c[lane, C_HEAD + lane // DK] = 1.0
    c[:, C_UPPER:C_UPPER + P] = lane[:, None] < lane[None, :]
    c[:, C_ONES:C_ONES + P] = 1.0
    e = np.arange(EXPERTS)
    c[:, C_EARLIER:C_TILE] = (e[None, :] < e[:, None]).reshape(1, -1)
    c[:, C_TILE:C_LANE] = np.arange(SLOT_TILES) * P
    c[:, C_LANE] = lane
    return c


def layouts(i):
    a = {k: np.asarray(v) for k, v in i.items()}
    f = np.float32
    d = {"x": a["x"].reshape(TOKENS, P), "consts": constants()}
    wqkv = a["L0_conv_W_qkv"]
    d["w0"] = np.concatenate([wqkv, a["L0_conv_W_out"]], 1)
    keys = np.full((HEADS, BLK, BLK + 2 * NEIGH), FAR, f)
    for s in range(BLK):
        keys[:, s, s:s + 2 * NEIGH + 1] = a["L0_conv_pos_bias"][:, s, :]
    rows = keys.reshape(PAIRS, 2 * BLK, -1).transpose(1, 0, 2)
    rows = np.repeat(rows, 2, 1)
    d["bias0"] = rows[:, :, NEIGH:NEIGH + BLK]
    d["pads0"] = np.concatenate([rows[:, :, :NEIGH], rows[:, :, NEIGH + BLK:]], 2)
    w1 = np.concatenate([a["L0_ffn_rw1"], a["L0_ffn_sw1"]])
    w2 = np.concatenate([a["L0_ffn_rw2"], a["L0_ffn_sw2"]])
    b1 = np.concatenate([a["L0_ffn_rb1"], a["L0_ffn_sb1"]])
    n = len(w1)
    d["experts0"] = np.concatenate([
        w1.transpose(0, 2, 1),
        w2.reshape(n, P, CH0, P).transpose(0, 3, 2, 1).reshape(n, P, FF0),
        b1.reshape(n, CH0, P).transpose(0, 2, 1)], 2)
    d["b2"] = np.concatenate([a["L0_ffn_rb2"], a["L0_ffn_sb2"]])
    d["gate0"] = np.concatenate([a["L0_ffn_gate_w"].T, np.tile(a["L0_ffn_gate_b"], (P, 1))], 1)
    d["w1"] = np.concatenate([a["L1_conv_Wq"].T, a["L1_conv_Wk"].T, a["L1_conv_Wv"].T, a["L1_conv_Wp"].T,
                              a["L1_conv_bq"][:, None], a["L1_conv_bk"][:, None]], 1)
    d["rows1"] = np.tile(np.concatenate([a["L1_conv_bv"], a["L1_conv_bp"]]), (P, 1))
    d["pos1"] = a["L1_conv_pos_bias"].reshape(PAIRS, P, BLK).transpose(1, 0, 2)
    mask = a["L1_conv_mask"].reshape(WINDOWS, BLK, BLK).transpose(1, 0, 2)
    d["mask1"] = np.concatenate([mask, mask])
    d["gate1"] = a["L1_ffn_gate_w"].T
    def layer(n):
        base = a[f"L1_ffn_base_w{n}"].transpose(0, 2, 1)[:, :, None, :]
        spline = a[f"L1_ffn_spline_w{n}"].transpose(0, 2, 3, 1)
        return np.concatenate([spline, base], 2), a[f"L1_ffn_scaler_w{n}"].transpose(0, 2, 1)
    (f1, s1), (f2, s2), (f3, s3) = layer(1), layer(2), layer(3)
    split = lambda m: m.reshape(EXPERTS, CH1, P, -1).transpose(0, 2, 1, 3).reshape(EXPERTS, P, -1)
    d["experts1"] = np.concatenate([np.concatenate([f1, f2], 3).reshape(EXPERTS, P, W12), split(f3)], 2)
    d["scalers1"] = np.concatenate([s1, s2, split(s3)], 2)
    return {k: np.ascontiguousarray(v) for k, v in d.items()}


def kernel(**inputs):
    import concourse.bacc as bacc
    from concourse.bass_utils import run_bass_kernel_spmd as run

    nc = bacc.Bacc("TRN2", target_bir_lowering=False, num_devices=1)
    arrays = layouts(inputs)
    d = {n: nc.dram_tensor(f"in_{n}", a.shape, mybir.dt.from_np(a.dtype), kind="ExternalInput").ap()
         for n, a in arrays.items()}
    out = nc.dram_tensor("out", (TOKENS, P), F32, kind="ExternalOutput").ap()
    build(nc, d, out)
    r = run(nc, [{f"in_{n}": a for n, a in arrays.items()}], core_ids=[0])
    return r.results[0]["out"].reshape(2, 16, 64, P)
```

```python
from contextlib import ExitStack

import concourse.bass as bass
import numpy as np
from concourse import mybir

F32 = mybir.dt.float32
U32 = mybir.dt.uint32
F32R = mybir.dt.float32r
ACT = mybir.ActivationFunctionType
ALU = mybir.AluOpType
X = mybir.AxisListType.X

P = 128
TOKENS = 2048
TILES = TOKENS // P
GROUP = 4
TURNS = TILES // GROUP
HEADS = 8
DK = 16
PAIRS = HEADS // 2
BLK = 64
NEIGH = 3
FAR = -1.0e30
WINDOWS = 16
EXPERTS = 8
SHARED = 2
FF0 = 512
CH0 = FF0 // P
ROW0 = 2 * FF0 + CH0
FF1 = 256
CH1 = FF1 // P
BASES = 8
FEAT = BASES + 1
W12 = FEAT * 2 * FF1
W3 = CH1 * FEAT * P
ROW1 = W12 + W3
SCAL12 = 2 * FF1
SCAL1 = SCAL12 + CH1 * P
CHOICES = 2
SLOT_TILES = CHOICES * TOKENS // P + EXPERTS - 1
SPARE = P
PAIRED = CHOICES * TILES
KNOTS_PER_UNIT = 2.5
FIRST_CENTRE = -3.5

C_ID = 0
C_HEAD = C_ID + P
C_HALF = C_HEAD + HEADS
C_UPPER = C_HALF + 2
C_ONES = C_UPPER + P
C_EARLIER = C_ONES + P
C_TILE = C_EARLIER + EXPERTS * EXPERTS
C_LANE = C_TILE + SLOT_TILES
C_ROW = C_LANE + 1
C_TOKEN = C_ROW + P
C_SPARE = C_TOKEN + TILES
C_END = C_SPARE + 1


class Count:

    def __init__(self, sem, per_turn, credit=0):
        self.sem, self.per_turn, self.credit = sem, per_turn, credit

    def give_credit(self, eng):
        eng.sem_inc(self.sem, self.credit)

    def wait(self, eng, turn, n):
        eng.wait_ge(self.sem, turn * self.per_turn + (self.credit + n))


class TileCount:

    def __init__(self, sem, times=1, unroll=2, before=2):
        self.sem, self.times, self.unroll = sem, times, unroll
        self.credit = before * times

    def give_credit(self, eng):
        eng.sem_inc(self.sem, self.credit)

    def wait(self, eng, turn, n, part=None):
        done = self.times if part is None else part + 1
        eng.wait_ge(self.sem, turn * (self.unroll * self.times) + (n * self.times + done + self.credit))


class Chain:

    def __init__(self, eng, sem, turn=0, per_turn=0, done=0):
        self.eng, self.sem, self.turn, self.per_turn, self.done = eng, sem, turn, per_turn, done

    def after(self, ins):
        ins.then_inc(self.sem, 1)
        self.done += 1
        self.eng.wait_ge(self.sem, self.turn * self.per_turn + self.done if self.per_turn else self.done)


def layer_norm_stats(sb, sem, tag, x_sb, eps, stats=None, arrivals=None):
    taken = stats is not None
    if not taken:
        stats = sb(f"{tag}_stats", [P, TILES, 6])
    moments = sb(f"{tag}_moments", [P, TILES, 2])
    dev = sb(f"{tag}_dev", [P, TILES])
    rstd = sb(f"{tag}_rstd", [P, TILES])
    s_stats, s_mom, s_dev, s_rstd = (sem(f"{tag}_{n}") for n in ("s_stats", "s_mom", "s_dev", "s_rstd"))

    def vector(eng):
        if not taken:
            for t in range(TILES):
                if arrivals is not None and t % GROUP == 0:
                    eng.wait_ge(arrivals[t // GROUP], 16)
                eng.bn_stats(stats[:, t, :], x_sb[:, t, :]).then_inc(s_stats, 1)
        for t in range(TILES):
            if not taken:
                eng.wait_ge(s_stats, t + 1)
            eng.bn_aggr(moments[:, t, :], stats[:, t, :]).then_inc(s_mom, 1)
        eng.wait_ge(s_mom, TILES)
        eng.tensor_scalar(dev[:, :], moments[:, :, 1], eps, None, ALU.add).then_inc(s_mom, 1)
        eng.wait_ge(s_dev, 1)
        eng.reciprocal(rstd[:, :], dev[:, :]).then_inc(s_rstd, 1)
        eng.wait_ge(s_rstd, 1)

    def scalar(eng):
        eng.preload_act_table(ACT.Sqrt)
        eng.wait_ge(s_mom, TILES + 1)
        eng.activation(dev[:, :], dev[:, :], ACT.Sqrt).then_inc(s_dev, 1)

    return moments, rstd, vector, scalar


def attention(nc, sem, tag, x_sb, consts, load, arrived, keys, bias_of, fill, w, eps, next_stats,
              x_stats=None, x_arrivals=None):
    LAG = GROUP
    V_BUFFERS = LAG
    ident = consts[:, C_ID:C_ID + P]
    head_scales = consts[:, C_HEAD:C_HEAD + HEADS]
    half_of = [consts[:, C_HALF + i:C_HALF + i + 1] for i in range(2)]
    bq, bk, bv, bp = w.get("bq"), w.get("bk"), w.get("bv"), w.get("bp")
    with ExitStack() as own:
        def sb(name, shape, dt=F32):
            return own.enter_context(nc.sbuf_tensor(f"{tag}_{name}", shape, dt))

        def two(name, shape):
            return [sb(f"{name}{i}", shape) for i in range(2)]

        def ps(name, shape):
            return own.enter_context(nc.psum_tensor(f"{tag}_{name}", shape, F32))

        moments, rstd, stats_vector, stats_scalar = layer_norm_stats(sb, sem, "ln", x_sb, eps, x_stats, x_arrivals)
        xn = two("xn", [P, P])
        xnT = two("xnT", [P, P])
        qT = two("qT", [P, P])
        kT = two("kT", [P, P])
        v = [sb(f"v{i}", [P, P]) for i in range(V_BUFFERS)]
        q_heads = two("q_heads", [P, 2, HEADS, BLK])
        logits = two("logits", [P, HEADS, keys])
        probs = two("probs", [P, HEADS, keys])
        weights = two("weights", [P, HEADS, BLK])
        probsT = two("probsT", [P, PAIRS, P])
        top = two("top", [P, HEADS])
        total = two("total", [P, HEADS])
        zT = two("zT", [P, P])

        ps_x = ps("ps_x", [P, P])
        ps_out = ps("ps_out", [P, 1, P])
        ps_qkv = ps("ps_qkv", [P, 3, P])
        ps_S = [ps(f"ps_S{i}", [P, HEADS, BLK]) for i in range(2)]
        ps_P = ps("ps_P", [P, PAIRS, P])
        ps_Z = [ps(f"ps_Z{b}", [P, P]) for b in range(2)]

        def tile_count(name):
            return TileCount(sem(name), unroll=LAG, before=LAG)

        normed = tile_count("normed")
        turned = tile_count("turned")
        xnT_ok = tile_count("xnT_ok")
        proj = tile_count("proj")
        q_ok = tile_count("q_ok")
        k_ok = tile_count("k_ok")
        v_copied = tile_count("v_copied")
        v_ok = tile_count("v_ok") if bv is not None else v_copied
        heads_ok = tile_count("heads_ok")
        scored = tile_count("scored")
        biased = tile_count("biased")
        topped = tile_count("topped")
        shifted = tile_count("shifted")
        exped = tile_count("exped")
        summed = tile_count("summed")
        inv = tile_count("inv")
        norm_p = tile_count("norm_p")
        probs_turned = tile_count("probs_turned")
        probsT_ok = tile_count("probsT_ok")
        mixed = tile_count("mixed")
        z_half = tile_count("z_half")
        z_ok = tile_count("z_ok")
        out_done = tile_count("out_done")
        based = tile_count("based")
        added = tile_count("added")
        measured = TileCount(sem("measured"), unroll=LAG, before=0)
        gate = sem("gate")

        assert TILES % LAG == 0

        def steps(eng, step):
            for n in range(LAG):
                step(0, n)
            with eng.Fori(0, TILES // LAG - 1) as i:
                for n in range(LAG, 2 * LAG):
                    step(i, n)
            for n in range(LAG, 2 * LAG):
                step(TILES // LAG - 1, n)

        def stage(work):
            def run(turn, n):
                if not isinstance(turn, int) or 0 <= LAG * turn + n < TILES:
                    work(turn, n)
            return run

        def tile(turn, n):
            return bass.ds(LAG * turn + n, 1)

        with nc.Block() as block:
            @block.sync
            def _(eng):
                load(eng)

            @block.tensor
            def _(eng):
                for c in (xnT_ok, q_ok, k_ok, v_copied, biased, probsT_ok, z_ok, added):
                    c.give_credit(eng)
                arrived(eng)

                @stage
                def turn_x(turn, n):
                    normed.wait(eng, turn, n)
                    xnT_ok.wait(eng, turn, n - 1)
                    eng.transpose(ps_x[:, :], xn[n % 2][:, :], ident).then_inc(turned.sem, 1)

                @stage
                def project(turn, n):
                    xnT_ok.wait(eng, turn, n)
                    for c in (q_ok, k_ok, v_copied):
                        c.wait(eng, turn, n - 1)
                    x, to = xnT[n % 2][:, :], ps_qkv
                    eng.matmul(to[:, 0, :], w["wq"], x, start=True, stop=True)
                    eng.matmul(to[:, 1, :], w["wk"], x, start=True, stop=True)
                    eng.matmul(to[:, 2, :], x, w["wv"], start=True, stop=True).then_inc(proj.sem, 1)

                @stage
                def score(turn, n):
                    heads_ok.wait(eng, turn, n)
                    k_ok.wait(eng, turn, n)
                    biased.wait(eng, turn, n - 2)
                    for hp in range(PAIRS):
                        for b in range(2):
                            mm = eng.matmul(ps_S[n % 2][:, 2 * hp + b, :],
                                            q_heads[n % 2][:, b, 2 * hp:2 * hp + 2, :],
                                            kT[n % 2][:, b * BLK:(b + 1) * BLK], start=True, stop=True)
                    mm.then_inc(scored.sem, 1)

                @stage
                def turn_probs(turn, n):
                    norm_p.wait(eng, turn, n)
                    probsT_ok.wait(eng, turn, n - 1)
                    for hp in range(PAIRS):
                        mm = eng.transpose(ps_P[:, hp, :], weights[n % 2][:, 2 * hp:2 * hp + 2, :], ident)
                    mm.then_inc(probs_turned.sem, 1)

                @stage
                def mix(turn, n):
                    probsT_ok.wait(eng, turn, n)
                    v_ok.wait(eng, turn, n)
                    z_ok.wait(eng, turn, n - 1)
                    eng.sem_inc(gate, 1)
                    for hp in range(PAIRS):
                        cols = slice(2 * DK * hp, 2 * DK * (hp + 1))
                        for b in range(2):
                            rows = slice(b * BLK, (b + 1) * BLK)
                            mm = eng.matmul(ps_Z[b][cols, :], v[n % V_BUFFERS][rows, cols],
                                            probsT[n % 2][rows, hp, :], start=True, stop=True)
                    mm.then_inc(mixed.sem, 1)

                @stage
                def project_out(turn, n):
                    z_ok.wait(eng, turn, n)
                    added.wait(eng, turn, n - 1)
                    eng.matmul(ps_out[:, 0, :], zT[n % 2][:, :], w["wo"], start=True, stop=True)\
                       .then_inc(out_done.sem, 1)

                def step(turn, n):
                    project(turn, n - 1)
                    mix(turn, n - 4)
                    score(turn, n - 2)
                    turn_x(turn, n)
                    project_out(turn, n - 4)
                    turn_probs(turn, n - 3)

                steps(eng, step)

            @block.scalar
            def _(eng):
                for c in (turned, proj, heads_ok, scored, mixed, probs_turned, shifted):
                    c.give_credit(eng)
                stats_scalar(eng)
                arrived(eng)
                eng.preload_act_table(ACT.Exp)

                @stage
                def copy_x(turn, n):
                    turned.wait(eng, turn, n)
                    proj.wait(eng, turn, n - 2)
                    eng.activation(xnT[n % 2][:, :], ps_x[:, :], ACT.Copy).then_inc(xnT_ok.sem, 1)

                @stage
                def copy_qkv(turn, n):
                    proj.wait(eng, turn, n)
                    heads_ok.wait(eng, turn, n - 2)
                    if bq is not None:
                        eng.activation(qT[n % 2][:, :], ps_qkv[:, 0, :], ACT.Identity, bias=bq)\
                           .then_inc(q_ok.sem, 1)
                    else:
                        eng.activation(qT[n % 2][:, :], ps_qkv[:, 0, :], ACT.Copy).then_inc(q_ok.sem, 1)
                    scored.wait(eng, turn, n - 2)
                    if bk is not None:
                        eng.activation(kT[n % 2][:, :], ps_qkv[:, 1, :], ACT.Identity, bias=bk)\
                           .then_inc(k_ok.sem, 1)
                    else:
                        eng.activation(kT[n % 2][:, :], ps_qkv[:, 1, :], ACT.Copy).then_inc(k_ok.sem, 1)
                    mixed.wait(eng, turn, n - V_BUFFERS)
                    eng.activation(v[n % V_BUFFERS][:, :], ps_qkv[:, 2, :], ACT.Copy).then_inc(v_copied.sem, 1)

                @stage
                def exponentials(turn, n):
                    shifted.wait(eng, turn, n)
                    eng.activation(probs[n % 2][:, :, :], probs[n % 2][:, :, :], ACT.Exp).then_inc(exped.sem, 1)

                @stage
                def copy_probs(turn, n):
                    probs_turned.wait(eng, turn, n)
                    mixed.wait(eng, turn, n - 2)
                    eng.activation(probsT[n % 2][:, :, :], ps_P[:, :, :], ACT.Copy).then_inc(probsT_ok.sem, 1)

                def step(turn, n):
                    copy_qkv(turn, n - 1)
                    copy_x(turn, n)
                    copy_probs(turn, n - 3)
                    exponentials(turn, n - 2)

                steps(eng, step)

            @block.gpsimd
            def _(eng):
                if bv is not None:
                    v_ok.give_credit(eng)
                arrived(eng)

                @stage
                def spread_heads(turn, n):
                    q_ok.wait(eng, turn, n)
                    scored.wait(eng, turn, n - 2)
                    shape = [P, 2, HEADS, BLK]
                    eng.tensor_tensor(q_heads[n % 2][:, :, :, :],
                                      qT[n % 2][:, :].rearrange("p (b i) -> p b i", b=2).unsqueeze(2).to_broadcast(shape),
                                      head_scales.unsqueeze(1).unsqueeze(3).to_broadcast(shape), ALU.mult)\
                       .then_inc(heads_ok.sem, 1)

                @stage
                def normalise(turn, n):
                    inv.wait(eng, turn, n)
                    probs_turned.wait(eng, turn, n - 2)
                    eng.tensor_tensor(weights[n % 2][:, :, :], probs[n % 2][:, :, 0:BLK],
                                      total[n % 2][:, :].unsqueeze(2).to_broadcast([P, HEADS, BLK]), ALU.mult)\
                       .then_inc(norm_p.sem, 1)

                @stage
                def add_bv(turn, n):
                    v_copied.wait(eng, turn, n)
                    eng.tensor_tensor(v[n % V_BUFFERS][:, :], v[n % V_BUFFERS][:, :], bv, ALU.add).then_inc(v_ok.sem, 1)

                @stage
                def add_bp(turn, n):
                    normed.wait(eng, turn, n)
                    eng.sem_inc(gate, 1)
                    eng.tensor_tensor(x_sb[:, tile(turn, n), :], x_sb[:, tile(turn, n), :], bp.unsqueeze(1), ALU.add)\
                       .then_inc(based.sem, 1)

                def step(turn, n):
                    normalise(turn, n - 3)
                    spread_heads(turn, n - 1)
                    if bv is not None:
                        add_bv(turn, n - 1)
                    if bp is not None:
                        add_bp(turn, n)

                steps(eng, step)

            @block.vector
            def _(eng):
                for c in (normed, topped, summed, exped, inv, norm_p, out_done, z_half, based):
                    c.give_credit(eng)
                stats_vector(eng)
                arrived(eng)
                fill(eng, logits)

                @stage
                def norm(turn, n):
                    turned.wait(eng, turn, n - 2)
                    at = tile(turn, n)
                    eng.tensor_scalar(xn[n % 2][:, :], x_sb[:, at, :], moments[:, at, 0], rstd[:, at],
                                      ALU.subtract, ALU.mult).then_inc(normed.sem, 1)

                @stage
                def add_bias(turn, n):
                    scored.wait(eng, turn, n)
                    shifted.wait(eng, turn, n - 2)
                    eng.tensor_tensor(logits[n % 2][:, :, 0:BLK], ps_S[n % 2][:, :, :], bias_of(turn, n), ALU.add)\
                       .then_inc(biased.sem, 1)

                @stage
                def shift(turn, n):
                    biased.wait(eng, turn, n)
                    eng.tensor_reduce(top[n % 2][:, :], logits[n % 2][:, :, :], X, ALU.max).then_inc(topped.sem, 1)
                    topped.wait(eng, turn, n)
                    norm_p.wait(eng, turn, n - 2)
                    eng.tensor_tensor(probs[n % 2][:, :, :], logits[n % 2][:, :, :],
                                      top[n % 2][:, :].unsqueeze(2).to_broadcast([P, HEADS, keys]), ALU.subtract)\
                       .then_inc(shifted.sem, 1)

                @stage
                def row_sums(turn, n):
                    exped.wait(eng, turn, n)
                    eng.tensor_reduce(total[n % 2][:, :], probs[n % 2][:, :, :], X, ALU.add).then_inc(summed.sem, 1)

                @stage
                def invert_sums(turn, n):
                    summed.wait(eng, turn, n)
                    eng.reciprocal(total[n % 2][:, :], total[n % 2][:, :]).then_inc(inv.sem, 1)

                def z_block(n, b):
                    return zT[n % 2][:, b * BLK:(b + 1) * BLK]

                @stage
                def first_heads(turn, n):
                    mixed.wait(eng, turn, n)
                    out_done.wait(eng, turn, n - 2)
                    for b in range(2):
                        ins = eng.tensor_scalar(z_block(n, b), ps_Z[b][:, 0:BLK], half_of[0], None, ALU.mult)
                    ins.then_inc(z_half.sem, 1)

                @stage
                def second_heads(turn, n):
                    z_half.wait(eng, turn, n)
                    for b in range(2):
                        ins = eng.scalar_tensor_tensor(z_block(n, b), ps_Z[b][:, BLK:], half_of[1], z_block(n, b),
                                                       ALU.mult, ALU.add)
                    ins.then_inc(z_ok.sem, 1)

                @stage
                def add_out(turn, n):
                    out_done.wait(eng, turn, n)
                    if bp is not None:
                        based.wait(eng, turn, n)
                    at = tile(turn, n)
                    eng.tensor_tensor(x_sb[:, at, :], x_sb[:, at, :], ps_out[:, :, :], ALU.add)\
                       .then_inc(added.sem, 1)

                @stage
                def measure(turn, n):
                    added.wait(eng, turn, n)
                    eng.sem_inc(gate, 1)
                    at = tile(turn, n)
                    eng.bn_stats(next_stats[:, at, :], x_sb[:, at, :]).then_inc(measured.sem, 1)

                def step(turn, n):
                    norm(turn, n)
                    row_sums(turn, n - 3)
                    first_heads(turn, n - 4)
                    invert_sums(turn, n - 3)
                    second_heads(turn, n - 4)
                    add_bias(turn, n - 2)
                    add_out(turn, n - 4)
                    shift(turn, n - 2)
                    measure(turn, n - 4)

                steps(eng, step)
                measured.wait(eng, TILES // LAG - 1, LAG - 1)


def rank_experts(eng, chain, sb, scores, earlier, tag):
    shape = [P, TILES, EXPERTS, EXPERTS]
    above = sb(f"{tag}_above", shape)
    level = sb(f"{tag}_level", shape)
    rank = sb(f"{tag}_rank", [P, TILES, EXPERTS])
    other = scores.unsqueeze(2).to_broadcast(shape)
    own = scores.unsqueeze(3).to_broadcast(shape)
    first = earlier.rearrange("p (a b) -> p a b", b=EXPERTS).unsqueeze(1).to_broadcast(shape)
    eng.tensor_tensor(above[:, :, :, :], other, own, ALU.is_gt)
    chain.after(eng.tensor_tensor(level[:, :, :, :], other, own, ALU.is_equal))
    chain.after(eng.tensor_tensor(level[:, :, :, :], level[:, :, :, :], first, ALU.mult))
    chain.after(eng.tensor_tensor(above[:, :, :, :], above[:, :, :, :], level[:, :, :, :], ALU.add))
    chain.after(eng.tensor_reduce(rank[:, :, :], above[:, :, :, :], X, ALU.add))
    return rank


def gelu_experts(nc, ctx, x_sb, consts, d, pool_work, to_clear, stats):
    ident = consts[:, C_ID:C_ID + P]
    with ExitStack() as own:
        def sb(name, shape, dt=F32):
            return own.enter_context(nc.sbuf_tensor(f"f0_{name}", shape, dt))

        def ps(name, shape):
            return own.enter_context(nc.psum_tensor(f"f0_{name}", shape, F32))

        def sem(name):
            return ctx.enter_context(nc.semaphore(f"f0_{name}"))

        ALL = EXPERTS + SHARED
        moments, rstd, stats_vector, stats_scalar = layer_norm_stats(sb, sem, "ln", x_sb, 1e-5, stats)
        xn = sb("xn", [P, TILES, P])
        nT = sb("nT", [P, TILES, P])
        gate = sb("gate", [P, 2 * EXPERTS])
        b2 = sb("b2", [ALL, P])
        probs = sb("probs", [P, TILES, EXPERTS])
        top = sb("top", [P, TILES])
        mix = sb("mix", [P, TILES, ALL])
        mixT = sb("mixT", [ALL, TILES, P])
        wt = [sb(f"wt{i}", [P, ROW0]) for i in range(2)]
        mix_now = [sb(f"mix_now{i}", [P, TILES]) for i in range(2)]
        hid = [sb(f"hid{i}", [P, CH0, GROUP * P]) for i in range(2)]
        n_parts = [sb(f"n_part{j}", [P, TILES, P], F32R) for j in range(2)]
        w_parts = [[sb(f"w_part{j}_{i}", [P, FF0], F32R) for j in range(2)] for i in range(2)]
        ps_up = [ps(f"ps_up{i}", [P, GROUP * P]) for i in range(4)]
        ps_dn = [ps(f"ps_dn{i}", [P, GROUP, P]) for i in range(2)]
        ps_free = [ps(f"ps_free{i}", [P, GROUP, P]) for i in range(2)]
        ps_t = ps_free[0]
        ps_g = ps_free[1][:, :, :].rearrange("p a b -> p (a b)")[:, 0:TILES * EXPERTS]\
            .rearrange("p (t e) -> p t e", e=EXPERTS)

        HALF = ALL // 2
        STEPS = 2 * TURNS
        PARTS = ((0, 0), (0, 1), (1, 0))
        LATE = STEPS - TURNS
        s_small = sem("s_small")
        s_w = [Count(sem(f"s_w{i}"), 16) for i in range(2)]
        normed = sem("normed")
        turned = sem("turned")
        turned_out = sem("turned_out")
        gated = sem("gated")
        s_exp = sem("s_exp")
        s_shift = sem("s_shift")
        mixed = sem("mixed")
        mixT_mm = sem("mixT_mm")
        mixT_out = sem("mixT_out")
        b2_mm = sem("b2_mm")
        b2_added = sem("b2_added")
        up = Count(sem("up"), STEPS * CH0)
        acted = Count(sem("acted"), STEPS * CH0, credit=4)
        n_split = sem("n_split")
        measured = sem("measured")
        w_high = Count(sem("w_high"), 2)
        w_split = Count(sem("w_split"), 2)
        down = Count(sem("down"), STEPS, credit=TURNS + 1)
        added = Count(sem("added"), STEPS * GROUP, credit=2 * GROUP)
        cols = Count(sem("cols"), 2)
        s_chain = sem("chain")

        def first(i):
            return isinstance(i, int) and i == 0

        with nc.Block() as block:
            @block.sync
            def _(eng):
                eng.dma_start(gate[:, :], d["gate0"]).then_inc(s_small, 16)
                eng.dma_start(b2[:, :], d["b2"]).then_inc(s_small, 16)
                for s in to_clear:
                    eng.sem_clear(s)
                with eng.Fori(0, HALF) as i:
                    for a in range(2):
                        down.wait(eng, i, (a - 1) * TURNS)
                        eng.dma_start(wt[a][:, :], d["experts0"][bass.ds(2 * i + a, 1), :, :])\
                           .then_inc(s_w[a].sem, 16)

            @block.tensor
            def _(eng):
                acted.give_credit(eng)
                added.give_credit(eng)
                eng.wait_ge(s_small, 32)
                for g in range(TURNS + 1):
                    if g >= 1:
                        eng.wait_ge(turned_out, g)
                    if g < TURNS:
                        for t in range(GROUP):
                            eng.wait_ge(normed, g * GROUP + t + 1)
                            mm = eng.transpose(ps_t[:, t, :], xn[:, g * GROUP + t, :], ident)
                        mm.then_inc(turned, 1)
                    if g >= 1:
                        for t in range((g - 1) * GROUP, g * GROUP):
                            mm = eng.matmul(ps_g[:, t, :], nT[:, t, :], gate[:, 0:EXPERTS], start=True, stop=True)
                mm.then_inc(gated, 1)
                def turn_mix(g):
                    eng.wait_ge(mixed, 1)
                    if g >= 1:
                        eng.wait_ge(mixT_out, g)
                    for t in range(GROUP):
                        mm = eng.transpose(ps_t[0:ALL, t, :], mix[:, g * GROUP + t, :], ident)
                    mm.then_inc(mixT_mm, 1)

                def output_biases(g):
                    eng.wait_ge(mixT_out, TURNS)
                    if g >= 2:
                        eng.wait_ge(b2_added, g - 1)
                    for t in range(GROUP):
                        mm = eng.matmul(ps_free[g % 2][:, t, :], mixT[:, g * GROUP + t, :], b2[:, :],
                                        start=True, stop=True)
                    mm.then_inc(b2_mm, 1)

                def go_up(i, s):
                    a, g = divmod(s, TURNS)
                    if g == 0:
                        w_split.wait(eng, i, a + 1)
                    for c in range(CH0):
                        acted.wait(eng, i, s * CH0 + c + 1 - 4)
                        for j, (wj, nj) in enumerate(PARTS):
                            mm = eng.matmul(ps_up[c][:, :], w_parts[a][wj][:, c * P:(c + 1) * P],
                                            n_parts[nj][:, g * GROUP:(g + 1) * GROUP, :],
                                            start=(j == 0), stop=(j == len(PARTS) - 1))
                        mm.then_inc(up.sem, 1)

                def go_down(i, s):
                    a, g = divmod(s, TURNS)
                    acted.wait(eng, i, (s + 1) * CH0)
                    added.wait(eng, i, (s - 1) * GROUP)
                    for t in range(GROUP):
                        for c in range(CH0):
                            mm = eng.matmul(ps_dn[s % 2][:, t, :], hid[s % 2][:, c, t * P:(t + 1) * P],
                                            wt[a][:, FF0 + c * P:FF0 + (c + 1) * P],
                                            start=(c == 0), stop=(c == CH0 - 1))
                    mm.then_inc(down.sem, 1)

                def pair_of_experts(i):
                    for s in range(STEPS + 1):
                        if s < STEPS:
                            go_up(i, s)
                        if s >= 1:
                            go_down(i, s - 1)
                        if first(i) and LATE <= s < LATE + TURNS:
                            turn_mix(s - LATE)

                eng.wait_ge(n_split, TURNS)
                pair_of_experts(0)
                for g in range(TURNS):
                    output_biases(g)
                with eng.Fori(1, HALF - 1) as i:
                    pair_of_experts(i)
                pair_of_experts(HALF - 1)

            @block.scalar
            def _(eng):
                down.give_credit(eng)
                stats_scalar(eng)
                for g in range(TURNS):
                    eng.wait_ge(turned, g + 1)
                    eng.activation(nT[:, g * GROUP:(g + 1) * GROUP, :], ps_t[:, :, :], ACT.Copy)\
                       .then_inc(turned_out, 1)
                eng.wait_ge(s_shift, 1)
                eng.activation(probs[:, :, :], probs[:, :, :], ACT.Exp).then_inc(s_exp, 1)
                eng.preload_act_table(ACT.Gelu)

                def pair_of_experts(i):
                    for s in range(STEPS):
                        a = s // TURNS
                        down.wait(eng, i, s - 1)
                        for c in range(CH0):
                            up.wait(eng, i, s * CH0 + c + 1)
                            eng.activation(hid[s % 2][:, c, :], ps_up[c][:, :], ACT.Gelu,
                                           bias=wt[a][:, 2 * FF0 + c:2 * FF0 + c + 1]).then_inc(acted.sem, 1)
                        if first(i) and s >= LATE:
                            g = s - LATE
                            eng.wait_ge(mixT_mm, g + 1)
                            eng.activation(mixT[:, g * GROUP:(g + 1) * GROUP, :], ps_t[0:ALL, :, :], ACT.Copy)\
                               .then_inc(mixT_out, 1)

                pair_of_experts(0)
                with eng.Fori(1, HALF - 1) as i:
                    pair_of_experts(i)
                pair_of_experts(HALF - 1)

            @block.gpsimd
            def _(eng):
                pool_work(eng)

            @block.vector
            def _(eng):
                stats_vector(eng)
                for t in range(TILES):
                    eng.tensor_scalar(xn[:, t, :], x_sb[:, t, :], moments[:, t, 0:1], rstd[:, t:t + 1],
                                      ALU.subtract, ALU.mult).then_inc(normed, 1)
                chain = Chain(eng, s_chain)

                def split_weights(i, a):
                    s_w[a].wait(eng, i, 16)
                    eng.tensor_copy(w_parts[a][0][:, :], wt[a][:, 0:FF0]).then_inc(w_high.sem, 1)
                    w_high.wait(eng, i, a + 1)
                    eng.tensor_tensor(w_parts[a][1][:, :], wt[a][:, 0:FF0], w_parts[a][0][:, :].bitcast(F32),
                                      ALU.subtract).then_inc(w_split.sem, 1)

                for g in range(TURNS):
                    at = slice(g * GROUP, (g + 1) * GROUP)
                    eng.wait_ge(turned_out, g + 1)
                    chain.after(eng.tensor_copy(n_parts[0][:, at, :], nT[:, at, :]))
                    eng.tensor_tensor(n_parts[1][:, at, :], nT[:, at, :], n_parts[0][:, at, :].bitcast(F32),
                                      ALU.subtract).then_inc(n_split, 1)
                split_weights(0, 0)
                eng.wait_ge(s_small, 32)
                eng.wait_ge(gated, 1)
                wide = [P, TILES, EXPERTS]
                chain.after(eng.tensor_tensor(probs[:, :, :], ps_g[:, :, :],
                                              gate[:, EXPERTS:].unsqueeze(1).to_broadcast(wide), ALU.add))
                chain.after(eng.tensor_reduce(top[:, :], probs[:, :, :], X, ALU.max))
                eng.tensor_tensor(probs[:, :, :], probs[:, :, :], top[:, :].unsqueeze(2).to_broadcast(wide),
                                  ALU.subtract).then_inc(s_shift, 1)
                eng.wait_ge(s_exp, 1)
                chain.after(eng.tensor_reduce(top[:, :], probs[:, :, :], X, ALU.add))
                chain.after(eng.reciprocal(top[:, :], top[:, :]))
                chain.after(eng.tensor_tensor(probs[:, :, :], probs[:, :, :],
                                              top[:, :].unsqueeze(2).to_broadcast(wide), ALU.mult))
                rank = rank_experts(eng, chain, sb, probs[:, :, :], consts[:, C_EARLIER:C_TILE], "route")
                chain.after(eng.tensor_scalar(rank[:, :, :], rank[:, :, :], float(CHOICES), None, ALU.is_lt))
                eng.memset(mix[:, :, 0:SHARED], 1.0)
                eng.tensor_tensor(mix[:, :, SHARED:], rank[:, :, :], probs[:, :, :], ALU.mult)\
                   .then_inc(mixed, 1)
                eng.wait_ge(mixed, 1)

                def add(i, s):
                    a, g = divmod(s, TURNS)
                    if g == 0:
                        eng.tensor_copy(mix_now[a][:, :], mix[:, :, bass.ds(2 * i + a, 1)]).then_inc(cols.sem, 1)
                        cols.wait(eng, i, a + 1)
                        added.wait(eng, i, s * GROUP)
                    down.wait(eng, i, s + 1)
                    for t in range(GROUP):
                        xt = x_sb[:, g * GROUP + t, :]
                        eng.scalar_tensor_tensor(xt, ps_dn[s % 2][:, t, :],
                                                 mix_now[a][:, g * GROUP + t:g * GROUP + t + 1], xt,
                                                 ALU.mult, ALU.add).then_inc(added.sem, 1)

                def measure(s):
                    added.wait(eng, HALF - 1, (s + 1) * GROUP)
                    for t in range((s - TURNS) * GROUP, (s - TURNS + 1) * GROUP):
                        eng.bn_stats(stats[:, t, :], x_sb[:, t, :]).then_inc(measured, 1)

                def pair_of_experts(i):
                    last = isinstance(i, int) and i == HALF - 1
                    for s in range(STEPS):
                        add(i, s)
                        if last and s >= TURNS:
                            measure(s)
                        if s == 1:
                            split_weights(i, 1)
                        if s == TURNS + 1 and not last:
                            split_weights(i + 1, 0)

                pair_of_experts(0)
                added.wait(eng, 1, 0)
                for g in range(TURNS):
                    eng.wait_ge(b2_mm, g + 1)
                    at = slice(g * GROUP, (g + 1) * GROUP)
                    eng.tensor_tensor(x_sb[:, at, :], x_sb[:, at, :], ps_free[g % 2][:, :, :], ALU.add)\
                       .then_inc(b2_added, 1)
                eng.wait_ge(b2_added, TURNS)
                with eng.Fori(1, HALF - 1) as i:
                    pair_of_experts(i)
                pair_of_experts(HALF - 1)
                eng.wait_ge(measured, TILES)


def spline_weights(nc, sb, sem, d, w12_dram, w3_dram, window_bias):
    raw = [sb(f"raw{i}", [P, ROW1]) for i in range(2)]
    scal = [sb(f"scal{i}", [P, SCAL1]) for i in range(2)]
    pos1 = sb("pos1", [P, PAIRS, BLK])
    mask1 = sb("mask1", [P, WINDOWS, BLK])
    loaded = [Count(sem(f"loaded{i}"), 32) for i in range(2)]
    stored = [Count(sem(f"stored{i}"), 32) for i in range(2)]
    scaled = Count(sem("scaled"), 2)
    prepared = Count(sem("prepared"), 4)
    s_tab = sem("s_tab")
    gate = sem("gate")
    s_added = sem("s_added")

    def work(eng):
        eng.dma_start(pos1[:, :, :], d["pos1"]).then_inc(s_tab, 16)
        eng.dma_start(mask1[:, :, :], d["mask1"]).then_inc(s_tab, 16)
        eng.wait_ge(s_tab, 32)
        shape = [P, PAIRS, 2, BLK]
        for n in range(WINDOWS // 2):
            eng.tensor_tensor(window_bias[:, n, :, :].rearrange("p (h b) k -> p h b k", b=2),
                              pos1[:, :, :].unsqueeze(2).to_broadcast(shape),
                              mask1[:, 2 * n:2 * n + 2, :].unsqueeze(1).to_broadcast(shape), ALU.add)\
               .then_inc(s_added, 1)
        with eng.Fori(0, EXPERTS // 2) as i:
            for a in range(2):
                at = bass.ds(2 * i + a, 1)
                eng.dma_start(raw[a][:, :], d["experts1"][at, :, :]).then_inc(loaded[a].sem, 16)
                eng.dma_start(scal[a][:, :], d["scalers1"][at, :, :]).then_inc(loaded[a].sem, 16)
            for a in range(2):
                loaded[a].wait(eng, i, 32)
                eng.sem_inc(gate, 1)
                eng.tensor_scalar(scal[a][:, :], scal[a][:, :], -1.0 / 6.0, None, ALU.mult)\
                   .then_inc(scaled.sem, 1)
                scaled.wait(eng, i, a + 1)
                first = raw[a][:, 0:BASES * 2 * FF1].rearrange("p (c o) -> p c o", c=BASES)
                eng.tensor_tensor(first, first, scal[a][:, 0:SCAL12].unsqueeze(1)
                                  .to_broadcast([P, BASES, 2 * FF1]), ALU.mult).then_inc(prepared.sem, 1)
                last = raw[a][:, W12:].rearrange("p (k c o) -> p k c o", k=CH1, c=FEAT)[:, :, 0:BASES, :]
                eng.tensor_tensor(last, last, scal[a][:, SCAL12:].rearrange("p (k o) -> p k o", k=CH1)
                                  .unsqueeze(2).to_broadcast([P, CH1, BASES, P]), ALU.mult)\
                   .then_inc(prepared.sem, 1)
                prepared.wait(eng, i, 2 * a + 2)
                rows = bass.ds((2 * i + a) * P, P)
                eng.dma_start(w12_dram[rows, :], raw[a][:, 0:W12]).then_inc(stored[a].sem, 16)
                eng.dma_start(w3_dram[rows, :], raw[a][:, W12:]).then_inc(stored[a].sem, 16)
            for a in range(2):
                stored[a].wait(eng, i, 32)
        eng.wait_ge(s_added, WINDOWS // 2)
    return work


def route(nc, ctx, x_sb, consts, d, normed_dram, out, slots, lots, stats):
    ident = consts[:, C_ID:C_ID + P]
    with ExitStack() as own:
        def sb(name, shape, dt=F32):
            return own.enter_context(nc.sbuf_tensor(f"rt_{name}", shape, dt))

        def ps(name, shape):
            return own.enter_context(nc.psum_tensor(f"rt_{name}", shape, F32))

        def sem(name):
            return ctx.enter_context(nc.semaphore(f"rt_{name}"))

        moments, rstd, stats_vector, stats_scalar = layer_norm_stats(sb, sem, "ln", x_sb, 1e-5, stats)
        wide = [P, TILES, EXPERTS]
        xn = sb("xn", [P, TILES, P])
        nT = sb("nT", [P, TILES, P])
        gate = sb("gate", [P, EXPERTS])
        scores = sb("scores", wide)
        chosen = sb("chosen", wide)
        choice = [sb(f"choice{k}", wide) for k in range(CHOICES)]
        picked = sb("picked", wide)
        value = [sb(f"value{k}", [P, TILES]) for k in range(CHOICES)]
        base = sb("base", wide)
        total = sb("total", wide)
        upto = [sb(f"upto{i}", wide) for i in range(2)]
        many = sb("many", [P, EXPERTS, TILES])
        tiles_of = sb("tiles_of", [P, EXPERTS])
        before = sb("before", [P, EXPERTS, EXPERTS])
        start = sb("start", [P, EXPERTS])
        begun = sb("begun", [P, SLOT_TILES, EXPERTS])
        owner = sb("owner", [P, SLOT_TILES])
        share = sb("share", [P, CHOICES, TILES])
        slot = sb("slot", [P, CHOICES, TILES])
        reached = sb("reached", [P, CHOICES, TILES, SLOT_TILES + 2])
        tile_no = sb("tile_no", [P, CHOICES, TILES])
        in_tile = sb("in_tile", [P, CHOICES, TILES, SLOT_TILES + 1])
        entry = sb("entry", [P, CHOICES, TILES, 3, SLOT_TILES + 1], F32R)
        lane_hot = sb("lane_hot", [P, CHOICES, TILES, P], F32R)
        share_high = sb("share_high", [P, CHOICES, TILES], F32R)
        share_rest = sb("share_rest", [P, CHOICES, TILES])
        empty = sb("empty", [P, SLOT_TILES])
        ps_t = ps("ps_t", [P, GROUP, P])
        ps_g = ps("ps_g", wide)
        ps_before = ps("ps_before", wide)
        ps_total = ps("ps_total", wide)
        ps_slots = ps("ps_slots", [P, 3, SLOT_TILES + 1])
        s_gate = sem("s_gate")
        normed = sem("normed")
        turned = sem("turned")
        turned_out = sem("turned_out")
        gated = sem("gated")
        chosen_ok = sem("chosen_ok")
        counted = sem("counted")
        s_gap = sem("s_gap")
        s_exp = sem("s_exp")
        hot = sem("hot")
        listed = sem("listed")
        stored = sem("stored")
        s_chain = sem("chain")

        with nc.Block() as block:
            @block.sync
            def _(eng):
                eng.dma_start(gate[:, :], d["gate1"]).then_inc(s_gate, 16)
                eng.dma_start(out[0:TOKENS, :].rearrange("(t p) c -> p t c", p=P), x_sb[:, :, :]).then_inc(stored, 16)
                eng.dma_start(out[TOKENS:, :], x_sb[:, 0, :]).then_inc(stored, 16)
                eng.wait_ge(normed, TILES)
                eng.dma_start(normed_dram[0:TOKENS, :].rearrange("(t p) c -> p t c", p=P), xn[:, :, :])\
                   .then_inc(stored, 16)
                eng.dma_start(normed_dram[TOKENS:, :], xn[:, 0, :]).then_inc(stored, 16)
                eng.wait_ge(stored, 4 * 16)

            @block.tensor
            def _(eng):
                eng.wait_ge(s_gate, 16)
                for g in range(TURNS + 1):
                    if g >= 1:
                        eng.wait_ge(turned_out, g)
                    if g < TURNS:
                        for t in range(GROUP):
                            eng.wait_ge(normed, g * GROUP + t + 1)
                            mm = eng.transpose(ps_t[:, t, :], xn[:, g * GROUP + t, :], ident)
                        mm.then_inc(turned, 1)
                    if g >= 1:
                        for t in range((g - 1) * GROUP, g * GROUP):
                            mm = eng.matmul(ps_g[:, t, :], nT[:, t, :], gate[:, :], start=True, stop=True)
                mm.then_inc(gated, 1)
                eng.wait_ge(chosen_ok, 1)
                eng.matmul(ps_before[:, :, :], consts[:, C_UPPER:C_UPPER + P], chosen[:, :, :],
                           start=True, stop=True)
                eng.matmul(ps_total[:, :, :], consts[:, C_ONES:C_ONES + P], chosen[:, :, :],
                           start=True, stop=True).then_inc(counted, 1)
                for i in range(PAIRED):
                    k, t = divmod(i, TILES)
                    eng.wait_ge(hot, i + 1)
                    mm = eng.matmul(ps_slots[:, :, :], lane_hot[:, k, t, :], entry[:, k, t, :, :],
                                    start=(i == 0), stop=(i == PAIRED - 1))
                mm.then_inc(listed, 1)

            @block.scalar
            def _(eng):
                stats_scalar(eng)
                for g in range(TURNS):
                    eng.wait_ge(turned, g + 1)
                    eng.activation(nT[:, g * GROUP:(g + 1) * GROUP, :], ps_t[:, :, :], ACT.Copy)\
                       .then_inc(turned_out, 1)
                eng.wait_ge(s_gap, 1)
                eng.activation(value[1][:, :], value[1][:, :], ACT.Exp).then_inc(s_exp, 1)

            @block.vector
            def _(eng):
                stats_vector(eng)
                for t in range(TILES):
                    eng.tensor_scalar(xn[:, t, :], x_sb[:, t, :], moments[:, t, 0:1], rstd[:, t:t + 1],
                                      ALU.subtract, ALU.mult).then_inc(normed, 1)
                eng.wait_ge(gated, 1)
                chain = Chain(eng, s_chain)
                chain.after(eng.tensor_copy(scores[:, :, :], ps_g[:, :, :]))
                rank = rank_experts(eng, chain, sb, scores[:, :, :], consts[:, C_EARLIER:C_TILE], "route")
                for k in range(CHOICES):
                    chain.after(eng.tensor_scalar(choice[k][:, :, :], rank[:, :, :], float(k), None, ALU.is_equal))
                eng.tensor_tensor(chosen[:, :, :], choice[0][:, :, :], choice[1][:, :, :], ALU.add)\
                   .then_inc(chosen_ok, 1)
                for k in range(CHOICES):
                    chain.after(eng.tensor_tensor(picked[:, :, :], choice[k][:, :, :], scores[:, :, :], ALU.mult))
                    chain.after(eng.tensor_reduce(value[k][:, :], picked[:, :, :], X, ALU.add))
                eng.tensor_tensor(value[1][:, :], value[1][:, :], value[0][:, :], ALU.subtract).then_inc(s_gap, 1)

                eng.wait_ge(counted, 1)
                chain.after(eng.tensor_copy(total[:, :, :], ps_total[:, :, :]))
                chain.after(eng.tensor_copy(upto[0][:, :, :], total[:, :, :]))
                a, step = 0, 1
                while step < TILES:
                    new, old = upto[1 - a], upto[a]
                    eng.tensor_copy(new[:, 0:step, :], old[:, 0:step, :])
                    chain.after(eng.tensor_tensor(new[:, step:, :], old[:, step:, :], old[:, 0:TILES - step, :],
                                                  ALU.add))
                    a, step = 1 - a, 2 * step
                starts = consts[:, C_TILE:C_TILE + SLOT_TILES]
                shape = [P, EXPERTS, TILES]
                chain.after(eng.tensor_tensor(many[:, :, :], upto[a][:, TILES - 1, :].unsqueeze(2).to_broadcast(shape),
                                              starts[:, 0:TILES].unsqueeze(1).to_broadcast(shape), ALU.is_gt))
                chain.after(eng.tensor_reduce(tiles_of[:, :], many[:, :, :], X, ALU.add))
                shape = [P, EXPERTS, EXPERTS]
                chain.after(eng.tensor_tensor(
                    before[:, :, :], tiles_of[:, :].unsqueeze(1).to_broadcast(shape),
                    consts[:, C_EARLIER:C_TILE].rearrange("p (a b) -> p a b", b=EXPERTS), ALU.mult))
                chain.after(eng.tensor_reduce(start[:, :], before[:, :, :], X, ALU.add))
                chain.after(eng.tensor_scalar(start[:, :], start[:, :], float(P), None, ALU.mult))
                chain.after(eng.tensor_tensor(base[:, :, :], upto[a][:, :, :], total[:, :, :], ALU.subtract))
                chain.after(eng.tensor_tensor(base[:, :, :], base[:, :, :], ps_before[:, :, :], ALU.add))
                chain.after(eng.tensor_tensor(base[:, :, :], base[:, :, :],
                                              start[:, :].unsqueeze(1).to_broadcast(wide), ALU.add))
                for k in range(CHOICES):
                    chain.after(eng.tensor_tensor(picked[:, :, :], choice[k][:, :, :], base[:, :, :], ALU.mult))
                    chain.after(eng.tensor_reduce(slot[:, k, :], picked[:, :, :], X, ALU.add))
                shape = [P, CHOICES, TILES, SLOT_TILES]
                eng.memset(reached[:, :, :, SLOT_TILES:], 0.0)
                chain.after(eng.tensor_tensor(reached[:, :, :, 0:SLOT_TILES], slot[:, :, :].unsqueeze(3).to_broadcast(shape),
                                              starts.unsqueeze(1).unsqueeze(1).to_broadcast(shape), ALU.is_ge))
                chain.after(eng.tensor_reduce(tile_no[:, :, :], reached[:, :, :, 0:SLOT_TILES], X, ALU.add))
                chain.after(eng.scalar_tensor_tensor(tile_no[:, :, :], tile_no[:, :, :], -float(P), slot[:, :, :],
                                                     ALU.mult, ALU.add))
                chain.after(eng.tensor_tensor(in_tile[:, :, :, :], reached[:, :, :, 0:SLOT_TILES + 1],
                                              reached[:, :, :, 1:], ALU.subtract))
                eng.wait_ge(s_exp, 1)
                chain.after(eng.tensor_scalar(value[0][:, :], value[1][:, :], 1.0, None, ALU.add))
                chain.after(eng.reciprocal(share[:, 0, :], value[0][:, :]))
                chain.after(eng.tensor_tensor(share[:, 1, :], value[1][:, :], share[:, 0, :], ALU.mult))
                chain.after(eng.tensor_copy(share_high[:, :, :], share[:, :, :]))
                high = share_high[:, :, :].bitcast(F32)
                chain.after(eng.tensor_tensor(share_rest[:, :, :], share[:, :, :], high, ALU.subtract))
                shape = [P, CHOICES, TILES, SLOT_TILES + 1]
                eng.tensor_tensor(entry[:, :, :, 0, :], in_tile[:, :, :, :],
                                  consts[:, C_TOKEN:C_SPARE].unsqueeze(1).unsqueeze(3).to_broadcast(shape), ALU.mult)
                eng.tensor_tensor(entry[:, :, :, 1, :], in_tile[:, :, :, :],
                                  high.unsqueeze(3).to_broadcast(shape), ALU.mult)
                chain.after(eng.tensor_tensor(entry[:, :, :, 2, :], in_tile[:, :, :, :],
                                              share_rest[:, :, :].unsqueeze(3).to_broadcast(shape), ALU.mult))
                for i in range(PAIRED):
                    k, t = divmod(i, TILES)
                    eng.tensor_scalar(lane_hot[:, k, t, :], consts[:, C_ROW:C_TOKEN], tile_no[:, k, t:t + 1], None,
                                      ALU.is_equal).then_inc(hot, 1)
                shape = [P, SLOT_TILES, EXPERTS]
                chain.after(eng.tensor_tensor(begun[:, :, :], start[:, :].unsqueeze(1).to_broadcast(shape),
                                              starts.unsqueeze(2).to_broadcast(shape), ALU.is_le))
                chain.after(eng.tensor_reduce(owner[:, :], begun[:, :, :], X, ALU.add))
                chain.after(eng.tensor_scalar(owner[:, :], owner[:, :], float(P), consts[:, C_LANE:C_LANE + 1],
                                              ALU.mult, ALU.add))
                chain.after(eng.tensor_scalar(lots[:, :], owner[:, :], -float(P), None, ALU.add))
                eng.wait_ge(listed, 1)
                weight = slots[:, :, 1].bitcast(F32)
                chain.after(eng.tensor_copy(weight, ps_slots[:, 1, 0:SLOT_TILES]))
                eng.tensor_tensor(weight, weight, ps_slots[:, 2, 0:SLOT_TILES], ALU.add)
                chain.after(eng.tensor_scalar(empty[:, :], ps_slots[:, 0, 0:SLOT_TILES], 0.0, consts[:, C_SPARE:C_END],
                                              ALU.is_equal, ALU.mult))
                chain.after(eng.scalar_tensor_tensor(slots[:, :, 0], ps_slots[:, 0, 0:SLOT_TILES], -1.0, empty[:, :],
                                                     ALU.add, ALU.add))


class ArrivalCount:

    def __init__(self, even, odd):
        self.sems = (even, odd)

    def of(self, n):
        return self.sems[n % 2]

    def wait(self, eng, turn, n):
        eng.wait_ge(self.sems[n % 2], turn * 16 + 16 * (n // 2 + 1))


def spline_experts(nc, ctx, ident, normed_dram, out, w12_dram, w3_dram, slots, lots):
    with ExitStack() as own:
        def sb(name, shape, dt=F32):
            return own.enter_context(nc.sbuf_tensor(f"kan_{name}", shape, dt))

        def ps(name, shape):
            return own.enter_context(nc.psum_tensor(f"kan_{name}", shape, F32))

        def sem(name):
            return ctx.enter_context(nc.semaphore(f"kan_{name}"))

        def pair(name):
            return ArrivalCount(sem(name + "0"), sem(name + "1"))

        w12 = [sb(f"w12_{i}", [P, W12]) for i in range(2)]
        w3 = [sb(f"w3_{i}", [P, W3]) for i in range(2)]
        slot_x = [sb(f"slot_x{i}", [P, P]) for i in range(2)]
        y_sb = [sb(f"y_sb{i}", [P, P]) for i in range(2)]
        h1 = sb("h1", [P, FF1])
        h = sb("h", [P, FF1])
        h_u = sb("h_u", [P, FF1])
        offsets = sb("offsets", [P, BASES + 1])
        minus2 = offsets[:, BASES:BASES + 1]

        class Part:

            def __init__(self, tag, n, buffers, times):
                self.t = sb(tag + "t", [P, BASES, n])
                bases = [sb(f"{tag}f{i}", [P, BASES, n]) for i in range(buffers)]
                self.f = [bases[n % buffers] for n in range(2)]
                self.s = [sb(f"{tag}s{i}", [P, n]) for i in range(2)]
                self.near = sb(tag + "near", [P, BASES, n])
                self.far = sb(tag + "far", [P, BASES, n])
                self.turned = TileCount(sem(tag + "turned"))
                self.dist = TileCount(sem(tag + "dist"), times)
                self.near_square = TileCount(sem(tag + "near_square"), times)
                self.far_square = TileCount(sem(tag + "far_square"), times)
                self.near_cube = TileCount(sem(tag + "near_cube"), times)
                self.far_cube = TileCount(sem(tag + "far_cube"), times)
                self.silu = TileCount(sem(tag + "silu"))
                self.ready = TileCount(sem(tag + "ready"))
                self.used = TileCount(sem(tag + "used"))

        HALVES = 2
        px, ph = Part("x", P, buffers=2, times=1), Part("h", FF1, buffers=1, times=HALVES)
        layer1_ok = TileCount(sem("layer1_ok"), before=0)
        x_near = sb("x_near", [P, BASES, P])
        x_far = sb("x_far", [P, BASES, P])
        clamped = TileCount(sem("clamped"))
        near_part = TileCount(sem("near_part"))
        ps_x = [ps(f"ps_x{i}", [P, P]) for i in range(2)]
        ps_h = [[ps(f"ps_h{j}_{i}", [P, FF1]) for j in range(2)] for i in range(2)]
        ps_ht = ps("ps_ht", [P, CH1, P])
        ps_y = ps("ps_y", [P, P])
        in_x, in_12, in_3 = pair("in_x"), pair("in_12"), pair("in_3")
        tokens_x = [sb(f"tokens_x{i}", [P, 1], U32) for i in range(2)]
        slots_y = [sb(f"slots_y{i}", [P, 2], U32) for i in range(2)]
        tokens_ok = TileCount(sem("tokens_ok"))
        slots_ok = TileCount(sem("slots_ok"))
        scattered = TileCount(sem("scattered"), 16, before=0)
        out_y = TileCount(sem("out_y"))
        offsets_ok = sem("offsets_ok")
        gate = sem("gate")
        u_ok = TileCount(sem("u_ok"))
        offset_ok = TileCount(sem("offset_ok"), HALVES)
        h1_ok = TileCount(sem("h1_ok"))
        h_ok = TileCount(sem("h_ok"))
        y_ok = TileCount(sem("y_ok"))

        LAST = SLOT_TILES - 1
        FILLING = 2
        AFTER = 4
        LOOP = (SLOT_TILES - 1 - AFTER) // 2
        assert 1 + 2 * LOOP + AFTER == SLOT_TILES

        def tiles(eng, step):
            step(0, 0)
            with eng.Fori(0, LOOP) as i:
                step(i, 1)
                step(i, 2)
            for n in range(1, AFTER + 1):
                step(LOOP, n)

        def half_bases(i):
            return slice(i * BASES // HALVES, (i + 1) * BASES // HALVES)

        def exists(turn, n):
            return not isinstance(turn, int) or 0 <= 2 * turn + n <= LAST

        with nc.Block() as block:
            @block.sync
            def _(eng):
                px.used.give_credit(eng)
                ph.used.give_credit(eng)

                def fetch_weights(turn, n, buffers, table, arrived):
                    def lot(n):
                        return eng.value_load(lots[0:1, bass.ds(2 * turn + n, 1)], min_val=0,
                                              max_val=(EXPERTS - 1) * P)

                    def fetch():
                        eng.dma_start(buffers[n % 2][:, :], table[bass.ds(now, P), :]).then_inc(arrived.of(n), 16)

                    now = lot(n)
                    if isinstance(turn, int) and 2 * turn + n < 2:
                        fetch()
                        return
                    with eng.If(now != lot(n - 2)):
                        fetch()
                    with eng.Else():
                        eng.sem_inc(arrived.of(n), 16)

                def fetch12(turn, n):
                    if exists(turn, n):
                        px.used.wait(eng, turn, n - 2)
                        eng.sem_inc(gate, 1)
                        fetch_weights(turn, n, w12, w12_dram, in_12)

                def fetch3(turn, n):
                    if exists(turn, n):
                        ph.used.wait(eng, turn, n - 2)
                        eng.sem_inc(gate, 1)
                        fetch_weights(turn, n, w3, w3_dram, in_3)

                in_x.wait(eng, 0, 0)
                in_x.wait(eng, 0, 1)
                fetch12(0, 0)
                fetch12(0, 1)
                fetch3(0, 0)

                def step(turn, n):
                    fetch12(turn, n + 2)
                    fetch3(turn, n + 1)

                tiles(eng, step)

            @block.tensor
            def _(eng):
                px.silu.give_credit(eng)
                ph.silu.give_credit(eng)
                h_ok.give_credit(eng)

                def turn_x(turn, n):
                    if exists(turn, n):
                        in_x.wait(eng, turn, n)
                        px.silu.wait(eng, turn, n - 2)
                        px.dist.wait(eng, turn, n - 2)
                        eng.transpose(ps_x[n % 2][:, :], slot_x[n % 2][:, :], ident).then_inc(px.turned.sem, 1)

                def layers12(turn, n):
                    if exists(turn, n):
                        in_12.wait(eng, turn, n)
                        h_ok.wait(eng, turn, n - 2)
                        px.silu.wait(eng, turn, n)
                        px.ready.wait(eng, turn, n)
                        for j, done in enumerate((layer1_ok, px.used)):
                            for c in range(FEAT):
                                lhs = px.f[n % 2][:, c, :] if c < BASES else px.s[n % 2][:, :]
                                at = (2 * c + j) * FF1
                                mm = eng.matmul(ps_h[n % 2][j][:, :], lhs, w12[n % 2][:, at:at + FF1],
                                                start=(c == 0), stop=(c == BASES))
                            mm.then_inc(done.sem, 1)

                def turn_h(turn, n):
                    h_ok.wait(eng, turn, n)
                    u_ok.wait(eng, turn, n - 1)
                    ph.silu.wait(eng, turn, n - 1)
                    for k in range(CH1):
                        mm = eng.transpose(ps_ht[:, k, :], h[:, k * P:(k + 1) * P], ident)
                    mm.then_inc(ph.turned.sem, 1)

                def layer3(turn, n, part):
                    if not exists(turn, n):
                        return
                    if part == 0:
                        in_3.wait(eng, turn, n)
                        y_ok.wait(eng, turn, n - 1)
                        ph.silu.wait(eng, turn, n)
                        ph.ready.wait(eng, turn, n)
                    every = range(CH1 * FEAT)
                    for i in every[:FILLING] if part == 0 else every[FILLING:]:
                        k, c = divmod(i, FEAT)
                        cols = slice(k * P, (k + 1) * P)
                        lhs = ph.f[n % 2][:, c, cols] if c < BASES else ph.s[n % 2][:, cols]
                        mm = eng.matmul(ps_y[:, :], lhs, w3[n % 2][:, i * P:(i + 1) * P],
                                        start=(i == 0), stop=(i == CH1 * FEAT - 1))
                    if part == 1:
                        mm.then_inc(ph.used.sem, 1)

                turn_x(0, 0)
                turn_x(0, 1)
                layers12(0, 0)
                turn_x(0, 2)

                def step(turn, n):
                    layer3(turn, n - 1, 0)
                    turn_h(turn, n)
                    turn_x(turn, n + 3)
                    layer3(turn, n - 1, 1)
                    layers12(turn, n + 1)

                tiles(eng, step)
                layer3(LOOP, AFTER, 0)
                layer3(LOOP, AFTER, 1)

            @block.scalar
            def _(eng):
                clamped.give_credit(eng)
                px.near_cube.give_credit(eng)
                px.far_cube.give_credit(eng)
                ph.near_cube.give_credit(eng)
                px.dist.give_credit(eng)
                ph.dist.give_credit(eng)
                px.ready.give_credit(eng)
                ph.ready.give_credit(eng)
                out_y.give_credit(eng)
                slots_ok.give_credit(eng)
                eng.wait_ge(offsets_ok, 1)
                eng.preload_act_table(ACT.Silu)

                def distances_x(turn, n):
                    if exists(turn, n):
                        px.turned.wait(eng, turn, n)
                        clamped.wait(eng, turn, n - 1)
                        for c in range(BASES):
                            ins = eng.activation(px.t[:, c, :], ps_x[n % 2][:, :], ACT.Abs,
                                                 bias=offsets[:, c:c + 1], scale=KNOTS_PER_UNIT)
                        ins.then_inc(px.dist.sem, 1)

                def silu_x(turn, n):
                    if exists(turn, n):
                        px.turned.wait(eng, turn, n)
                        px.used.wait(eng, turn, n - 2)
                        eng.activation(px.s[n % 2][:, :], ps_x[n % 2][:, :], ACT.Silu).then_inc(px.silu.sem, 1)

                def take_h(turn, n):
                    ph.turned.wait(eng, turn, n)
                    ph.dist.wait(eng, turn, n - 1)
                    eng.activation(h_u[:, :], ps_ht[:, :, :], ACT.Copy, scale=KNOTS_PER_UNIT).then_inc(u_ok.sem, 1)
                    ph.used.wait(eng, turn, n - 2)
                    eng.activation(ph.s[n % 2][:, :], ps_ht[:, :, :], ACT.Silu).then_inc(ph.silu.sem, 1)

                def squares_x(turn, n):
                    if exists(turn, n):
                        clamped.wait(eng, turn, n)
                        px.ready.wait(eng, turn, n - 1)
                        eng.activation(px.near[:, :, :], x_near[:, :, :], ACT.Square, scale=2.0)\
                           .then_inc(px.near_square.sem, 1)
                        eng.activation(px.far[:, :, :], x_far[:, :, :], ACT.Square).then_inc(px.far_square.sem, 1)

                def squares_h(turn, n):
                    ph.ready.wait(eng, turn, n - 1)
                    for i in range(HALVES):
                        ph.dist.wait(eng, turn, n, i)
                        eng.activation(ph.near[:, half_bases(i), :], ph.t[:, half_bases(i), :], ACT.Square,
                                       bias=minus2, scale=2.0).then_inc(ph.near_square.sem, 1)
                    for i in range(HALVES):
                        eng.activation(ph.far[:, half_bases(i), :], ph.t[:, half_bases(i), :], ACT.Square,
                                       bias=minus2, scale=1.0).then_inc(ph.far_square.sem, 1)

                def near_part_h(turn, n):
                    ph.near_cube.wait(eng, turn, n)
                    eng.activation(ph.near[:, :, :], ph.near[:, :, :], ACT.Relu, scale=-1.0)\
                       .then_inc(near_part.sem, 1)

                def half(turn, n):
                    layer1_ok.wait(eng, turn, n)
                    h_ok.wait(eng, turn, n - 1)
                    eng.activation(h1[:, :], ps_h[n % 2][0][:, :], ACT.Copy).then_inc(h1_ok.sem, 1)

                def store(turn, n):
                    if exists(turn, n):
                        ph.used.wait(eng, turn, n)
                        out_y.wait(eng, turn, n - 2)
                        slots_ok.wait(eng, turn, n)
                        eng.activation(y_sb[n % 2][:, :], ps_y[:, :], ACT.Copy, scale=slots_y[n % 2][:, 1:2].bitcast(F32))\
                           .then_inc(y_ok.sem, 1)

                for n in range(2):
                    distances_x(0, n)
                    squares_x(0, n)
                    silu_x(0, n)
                distances_x(0, 2)

                def step(turn, n):
                    half(turn, n)
                    take_h(turn, n)
                    squares_x(turn, n + 2)
                    squares_h(turn, n)
                    store(turn, n - 1)
                    near_part_h(turn, n)
                    silu_x(turn, n + 2)
                    distances_x(turn, n + 3)

                tiles(eng, step)
                store(LOOP, AFTER)

            @block.vector
            def _(eng):
                ph.near_square.give_credit(eng)
                ph.far_square.give_credit(eng)
                near_part.give_credit(eng)
                ph.far_cube.give_credit(eng)
                ph.turned.give_credit(eng)
                u_ok.give_credit(eng)
                offset_ok.give_credit(eng)
                h1_ok.give_credit(eng)
                for c in range(BASES):
                    eng.memset(offsets[:, c:c + 1], -(FIRST_CENTRE + c))
                eng.memset(minus2, -2.0).then_inc(offsets_ok, 1)

                def distances_h(turn, n):
                    u_ok.wait(eng, turn, n)
                    ph.ready.wait(eng, turn, n - 1)
                    for i in range(HALVES):
                        for c in range(BASES)[half_bases(i)]:
                            ins = eng.tensor_scalar(ph.t[:, c, :], h_u[:, :], FIRST_CENTRE + c, None, ALU.subtract)
                        ins.then_inc(offset_ok.sem, 1)
                        offset_ok.wait(eng, turn, n, i)
                        bits = ph.t[:, half_bases(i), :].bitcast(U32)
                        eng.tensor_scalar(bits, bits, 0x7FFFFFFF, None, ALU.bitwise_and).then_inc(ph.dist.sem, 1)

                def cubes_h(turn, n):
                    for squares, cubes, to, shift in ((ph.near_square, ph.near_cube, ph.near, 1.0),
                                                      (ph.far_square, ph.far_cube, ph.far, 2.0)):
                        for i in range(HALVES):
                            squares.wait(eng, turn, n, i)
                            part = to[:, half_bases(i), :]
                            eng.scalar_tensor_tensor(part, ph.t[:, half_bases(i), :], shift, part,
                                                     ALU.subtract, ALU.mult).then_inc(cubes.sem, 1)

                def bases_h(turn, n):
                    ph.far_cube.wait(eng, turn, n)
                    near_part.wait(eng, turn, n)
                    ph.used.wait(eng, turn, n - 1)
                    eng.scalar_tensor_tensor(ph.f[n % 2][:, :, :], ph.far[:, :, :], 0.0, ph.near[:, :, :],
                                             ALU.min, ALU.add).then_inc(ph.ready.sem, 1)

                def clamp_x(turn, n):
                    if exists(turn, n):
                        px.dist.wait(eng, turn, n)
                        px.near_cube.wait(eng, turn, n - 1)
                        eng.tensor_scalar(x_near[:, :, :], px.t[:, :, :], 1.0, 0.0, ALU.subtract, ALU.min)
                        px.far_cube.wait(eng, turn, n - 1)
                        eng.tensor_scalar(x_far[:, :, :], px.t[:, :, :], 2.0, 0.0, ALU.subtract, ALU.min)\
                           .then_inc(clamped.sem, 1)

                def product(turn, n):
                    h1_ok.wait(eng, turn, n)
                    px.used.wait(eng, turn, n)
                    ph.turned.wait(eng, turn, n - 1)
                    eng.tensor_tensor(h[:, :], h1[:, :], ps_h[n % 2][1][:, :], ALU.mult).then_inc(h_ok.sem, 1)

                clamp_x(0, 0)
                clamp_x(0, 1)

                def step(turn, n):
                    product(turn, n)
                    clamp_x(turn, n + 2)
                    distances_h(turn, n)
                    cubes_h(turn, n)
                    bases_h(turn, n)

                tiles(eng, step)

            @block.gpsimd
            def _(eng):
                px.near_square.give_credit(eng)
                px.far_square.give_credit(eng)
                px.turned.give_credit(eng)
                tokens_ok.give_credit(eng)
                y_ok.give_credit(eng)

                def gather_x(turn, n):
                    if exists(turn, n):
                        px.turned.wait(eng, turn, n - 2)
                        eng.sem_inc(gate, 1)
                        eng.tensor_copy(tokens_x[n % 2][:, :], slots[:, bass.ds(2 * turn + n, 1), 0])\
                           .then_inc(tokens_ok.sem, 1)
                        tokens_ok.wait(eng, turn, n)
                        eng.sem_inc(gate, 1)
                        eng.indirect_dma_start(out=slot_x[n % 2][:, :], out_offset=None, in_=normed_dram,
                                               in_offset=bass.IndirectOffsetOnAxis(ap=tokens_x[n % 2][:, 0:1], axis=0))\
                           .then_inc(in_x.of(n), 16)

                def slots_of(turn, n):
                    if exists(turn, n):
                        eng.tensor_copy(slots_y[n % 2][:, :].unsqueeze(1), slots[:, bass.ds(2 * turn + n, 1), :])\
                           .then_inc(slots_ok.sem, 1)

                def scatter_y(turn, n):
                    if exists(turn, n):
                        y_ok.wait(eng, turn, n)
                        slots_ok.wait(eng, turn, n)
                        eng.sem_inc(gate, 1)
                        eng.indirect_dma_start(
                            out=out, out_offset=bass.IndirectOffsetOnAxis(ap=slots_y[n % 2][:, 0:1], axis=0),
                            in_=y_sb[n % 2][:, :], in_offset=None, compute_op=ALU.add).then_inc(scattered.sem, 16)
                        scattered.wait(eng, turn, n)
                        eng.sem_inc(out_y.sem, 1)

                def bases_x(turn, n):
                    if exists(turn, n):
                        for squares, cubes, to, base in ((px.near_square, px.near_cube, px.near, x_near),
                                                         (px.far_square, px.far_cube, px.far, x_far)):
                            squares.wait(eng, turn, n)
                            eng.tensor_tensor(to[:, :, :], to[:, :, :], base[:, :, :], ALU.mult)\
                               .then_inc(cubes.sem, 1)
                        px.near_cube.wait(eng, turn, n)
                        px.far_cube.wait(eng, turn, n)
                        px.used.wait(eng, turn, n - 2)
                        eng.tensor_tensor(px.f[n % 2][:, :, :], px.far[:, :, :], px.near[:, :, :], ALU.subtract)\
                           .then_inc(px.ready.sem, 1)

                for n in range(4):
                    if n >= 2:
                        bases_x(0, n - 2)
                    gather_x(0, n)

                def step(turn, n):
                    gather_x(turn, n + 4)
                    slots_of(turn, n)
                    bases_x(turn, n + 2)
                    scatter_y(turn, n - 1)

                tiles(eng, step)
                scatter_y(LOOP, AFTER)


def build(nc, d, out):
    with ExitStack() as ctx:
        def sb(name, shape, dt=F32):
            return ctx.enter_context(nc.sbuf_tensor(name, shape, dt))

        def sem(name):
            return ctx.enter_context(nc.semaphore(name))

        x_sb = sb("x_sb", [P, TILES, P])
        consts = sb("consts", [P, C_END])
        ident = consts[:, C_ID:C_ID + P]
        stats = sb("stats", [P, TILES, 6])
        w0_sb = sb("w0_sb", [P, 4 * P])
        s_x = [sem(f"s_x{g}") for g in range(TURNS)]
        s_c = sem("s_c")
        s_w0 = sem("s_w0")
        attention_sems = {}

        def attention_sem(name):
            if name not in attention_sems:
                attention_sems[name] = sem(f"att_{name}")
            return attention_sems[name]

        with ExitStack() as own:
            bias0 = own.enter_context(nc.sbuf_tensor("bias0", [P, HEADS, BLK], F32))
            pads0 = own.enter_context(nc.sbuf_tensor("pads0", [P, HEADS, 2 * NEIGH], F32))
            filled = sem("filled")

            def load0(eng):
                for g in range(TURNS):
                    at = slice(g * GROUP, (g + 1) * GROUP)
                    eng.dma_start(x_sb[:, at, :], d["x"].rearrange("(t p) c -> p t c", p=P)[:, at, :])\
                       .then_inc(s_x[g], 16)
                eng.dma_start(consts[:, :], d["consts"]).then_inc(s_c, 16)
                eng.dma_start(w0_sb[:, :], d["w0"]).then_inc(s_w0, 16)
                eng.dma_start(bias0[:, :, :], d["bias0"]).then_inc(s_w0, 16)
                eng.dma_start(pads0[:, :, :], d["pads0"]).then_inc(s_w0, 16)

            def arrived0(eng):
                eng.wait_ge(s_c, 16)
                eng.wait_ge(s_w0, 48)

            def fill0(eng, logits):
                for lg in logits:
                    eng.tensor_copy(lg[:, :, BLK:BLK + 2 * NEIGH], pads0[:, :, :]).then_inc(filled, 1)
                eng.wait_ge(filled, 2)

            attention(nc, attention_sem, "a0", x_sb, consts, load0, arrived0, BLK + 2 * NEIGH,
                      lambda turn, n: bias0[:, :, :], fill0,
                      {n: w0_sb[:, i * P:(i + 1) * P] for i, n in enumerate(("wq", "wk", "wv", "wo"))}, 1e-6, stats,
                      x_arrivals=s_x)

        w12_dram = nc.dram_tensor("w12_dram", (EXPERTS * P, W12), F32).ap()
        w3_dram = nc.dram_tensor("w3_dram", (EXPERTS * P, W3), F32).ap()
        normed_dram = nc.dram_tensor("normed_dram", (TOKENS + SPARE, P), F32).ap()
        window_bias = sb("window_bias", [P, WINDOWS // 2, HEADS, BLK])
        slots = sb("slots", [P, SLOT_TILES, 2], U32)
        lots = sb("lots", [P, SLOT_TILES], U32)

        with ExitStack() as own:
            work = spline_weights(nc, lambda name, shape: own.enter_context(nc.sbuf_tensor(f"sw_{name}", shape, F32)),
                                  lambda name: sem(f"sw_{name}"), d, w12_dram, w3_dram, window_bias)
            gelu_experts(nc, ctx, x_sb, consts, d, work, attention_sems.values(), stats)

        with ExitStack() as own:
            w1_sb = own.enter_context(nc.sbuf_tensor("w1_sb", [P, 4 * P + 2], F32))
            rows1 = own.enter_context(nc.sbuf_tensor("rows1", [P, 2 * P], F32))
            s_w1 = sem("s_w1")

            def load1(eng):
                eng.dma_start(w1_sb[:, :], d["w1"]).then_inc(s_w1, 16)
                eng.dma_start(rows1[:, :], d["rows1"]).then_inc(s_w1, 16)

            def arrived1(eng):
                eng.wait_ge(s_w1, 32)

            def fill1(eng, logits):
                pass

            w = {n: w1_sb[:, i * P:(i + 1) * P] for i, n in enumerate(("wq", "wk", "wv", "wo"))}
            w |= {"bq": w1_sb[:, 4 * P:4 * P + 1], "bk": w1_sb[:, 4 * P + 1:4 * P + 2],
                  "bv": rows1[:, 0:P], "bp": rows1[:, P:]}
            attention(nc, attention_sem, "a1", x_sb, consts, load1, arrived1, BLK,
                      lambda turn, n: window_bias[:, bass.ds((turn * GROUP + n) % (WINDOWS // 2), 1), :, :],
                      fill1, w, 1e-6, stats, stats)

        route(nc, ctx, x_sb, consts, d, normed_dram, out, slots, lots, stats)
        spline_experts(nc, ctx, ident, normed_dram, out, w12_dram, w3_dram, slots, lots)


def constants():
    c = np.zeros((P, C_END), np.float32)
    lane = np.arange(P)
    c[:, C_ID:C_ID + P] = np.eye(P)
    c[lane, C_HEAD + lane // DK] = DK ** -0.5
    c[lane, C_HALF + lane // DK % 2] = 1.0
    c[:, C_UPPER:C_UPPER + P] = lane[:, None] < lane[None, :]
    c[:, C_ONES:C_ONES + P] = 1.0
    e = np.arange(EXPERTS)
    c[:, C_EARLIER:C_TILE] = (e[None, :] < e[:, None]).reshape(1, -1)
    c[:, C_TILE:C_LANE] = np.arange(SLOT_TILES) * P
    c[:, C_LANE] = lane
    c[:, C_ROW:C_TOKEN] = lane - P
    c[:, C_TOKEN:C_SPARE] = np.arange(TILES) * P + lane[:, None] + 1
    c[:, C_SPARE] = TOKENS + lane + 1
    return c


def layouts(i):
    a = {k: np.asarray(v) for k, v in i.items()}
    f = np.float32
    d = {"x": a["x"].reshape(TOKENS, P), "consts": constants()}
    wqkv = a["L0_conv_W_qkv"]
    d["w0"] = np.concatenate([wqkv, a["L0_conv_W_out"]], 1)
    keys = np.full((HEADS, BLK, BLK + 2 * NEIGH), FAR, f)
    for s in range(BLK):
        keys[:, s, s:s + 2 * NEIGH + 1] = a["L0_conv_pos_bias"][:, s, :]
    rows = keys.reshape(PAIRS, 2 * BLK, -1).transpose(1, 0, 2)
    rows = np.repeat(rows, 2, 1)
    d["bias0"] = rows[:, :, NEIGH:NEIGH + BLK]
    d["pads0"] = np.concatenate([rows[:, :, :NEIGH], rows[:, :, NEIGH + BLK:]], 2)
    w1 = np.concatenate([a["L0_ffn_sw1"], a["L0_ffn_rw1"]])
    w2 = np.concatenate([a["L0_ffn_sw2"], a["L0_ffn_rw2"]])
    b1 = np.concatenate([a["L0_ffn_sb1"], a["L0_ffn_rb1"]])
    n = len(w1)
    d["experts0"] = np.concatenate([
        w1.transpose(0, 2, 1),
        w2.reshape(n, P, CH0, P).transpose(0, 3, 2, 1).reshape(n, P, FF0),
        b1.reshape(n, CH0, P).transpose(0, 2, 1)], 2)
    d["b2"] = np.concatenate([a["L0_ffn_sb2"], a["L0_ffn_rb2"]])
    d["gate0"] = np.concatenate([a["L0_ffn_gate_w"].T, np.tile(a["L0_ffn_gate_b"], (P, 1))], 1)
    d["w1"] = np.concatenate([a["L1_conv_Wq"].T, a["L1_conv_Wk"].T, a["L1_conv_Wv"].T, a["L1_conv_Wp"].T,
                              a["L1_conv_bq"][:, None], a["L1_conv_bk"][:, None]], 1)
    d["rows1"] = np.tile(np.concatenate([a["L1_conv_bv"], a["L1_conv_bp"]]), (P, 1))
    d["pos1"] = a["L1_conv_pos_bias"].reshape(PAIRS, P, BLK).transpose(1, 0, 2)
    mask = a["L1_conv_mask"].reshape(WINDOWS, BLK, BLK).transpose(1, 0, 2)
    d["mask1"] = np.concatenate([mask, mask])
    d["gate1"] = a["L1_ffn_gate_w"].T
    def layer(n):
        base = a[f"L1_ffn_base_w{n}"].transpose(0, 2, 1)[:, :, None, :]
        spline = a[f"L1_ffn_spline_w{n}"].transpose(0, 2, 3, 1)
        return np.concatenate([spline, base], 2), a[f"L1_ffn_scaler_w{n}"].transpose(0, 2, 1)
    (f1, s1), (f2, s2), (f3, s3) = layer(1), layer(2), layer(3)
    split = lambda m: m.reshape(EXPERTS, CH1, P, -1).transpose(0, 2, 1, 3).reshape(EXPERTS, P, -1)
    d["experts1"] = np.concatenate([np.concatenate([f1, f2], 3).reshape(EXPERTS, P, W12), split(f3)], 2)
    d["scalers1"] = np.concatenate([s1, s2, split(s3)], 2)
    return {k: np.ascontiguousarray(v) for k, v in d.items()}


def kernel(**inputs):
    import concourse.bacc as bacc
    from concourse.bass_utils import run_bass_kernel_spmd as run

    nc = bacc.Bacc("TRN2", target_bir_lowering=False, num_devices=1)
    arrays = layouts(inputs)
    d = {n: nc.dram_tensor(f"in_{n}", a.shape, mybir.dt.from_np(a.dtype), kind="ExternalInput").ap()
         for n, a in arrays.items()}
    out = nc.dram_tensor("out", (TOKENS + SPARE, P), F32, kind="ExternalOutput").ap()
    build(nc, d, out)
    r = run(nc, [{f"in_{n}": a for n, a in arrays.items()}], core_ids=[0])
    return r.results[0]["out"][:TOKENS].reshape(2, 16, 64, P)
```
